# Optimizing a Trainium2 kernel written in Bass

```python
import numpy as np
import jax
import jax.numpy as jnp

def _softmax(x, axis=-1):
    return jax.nn.softmax(x, axis=axis)

def _gelu(x):
    return jax.nn.gelu(x, approximate=True)

def _silu(x):
    return jax.nn.silu(x)

def _sigmoid(x):
    return jax.nn.sigmoid(x)

def _layernorm(x, axis=-1, eps=1e-05):
    m = jnp.mean(x, axis=axis, keepdims=True)
    v = jnp.var(x, axis=axis, keepdims=True)
    return (x - m) / jnp.sqrt(v + eps)

def _scatter_add(tgt, idx, src, axis=0):
    return tgt.at[idx].add(src)

def _segment_sum(src, seg, n):
    return jax.ops.segment_sum(src, seg, n)
kernel_name = 'mk_lm_tower_d2_tok_ids1024_r4_ba9123'

def setup_inputs(seed: int=0):
    np.random.seed(seed)
    _w = jnp.asarray

    def _rec_inputs():
        import jax
        import jax.numpy as jnp
        _rk = jax.random.key(seed)
        x = jax.random.randint(jax.random.fold_in(_rk, 1), (8, 256), 0, 250, jnp.int32)
        return x
    x = _rec_inputs()

    def _L0_tok_setup():
        import math
        import jax, jax.numpy as jnp
        import numpy as np
        PAD_IDX = 1
        SEP_ID = 4
        STARTPOS = 1025
        BSZ, SEQ_LEN, EMBED_DIM = (32, 1024, 256)

        def _build_table(num_cons, dim, padding_idx, startpos):
            half = dim // 2
            freqs = jnp.exp(jnp.arange(half, dtype=jnp.float32) * -(math.log(10000.0) / (half - 1)))
            ang = jnp.arange(startpos, startpos + num_cons, dtype=jnp.float32)[:, None] * freqs[None, :]
            tab = jnp.concatenate([jnp.sin(ang), jnp.cos(ang)], axis=1)
            return tab.at[padding_idx].set(0.0)

        def _positions(tokens):
            L = tokens.shape[1]
            valid = jnp.cumprod((tokens != PAD_IDX).astype(jnp.int32), axis=1).astype(bool)
            j = jnp.arange(L, dtype=jnp.int32)
            sep_j = jnp.where(tokens == SEP_ID, j, 0)
            last_sep = jax.lax.associative_scan(jnp.maximum, sep_j, axis=1)
            pos = j - last_sep + 2
            return jnp.where(valid, pos, 1)
        key = jax.random.key(seed)
        tokens = jax.random.randint(key, (BSZ, SEQ_LEN), 0, 250, dtype=jnp.int64)
        num_cons = PAD_IDX + 1 + SEQ_LEN
        weights = _build_table(num_cons, EMBED_DIM, PAD_IDX, STARTPOS)
        return {'input': tokens, 'weights': weights}
    _L0_tok_all = _L0_tok_setup()
    _L0_tok_in = {k: v for k, v in _L0_tok_all.items() if k in ('weights',)}
    del _L0_tok_all

    def _L0_attn_setup():
        import math
        import jax, jax.numpy as jnp
        import numpy as np
        B, T, D, H = (4, 512, 256, 16)
        HD = D // H

        def apply_rope(x, base=10000.0):
            _, t, _, dh = x.shape
            half = dh // 2
            inv_freq = 1.0 / base ** (jnp.arange(half, dtype=jnp.float32) / float(half))
            pos = jnp.arange(t, dtype=jnp.float32)
            angles = pos[:, None] * inv_freq[None, :]
            sin = jnp.sin(angles)[None, :, None, :]
            cos = jnp.cos(angles)[None, :, None, :]
            x1 = x[..., :half]
            x2 = x[..., half:2 * half]
            rot1 = x1 * cos - x2 * sin
            rot2 = x1 * sin + x2 * cos
            return jnp.concatenate([rot1, rot2, x[..., 2 * half:]], axis=-1)
        key = jax.random.key(seed)
        k1, k2, k3 = jax.random.split(key, 3)
        x = jax.random.normal(k1, (B, T, D), dtype=jnp.float32)
        Wqkv = jax.random.normal(k2, (D, 3 * D), dtype=jnp.float32) / math.sqrt(D)
        Wo = jax.random.normal(k3, (D, D), dtype=jnp.float32) / math.sqrt(D)
        bo = jnp.zeros((D,), dtype=jnp.float32)
        return {'x': x, 'Wqkv': Wqkv, 'Wo': Wo, 'bo': bo}
    _L0_attn_all = _L0_attn_setup()
    _L0_attn_in = {k: v for k, v in _L0_attn_all.items() if k in ('Wqkv', 'Wo', 'bo')}
    del _L0_attn_all

    def _L0_ffn_setup():
        import jax, jax.numpy as jnp
        import numpy as np
        EMBED_DIM = 256
        HIDDEN_DIM = 1024
        NUM_EXPERTS = 8
        TOP_K = 2
        key = jax.random.key(seed)
        ks = jax.random.split(key, 4)
        std1 = float(np.sqrt(2.0 / EMBED_DIM))
        std2 = float(np.sqrt(2.0 / HIDDEN_DIM))
        x = jax.random.normal(ks[0], (1, 512, EMBED_DIM), dtype=jnp.float32)
        w_router = jax.random.normal(ks[1], (EMBED_DIM, NUM_EXPERTS), dtype=jnp.float32) * 0.02
        w1 = jax.random.normal(ks[2], (NUM_EXPERTS, EMBED_DIM, HIDDEN_DIM), dtype=jnp.float32) * std1
        b1 = jnp.zeros((NUM_EXPERTS, HIDDEN_DIM), dtype=jnp.float32)
        w2 = jax.random.normal(ks[3], (NUM_EXPERTS, HIDDEN_DIM, EMBED_DIM), dtype=jnp.float32) * std2
        b2 = jnp.zeros((NUM_EXPERTS, EMBED_DIM), dtype=jnp.float32)
        return {'x': x, 'w_router': w_router, 'w1': w1, 'b1': b1, 'w2': w2, 'b2': b2}
    _L0_ffn_all = _L0_ffn_setup()
    _L0_ffn_in = {k: v for k, v in _L0_ffn_all.items() if k in ('w_router', 'w1', 'b1', 'w2', 'b2')}
    del _L0_ffn_all

    def _L1_attn_setup():
        import jax, jax.numpy as jnp
        import numpy as np
        B, T, C, H = (2, 256, 256, 16)
        D = C // H
        EPS = 1e-06
        key = jax.random.key(seed)
        k1, k2, k3, k4, k5 = jax.random.split(key, 5)
        s = 0.02
        return {'x': jax.random.normal(k1, (B, T, C), dtype=jnp.float32), 'w_qkv': jax.random.normal(k2, (3 * C, C), dtype=jnp.float32) * s, 'b_qkv': jax.random.normal(k3, (3 * C,), dtype=jnp.float32) * s, 'w_out': jax.random.normal(k4, (C, C), dtype=jnp.float32) * s, 'b_out': jax.random.normal(k5, (C,), dtype=jnp.float32) * s}
    _L1_attn_all = _L1_attn_setup()
    _L1_attn_in = {k: v for k, v in _L1_attn_all.items() if k in ('w_qkv', 'b_qkv', 'w_out', 'b_out')}
    del _L1_attn_all

    def _L1_ffn_setup():
        import jax, jax.numpy as jnp
        import numpy as np
        B, N, D = (4, 512, 256)
        SPARSITY = 0.01
        key = jax.random.key(seed)
        k1, k2, k3 = jax.random.split(key, 3)
        x = jax.random.normal(k1, (B, N, D), dtype=jnp.float32)
        spatial = jax.random.normal(k2, (D, D), dtype=jnp.float32) * 0.02
        freq = jnp.fft.fft(spatial, axis=-1)
        k = int(D * SPARSITY)
        mag = jnp.abs(freq)
        kth = jax.lax.top_k(mag, k)[0][:, -1:]
        w_sparse = jnp.where(mag >= kth, freq, 0.0 + 0j)
        bias = jax.random.normal(k3, (D,), dtype=jnp.float32) * 0.01
        return {'x': x, 'w_freq_real': jnp.real(w_sparse).astype(jnp.float32), 'w_freq_imag': jnp.imag(w_sparse).astype(jnp.float32), 'bias': bias}
    _L1_ffn_all = _L1_ffn_setup()
    _L1_ffn_in = {k: v for k, v in _L1_ffn_all.items() if k in ('w_freq_real', 'w_freq_imag', 'bias')}
    del _L1_ffn_all
    return {'x': x, 'L0_tok_weights': _L0_tok_in['weights'], 'L0_attn_Wqkv': _L0_attn_in['Wqkv'], 'L0_attn_Wo': _L0_attn_in['Wo'], 'L0_attn_bo': _L0_attn_in['bo'], 'L0_ffn_w_router': _L0_ffn_in['w_router'], 'L0_ffn_w1': _L0_ffn_in['w1'], 'L0_ffn_b1': _L0_ffn_in['b1'], 'L0_ffn_w2': _L0_ffn_in['w2'], 'L0_ffn_b2': _L0_ffn_in['b2'], 'L1_attn_w_qkv': _L1_attn_in['w_qkv'], 'L1_attn_b_qkv': _L1_attn_in['b_qkv'], 'L1_attn_w_out': _L1_attn_in['w_out'], 'L1_attn_b_out': _L1_attn_in['b_out'], 'L1_ffn_w_freq_real': _L1_ffn_in['w_freq_real'], 'L1_ffn_w_freq_imag': _L1_ffn_in['w_freq_imag'], 'L1_ffn_bias': _L1_ffn_in['bias']}

def reference(x, L0_tok_weights, L0_attn_Wqkv, L0_attn_Wo, L0_attn_bo, L0_ffn_w_router, L0_ffn_w1, L0_ffn_b1, L0_ffn_w2, L0_ffn_b2, L1_attn_w_qkv, L1_attn_b_qkv, L1_attn_w_out, L1_attn_b_out, L1_ffn_w_freq_real, L1_ffn_w_freq_imag, L1_ffn_bias):
    import jax
    import jax.numpy as jnp

    def _L0_tok_ref(input, weights):
        import math
        import jax, jax.numpy as jnp
        import numpy as np
        PAD_IDX = 1
        SEP_ID = 4
        STARTPOS = 1025
        BSZ, SEQ_LEN, EMBED_DIM = (32, 1024, 256)

        def _build_table(num_cons, dim, padding_idx, startpos):
            half = dim // 2
            freqs = jnp.exp(jnp.arange(half, dtype=jnp.float32) * -(math.log(10000.0) / (half - 1)))
            ang = jnp.arange(startpos, startpos + num_cons, dtype=jnp.float32)[:, None] * freqs[None, :]
            tab = jnp.concatenate([jnp.sin(ang), jnp.cos(ang)], axis=1)
            return tab.at[padding_idx].set(0.0)

        def _positions(tokens):
            L = tokens.shape[1]
            valid = jnp.cumprod((tokens != PAD_IDX).astype(jnp.int32), axis=1).astype(bool)
            j = jnp.arange(L, dtype=jnp.int32)
            sep_j = jnp.where(tokens == SEP_ID, j, 0)
            last_sep = jax.lax.associative_scan(jnp.maximum, sep_j, axis=1)
            pos = j - last_sep + 2
            return jnp.where(valid, pos, 1)
        pos = _positions(input)
        return jnp.take(weights, pos, axis=0)

    def _L0_attn_ref(x, Wqkv, Wo, bo):
        import math
        import jax, jax.numpy as jnp
        import numpy as np
        B, T, D, H = (4, 512, 256, 16)
        HD = D // H

        def apply_rope(x, base=10000.0):
            _, t, _, dh = x.shape
            half = dh // 2
            inv_freq = 1.0 / base ** (jnp.arange(half, dtype=jnp.float32) / float(half))
            pos = jnp.arange(t, dtype=jnp.float32)
            angles = pos[:, None] * inv_freq[None, :]
            sin = jnp.sin(angles)[None, :, None, :]
            cos = jnp.cos(angles)[None, :, None, :]
            x1 = x[..., :half]
            x2 = x[..., half:2 * half]
            rot1 = x1 * cos - x2 * sin
            rot2 = x1 * sin + x2 * cos
            return jnp.concatenate([rot1, rot2, x[..., 2 * half:]], axis=-1)
        b, t, d = x.shape
        qkv = x @ Wqkv
        q, k, v = jnp.split(qkv, 3, axis=-1)
        q = q.reshape(b, t, H, HD)
        k = k.reshape(b, t, H, HD)
        v = v.reshape(b, t, H, HD)
        q = apply_rope(q)
        k = apply_rope(k)
        q = q / jnp.sqrt(jnp.sum(q * q, axis=-1, keepdims=True) + 1e-06)
        k = k / jnp.sqrt(jnp.sum(k * k, axis=-1, keepdims=True) + 1e-06)
        attn = jnp.einsum('bthd,bshd->bhts', q, k) / math.sqrt(HD)
        attn = jax.nn.softmax(attn, axis=-1)
        out = jnp.einsum('bhts,bshd->bthd', attn, v).reshape(b, t, d)
        return out @ Wo + bo

    def _L0_ffn_ref(x, w_router, w1, b1, w2, b2):
        import jax, jax.numpy as jnp
        import numpy as np
        EMBED_DIM = 256
        HIDDEN_DIM = 1024
        NUM_EXPERTS = 8
        TOP_K = 2
        orig_shape = x.shape
        xf = x.reshape(-1, EMBED_DIM)
        logits = xf @ w_router
        probs = jax.nn.softmax(logits, axis=-1)
        topk_w, topk_idx = jax.lax.top_k(probs, TOP_K)
        mask = jax.nn.one_hot(topk_idx, NUM_EXPERTS, dtype=xf.dtype)
        weights = jnp.sum(topk_w[..., None] * mask, axis=1)
        h = jnp.einsum('te,ieh->tih', xf, w1) + b1
        h = jax.nn.gelu(h)
        out = jnp.einsum('tih,ihe->tie', h, w2) + b2
        out = jnp.sum(out * weights[..., None], axis=1)
        return out.reshape(orig_shape)

    def _L1_attn_ref(x, w_qkv, b_qkv, w_out, b_out):
        import jax, jax.numpy as jnp
        import numpy as np
        B, T, C, H = (2, 256, 256, 16)
        D = C // H
        EPS = 1e-06
        b, t, c = x.shape
        qkv = x @ w_qkv.T + b_qkv
        q, k, v = jnp.split(qkv, 3, axis=-1)

        def to_heads(u):
            return u.reshape(b, t, H, D).transpose(0, 2, 1, 3).astype(jnp.float32)
        q, k, v = (to_heads(q), to_heads(k), to_heads(v))
        q_prime = jax.nn.elu(q) + 1.0
        k_prime = jax.nn.elu(k) + 1.0
        kv_cumsum = jnp.cumsum(jnp.einsum('bhtd,bhte->bhtde', k_prime, v), axis=2)
        context = jnp.einsum('bhtd,bhtde->bhte', q_prime, kv_cumsum)
        norm = jnp.einsum('bhtd,bhtd->bht', q_prime, jnp.cumsum(k_prime, axis=2))
        out = context / (norm[..., None] + EPS)
        out = out.astype(x.dtype).transpose(0, 2, 1, 3).reshape(b, t, c)
        return out @ w_out.T + b_out

    def _L1_ffn_ref(x, w_freq_real, w_freq_imag, bias):
        import jax, jax.numpy as jnp
        import numpy as np
        B, N, D = (4, 512, 256)
        SPARSITY = 0.01
        w = jax.lax.complex(w_freq_real, w_freq_imag)
        x_freq = jnp.fft.fft(x, axis=-1)
        y_freq = jnp.einsum('bnd,do->bno', x_freq, w)
        y = jnp.real(jnp.fft.ifft(y_freq, axis=-1))
        return y + bias
    h = _L0_tok_ref(x, L0_tok_weights)
    h = h + _L0_attn_ref(_layernorm(h, axis=-1), L0_attn_Wqkv, L0_attn_Wo, L0_attn_bo)
    h = h + _L0_ffn_ref(_layernorm(h, axis=-1), L0_ffn_w_router, L0_ffn_w1, L0_ffn_b1, L0_ffn_w2, L0_ffn_b2)
    h = h + _L1_attn_ref(_layernorm(h, axis=-1), L1_attn_w_qkv, L1_attn_b_qkv, L1_attn_w_out, L1_attn_b_out)
    h = h + _L1_ffn_ref(_layernorm(h, axis=-1), L1_ffn_w_freq_real, L1_ffn_w_freq_imag, L1_ffn_bias)
    return h

_drawn_inputs = setup_inputs


def setup_inputs(seed=0):
    import zlib

    import numpy as np

    out = dict(_drawn_inputs(seed))
    spreads = {'L0_attn_bo': (0.0, 0.1), 'L0_ffn_b1': (0.0, 0.1), 'L0_ffn_b2': (0.0, 0.1)}
    factors = {'L1_attn_b_qkv': 3.648, 'L1_ffn_bias': 5.655}
    for name, (base, spread) in spreads.items():
        noise = np.random.default_rng([zlib.crc32(name.encode()), seed]).standard_normal(out[name].shape)
        drawn = base * np.exp(spread * noise) if base else spread * noise
        out[name] = jnp.asarray(drawn.astype(out[name].dtype))
    for name, factor in factors.items():
        out[name] = (out[name] * factor).astype(out[name].dtype)
    return out
```

```python
import concourse.bass as bass
from concourse import mybir
from contextlib import ExitStack

fp32 = mybir.dt.float32
fp16 = mybir.dt.float16
i32 = mybir.dt.int32
u32 = mybir.dt.uint32
ALU = mybir.AluOpType
ACT = mybir.ActivationFunctionType
AX = mybir.AxisListType

P = 128
NB, T, D = 8, 256, 256
NT = NB * T // P
H, HD = 16, 16
NE, HID, TOPK = 8, 1024, 2
VW = HD + 1
TAB = 3
MT = (TOPK * NB * T + NE * (P - 1)) // P
CH = HID // P
WS = 64.0
EPS_LN, EPS_QK, EPS_L1 = 1e-5, 1e-6, 1e-6
KC = D // P


def wait(eng, sem, value):
    if isinstance(value, int) and value <= 0:
        return
    eng.wait_ge(sem, value)


def lm_tower(nc, x, table, wqkv0, wo0, bo0, wr, w1, b1, w2, b2, wqkv1, bqkv1, wout1, bout1,
             fre, fim, fbias, c_ident, c_identh, c_rope, c_j, c_ltri, c_tpre, c_tsum, c_causal,
             c_dft, c_iota, out):
    ctx = ExitStack()
    with ctx:
        def sb(name, shape, dt):
            return ctx.enter_context(nc.sbuf_tensor(name, shape, dt))

        def sem(name):
            return ctx.enter_context(nc.semaphore(name))

        tab_qk = nc.dram_tensor("tab_qk", (TAB * P, 2 * D), fp32).ap()
        tab_v = nc.dram_tensor("tab_v", (TAB * P, H * VW), fp32).ap()
        xn_d = nc.dram_tensor("xn_d", (NT * P, 2 * D), fp16).ap()
        y_d = nc.dram_tensor("y_d", (MT * P, D), fp32).ap()

        WX = sb("expert_weights", [P, NE, 4, 2, 1024], fp16)
        h = sb("h", [P, NT, D], fp32)
        wA = sb("w_qkv_split", [P, KC, 2, 3 * D], fp16)
        wB = sb("w_o_split", [P, KC, 2, D], fp16)
        wM = sb("w_fft_split", [P, KC, 2, D], fp16)
        wR = sb("w_router_split", [P, KC, 2, NE], fp16)
        ident = sb("ident", [NB, NB], fp32)
        identh = sb("identh", [P, P], fp16)
        rope = sb("rope", [P, 2, 2, HD], fp32)
        pos_i = sb("pos_i", [P, NT + 4], i32)
        posx = sb("posx", [P, 2, 2, 1], i32)
        bias_bc = sb("bias_bc", [P, 5 * D], fp32)
        stage = sb("stage", [P, 2, 1024], fp32)
        lgt = sb("lgt", [P, NT, NE], fp32)
        mxt = sb("mxt", [P, NT, 2], fp32)
        ixt = sb("ixt", [P, NT, 2], fp32)
        gate = sb("gate", [P, NT, 2], fp32)
        slot_i = sb("slot_i", [P, NT + 2, 2], i32)
        inv_i = sb("inv_i", [P, MT], i32)
        ej = sb("ej", [1, MT], i32)
        posy = sb("posy", [P, 2, 2, 1], i32)
        b1s = sb("b1s", [P, NE, CH], fp32)
        small = sb("small", [P, 64], fp32)
        mexp = sb("minus_half", [P, 32], fp32)
        epsc = sb("epsc", [P, 1], fp32)
        lg = sb("lg", [P, NE], fp32)
        mx8 = sb("mx8", [P, 8], fp32)
        ix8 = sb("ix8", [P, 8], u32)
        AW = 9600
        arena = sb("arena", [P, AW], fp32)

        def view(at, shape, dt=fp32):
            n = 1
            for s in shape:
                n *= s
            words = n if dt in (fp32, i32, u32) else n // 2
            a = arena[:, at:at + words]
            if dt != fp32:
                a = a.bitcast(dt)
            names = " ".join("abcd"[i] for i in range(len(shape)))
            if len(shape) > 1:
                a = a.rearrange(f"p ({names}) -> p {names}", **{"abcd"[i]: shape[i] for i in range(1, len(shape))})
            return a, at + words

        at = 0
        qkg, at = view(at, [2, 2 * D])
        hg, at = view(at, [2, D])
        r, at = view(at, [2 * D])
        r2 = bias_bc[:, D:3 * D]
        hl, at = view(at, [2 * H, 4, HD], fp16)
        qkT, at = view(at, [8, 2, T], fp16)
        vaug, at = view(at, [2, H, VW])
        E, at = view(at, [2, 2, 2 * T])
        o, at = view(at, [2, D])
        osp, at = view(at, [2, 2, D], fp16)
        xT = [None, None]
        hs = [None, None]
        for i in range(2):
            xT[i], at = view(at, [2, KC, P], fp16)
            hs[i] = wM[:, i, :, :]
        hn = o[:, 0, :]
        ATT = at
        mask3, _ = view(2 * 2 * D, [3, P])
        x1, _ = view(0, [3 * D])
        assert ATT <= AW, ATT
        at = 0
        wst, at = view(at, [KC, 3 * D])
        tb, at = view(at, [TAB, D])
        u, at = view(at, [2 * D])
        usq, at = view(at, [2 * D])
        txT, at = view(at, [2, KC, P], fp16)
        ths, at = view(at, [2, D], fp16)
        tv, at = view(at, [H, VW])
        tokx_i, at = view(at, [T], i32)
        tokf, at = view(at, [T])
        jrow, at = view(at, [T])
        tm, at = view(at, [T])
        tsp, at = view(at, [T])
        tls, at = view(at, [T])
        tva, at = view(at, [T])
        thn, at = view(at, [D])
        wst2, at = view(at, [KC, D])
        wst3, at = view(at, [KC, NE])
        at = 0
        ltri, at = view(at, [P])
        tpre, at = view(at, [P])
        tsum, at = view(at, [NE])
        iota, at = view(at, [P + MT + NE + NT])
        iob, ioa, ioe, tokid = iota[:, 0:P], iota[:, P:P + MT], iota[:, P + MT:P + MT + NE], iota[:, P + MT + NE:]
        m0, at = view(at, [NT, NE])
        m1, at = view(at, [NT, NE])
        mc, at = view(at, [NT, NE])
        totb, at = view(at, [P])
        ohb, at = view(at, [2 * NT, P], fp16)
        oha, at = view(at, [2 * NT, MT], fp16)
        ra, at = view(at, [2 * NT])
        rb, at = view(at, [2 * NT])
        ri, at = view(at, [2 * NT], i32)
        ri2, at = view(at, [2 * NT], i32)
        ecmp, at = view(at, [MT, NE])
        e8, at = view(at, [8, NE])
        e8i, at = view(at, [NE], i32)
        pe8, at = view(at, [NT, NE])
        p1, at = view(at, [NT, NE])
        sf, at = view(at, [NT, 2])
        rq, at = view(at, [4 * NT])
        rqm, rqs, rqr = rq[:, 0:NT], rq[:, NT:2 * NT], rq[:, 2 * NT:3 * NT]
        onec, at = view(at, [1])
        rq_e, at = view(at, [MT])
        dft, at = view(at, [3, KC, D])
        fw, at = view(at, [2, KC, D])
        fa, at = view(at, [2, KC, D])
        assert at <= AW, at
        at = 0
        xs, at = view(at, [2, 2, D], fp16)
        exT, at = view(at, [2, 2, KC, P], fp16)
        g, at = view(at, [2, CH, P])
        gs, at = view(at, [2, 2, CH, P], fp16)
        y, at = view(at, [2, D])
        b2bc, at = view(at, [NE, D])
        mixr, at = view(at, [2, 1], i32)
        wst1, at = view(at, [KC, 3 * D])
        assert at <= AW, at
        wst1o = stage[:, 0, 0:KC * D].rearrange("p (a b) -> p a b", a=KC)
        sflat = stage[:].rearrange("p a b -> p (a b)")
        yg = sflat[:, 0:4 * D].rearrange("p (a b c) -> p a b c", a=2, b=2)
        hs1 = [sflat[:, 4 * D + D * i:4 * D + D * (i + 1)].bitcast(fp16).rearrange("p (a b) -> p a b", a=2) for i in range(2)]
        mn = sflat[:, 6 * D:8 * D]

        psT = [ctx.enter_context(nc.psum_tensor(f"psT{i}", [P, 512], fp32)) for i in range(2)]
        psS = ctx.enter_context(nc.psum_tensor("psS", [P, 4, 512], fp32))
        psO = [ctx.enter_context(nc.psum_tensor(f"psO{i}", [P, 512], fp32)) for i in range(2)]
        psTh = [t[:, 0:256].bitcast(fp16).rearrange("p (a b) -> p a b", a=4) for t in psT]


        ld_x, ld_ident, ld_small = sem("ld_x"), sem("ld_ident"), sem("ld_small")
        ld_w = sem("ld_w")
        ld_tab = sem("ld_tab")
        w_hi, w_lo = sem("w_hi"), sem("w_lo")
        pos_r, posT_r, posi_r = sem("pos_r"), sem("posT_r"), sem("posi_r")
        mexp_r, ones_r = sem("mexp_r"), sem("ones_r")
        t_var, t_pow, t_split, t_T, t_xT, t_mm = (sem(n) for n in ("t_var", "t_pow", "t_split", "t_T", "t_xT", "t_mm"))
        t_u, t_sum, t_rn, t_out, t_v, t_wr = (sem(n) for n in ("t_u", "t_sum", "t_rn", "t_out", "t_v", "t_wr"))
        g_qk = [sem("g_qk0"), sem("g_qk1")]
        g_h = [sem("g_h0"), sem("g_h1")]
        g_v = [sem("g_v0"), sem("g_v1")]
        pos_x = sem("pos_x")
        rope_r, split_r, hx_r = sem("rope_r"), sem("split_r"), sem("hx_r")
        tr_r, qk_r = sem("tr_r"), sem("qk_r")
        sc_r, ex_r, av_r = sem("sc_r"), sem("ex_r"), sem("av_r")
        no_r, osp_r = sem("no_r"), sem("osp_r")
        ot_r, otc_r, wo_r = sem("ot_r"), sem("otc_r"), sem("wo_r")
        var_r, pw_r, hs_r = sem("var_r"), sem("pw_r"), sem("hs_r")
        xn_w = [sem("xn_w0"), sem("xn_w1")]
        ht_r, htc_r, lgp_r, lgs_r = sem("ht_r"), sem("htc_r"), sem("lgp_r"), sem("lgs_r")
        h_r = sem("h_r")
        st_ld = [sem("st_ld0"), sem("st_ld1")]
        st_hi, st_free = sem("st_hi"), sem("st_free")
        dch, ach, pch = sem("dch"), sem("ach"), sem("pch")
        rt_a = sem("rt_a")
        w1_hi, w1_lo, w1_ld, l1_ld = sem("w1_hi"), sem("w1_lo"), sem("w1_ld"), sem("l1_ld")
        f_a, f_ac, f_m, f_mh, f_ml = (sem(n) for n in ("f_a", "f_ac", "f_m", "f_mh", "f_ml"))
        n_y = [[sem(f"n_y{k}{i}") for i in range(2)] for k in range(2)]
        (n_cmb, n_var, n_pow, n_hs, n_hT, n_hTc, n_qkv, n_x1, n_v, n_min, n_exp, n_r, n_spl, n_tr, n_qk, n_sc, n_ms, n_av,
         n_no, n_osp, n_oT, n_oTc, n_wo, n_h3, n_var2, n_pow2, n_hs2, n_gT, n_gTc, n_ff, n_out, n_hb, n_fb) = (
            sem("n_" + n) for n in ("cmb var pow hs hT hTc qkv x1 v min exp r spl tr qk sc ms av no osp oT oTc wo h3 "
                                    "var2 pow2 hs2 gT gTc ff out hb fb").split())
        rt_ld, rt_d, rt_e, rt_c, rt_tot, rt_totc, rt_pre, rt_oh, rt_inv, rt_idx = (
            sem(n) for n in ("rt_ld", "rt_d", "rt_e", "rt_c", "rt_tot", "rt_totc", "rt_pre", "rt_oh", "rt_inv", "rt_idx"))
        m_w = [sem("m_w0"), sem("m_w1")]
        m_x = [sem("m_x0"), sem("m_x1")]
        m_T, m_Tc, m_g1, m_act, m_gs, m_g2, m_y = (sem(n) for n in ("m_T", "m_Tc", "m_g1", "m_act", "m_gs", "m_g2", "m_y"))
        m_b2, m_hi = sem("m_b2"), sem("m_hi")
        m_yw = [sem("m_yw0"), sem("m_yw1")]
        out_w = sem("out_w")
        mv_t = small[:, 0:6].rearrange("p (a b) -> p a b", b=2)
        st_t = small[:, 8:26].rearrange("p (a b) -> p a b", b=6)
        bst = [small[:, 8:14], small[:, 14:20]]
        rden = small[:, 32:48].rearrange("p (a b) -> p a b", b=2)
        block = ctx.enter_context(nc.Block())

        def split3(ps, xhl, w, n0, n1, out0=0):
            k, last = 0, 3 * KC - 1
            for c in range(KC):
                for a, b in ((0, 0), (0, 1), (1, 0)):
                    m = nc.tensor.matmul(ps[:, out0:out0 + n1 - n0], xhl[:, a, c, :], w[:, c, b, n0:n1],
                                         start=(k == 0), stop=(k == last))
                    k += 1
            return m


        def table_view(a):
            return a.rearrange("(t p) n -> p t n", p=P)

        w1_v = w1.rearrange("e (c p) n -> p e c n", p=P)
        w2_v = w2.rearrange("e (g c p) n -> p e g c n", p=P, g=2)

        @block.sync
        def _(sp):
            sp.dma_start(tokx_i[0:NB, :], x).then_inc(ld_x, 16)
            sp.dma_start(jrow[0:NB, :], c_j).then_inc(ld_x, 16)
            sp.dma_start(tb, table_view(table[0:TAB * P, :])).then_inc(ld_tab, 16)
            sp.dma_start(ident[:], c_ident).then_inc(ld_ident, 16)
            sp.dma_start(identh[:], c_identh).then_inc(ld_ident, 16)
            sp.dma_start(wst, wqkv0.rearrange("(c p) n -> p c n", p=P)).then_inc(ld_w, 16)
            sp.dma_start(wst2, wo0.rearrange("(c p) n -> p c n", p=P)).then_inc(ld_w, 16)
            sp.dma_start(wst3, wr.rearrange("(c p) n -> p c n", p=P)).then_inc(ld_w, 16)
            sp.dma_start(rope[:], c_rope).then_inc(ld_small, 16)
            sp.dma_start(bias_bc[:, 0:D], bo0.partition_broadcast(P)).then_inc(ld_small, 16)
            sp.dma_start(b1s[:], b1).then_inc(ld_small, 16)
            for t in range(TAB):
                sp.wait_ge(t_out, t + 1)
                sp.dma_start(tab_qk[t * P:(t + 1) * P, :], u).then_inc(t_wr, 16)
                sp.wait_ge(t_v, t + 1)
                sp.wait_ge(ones_r, 1)
                sp.dma_start(tab_v[t * P:(t + 1) * P, :], tv.rearrange("p a b -> p (a b)")).then_inc(t_wr, 16)
            with sp.Fori(0, NB) as b:
                for q in range(4):
                    sp.wait_ge(st_free, b * 4 + q + 1)
                    if q < 2:
                        sp.dma_start(stage[:, q % 2, :], w1_v[:, bass.ds(b, 1), q, :].rearrange("p e n -> p (e n)")
                                     ).then_inc(st_ld[q % 2], 16)
                    else:
                        sp.dma_start(stage[:, q % 2, :].rearrange("p (c n) -> p c n", c=4),
                                     w2_v[:, bass.ds(b, 1), q - 2, :, :].rearrange("p e c n -> p (e c) n")
                                     ).then_inc(st_ld[q % 2], 16)
                for half in range(2):
                    sp.wait_ge(hs_r, b * 2 + half + 1)
                    sp.dma_start(table_view(xn_d)[:, bass.ds(b * 2 + half, 1), :].rearrange("p t n -> p (t n)"),
                                 hs[half].rearrange("p a b -> p (a b)")).then_inc(xn_w[half], 16)
            sp.wait_ge(xn_w[0], 16 * NB + 16)
            sp.wait_ge(xn_w[1], 16 * NB + 16)
            sp.wait_ge(lgs_r, NT + 1)
            sp.wait_ge(g_qk[0], 16 * (NB + 2))
            sp.wait_ge(g_qk[1], 16 * (NB + 2))
            sp.wait_ge(split_r, 2 * NB + 1)
            sp.wait_ge(rope_r, 2 * NB + 2)
            for dst, src in ((ltri, c_ltri), (tpre, c_tpre), (tsum, c_tsum), (iota, c_iota)):
                sp.dma_start(dst, src).then_inc(rt_ld, 16)
            sp.dma_start(dft, c_dft).then_inc(f_a, 16)
            sp.dma_start(fw[:, 0, :, :], fre.rearrange("(c p) n -> p c n", p=P)).then_inc(f_a, 16)
            sp.dma_start(fw[:, 1, :, :], fim.rearrange("(c p) n -> p c n", p=P)).then_inc(f_a, 16)
            sp.dma_start(wst1o, wout1.rearrange("(c p) n -> p c n", p=P)).then_inc(w1_ld, 16)
            sp.dma_start(bias_bc[:, 0:3 * D], bqkv1.partition_broadcast(P)).then_inc(l1_ld, 16)
            sp.dma_start(bias_bc[:, 3 * D:4 * D], bout1.partition_broadcast(P)).then_inc(l1_ld, 16)
            sp.dma_start(bias_bc[:, 4 * D:5 * D], fbias.partition_broadcast(P)).then_inc(l1_ld, 16)
            sp.wait_ge(rt_idx, 1)
            sp.wait_ge(f_ml, 1)
            sp.dma_start(b2bc.rearrange("p a b -> p (a b)"), b2.rearrange("a b -> (a b)").partition_broadcast(P)).then_inc(m_b2, 16)
            sp.dma_start(wst1, wqkv1.rearrange("(c p) n -> p c n", p=P)).then_inc(w1_ld, 16)

            def y_out(j, i):
                sp.wait_ge(m_y, j + 3)
                sp.dma_start(table_view(y_d)[:, bass.ds(j, 1), :].rearrange("p t n -> p (t n)"), y[:, i, :]).then_inc(m_yw[i], 16)

            with sp.Fori(0, MT // 2) as jj:
                for i in range(2):
                    y_out(jj * 2 + i, i)
            y_out(MT - 1, 0)
            for k in (0, 2):
                sp.dma_start(mask3[:, k, :], c_causal).then_inc(l1_ld, 16)
            with sp.Fori(0, NB) as b:
                for half in range(2):
                    sp.wait_ge(n_out, b * 2 + half + 1)
                    sp.dma_start(out.rearrange("b (s p) d -> p (b s) d", p=P)[:, bass.ds(b * 2 + half, 1), :],
                                 h[:, bass.ds(b * 2 + half, 1), :]).then_inc(out_w, 16)
            sp.wait_ge(out_w, 16 * NT)

        @block.gpsimd
        def _(pool):
            done = [0]

            def link(ins):
                ins.then_inc(pch, 1)
                done[0] = done[0] + 1
                pool.wait_ge(pch, done[0])

            nc.gpsimd.memset(tv[:, :, HD:VW], 1.0).then_inc(ones_r, 1)
            nc.gpsimd.memset(epsc[:], EPS_LN)
            nc.gpsimd.memset(mexp[:], -0.5).then_inc(mexp_r, 1)
            pool.wait_ge(mexp_r, 1)
            pool.wait_ge(t_var, 1)
            link(nc.gpsimd.tensor_scalar(small[:, 26:26 + TAB], mv_t[:, :, 1], EPS_LN, None, ALU.add))
            nc.gpsimd.tensor_tensor(small[:, 26:26 + TAB], small[:, 26:26 + TAB], mexp[:, 0:TAB], ALU.pow).then_inc(t_pow, 1)
            for t in range(TAB):
                pool.wait_ge(t_sum, t + 1)
                link(nc.gpsimd.tensor_scalar(small[:, 32:64], small[:, 32:64], EPS_QK, None, ALU.add))
                nc.gpsimd.tensor_tensor(small[:, 32:64], small[:, 32:64], mexp[:], ALU.pow).then_inc(t_rn, 1)

            def gather_qk(b, first=False):
                for half in range(2):
                    link(nc.gpsimd.tensor_copy(posx[:, 0, half, :], pos_i[:, bass.ds(b * 2 + half, 1)]))
                    nc.gpsimd.indirect_dma_start(qkg[:, half, :], None, tab_qk, bass.IndirectOffsetOnAxis(
                        ap=posx[:, 0, half, :], axis=0)).then_inc(g_qk[half], 16)

            def turn(b):
                for half in range(2):
                    xq = qkg[:, half, :].rearrange("p (a b) -> p a b", b=HD)
                    rv = r.rearrange("p (a b) -> p a b", b=HD)
                    r2v = r2.rearrange("p (a b) -> p a b", b=HD)
                    cs = rope[:, half, 0:1, :].to_broadcast([P, 2 * H, HD])
                    sn = rope[:, half, 1:2, :].to_broadcast([P, 2 * H, HD])
                    pool.wait_ge(g_qk[half], b * 16 + 16)
                    wait(pool, split_r, b * 2 + half)
                    nc.gpsimd.tensor_tensor(rv, xq, cs, ALU.mult)
                    nc.gpsimd.tensor_tensor(r2v[:, :, 0:8], xq[:, :, 8:16], sn[:, :, 0:8], ALU.mult)
                    link(nc.gpsimd.tensor_tensor(r2v[:, :, 8:16], xq[:, :, 0:8], sn[:, :, 8:16], ALU.mult))
                    nc.gpsimd.tensor_tensor(r, r, r2, ALU.add).then_inc(rope_r, 1)
                    pool.wait_ge(rope_r, b * 2 + half + 1)

            pool.wait_ge(posi_r, 2)
            pool.wait_ge(t_wr, 32 * TAB)
            pool.wait_ge(ld_small, 48)
            gather_qk(0)
            turn(0)
            gather_qk(1)
            with pool.Fori(0, NB) as b:
                pool.sem_clear(pch)
                done[0] = 0
                pool.wait_ge(av_r, b * 8 + 1)
                for half in range(2):
                    link(nc.gpsimd.tensor_copy(posx[:, 1, half, :], pos_i[:, bass.ds(b * 2 + half, 1)]))
                    nc.gpsimd.indirect_dma_start(vaug[:, half, :, :].rearrange("p a b -> p (a b)"), None, tab_v,
                                                 bass.IndirectOffsetOnAxis(ap=posx[:, 1, half, :], axis=0)
                                                 ).then_inc(g_v[half], 16)
                    nc.gpsimd.indirect_dma_start(hg[:, half, :], None, table,
                                                 bass.IndirectOffsetOnAxis(ap=posx[:, 1, half, :], axis=0)
                                                 ).then_inc(g_h[half], 16)
                turn(b + 1)
                gather_qk(b + 2)
                for half in range(2):
                    pool.wait_ge(g_h[half], b * 16 + 16)
                    pool.wait_ge(g_v[half], b * 16 + 16)
                    nc.gpsimd.tensor_tensor(h[:, bass.ds(b * 2 + half, 1), :].rearrange("p a b -> p (a b)"),
                                            hg[:, half, :], bias_bc[:, 0:D], ALU.add).then_inc(h_r, 1)
                pool.wait_ge(h_r, b * 2 + 2)
                for half in range(2):
                    pool.wait_ge(var_r, b * 2 + half + 1)
                    link(nc.gpsimd.tensor_tensor(small[:, 4 * half + 2:4 * half + 3], small[:, 4 * half + 1:4 * half + 2],
                                                 epsc[:], ALU.add))
                    nc.gpsimd.tensor_tensor(small[:, 4 * half + 2:4 * half + 3], small[:, 4 * half + 2:4 * half + 3],
                                            mexp[:, 0:1], ALU.pow).then_inc(pw_r, 1)
            pool.sem_clear(pch)
            done[0] = 0
            pool.wait_ge(g_qk[0], 16 * (NB + 2))
            pool.wait_ge(g_qk[1], 16 * (NB + 2))

            pool.wait_ge(rt_idx, 1)
            pool.wait_ge(f_ml, 1)
            pool.wait_ge(xn_w[0], 16 * NB + 16)
            pool.wait_ge(xn_w[1], 16 * NB + 16)
            pool.sem_inc(m_T, 2)

            def token_rows(j, i):
                pool.wait_ge(m_T, j + 1)
                link(nc.gpsimd.tensor_copy(mixr[:, i, :], inv_i[:, bass.ds(j, 1)]))
                nc.gpsimd.indirect_dma_start(xs[:, i, :, :].rearrange("p a b -> p (a b)"), None, xn_d,
                                             bass.IndirectOffsetOnAxis(ap=mixr[:, i, :], axis=0)).then_inc(m_x[i], 16)

            with pool.Fori(0, MT // 2) as jj:
                pool.sem_clear(pch)
                done[0] = 0
                for i in range(2):
                    token_rows(jj * 2 + i, i)
            token_rows(MT - 1, 0)

            def slot_rows(b):
                for half in range(2):
                    for k in range(2):
                        link(nc.gpsimd.tensor_copy(posy[:, k, half, :], slot_i[:, bass.ds(b * 2 + half, 1), k]))
                        nc.gpsimd.indirect_dma_start(yg[:, k, half, :], None, y_d, bass.IndirectOffsetOnAxis(
                            ap=posy[:, k, half, :], axis=0)).then_inc(n_y[k][half], 16)

            def inverse_root(half, count, raised):
                pool.wait_ge(raised[0], count)
                a = small[:, 4 * half + 2:4 * half + 3]
                link(nc.gpsimd.tensor_tensor(a, small[:, 4 * half + 1:4 * half + 2], epsc[:], ALU.add))
                nc.gpsimd.tensor_tensor(a, a, mexp[:, 0:1], ALU.pow).then_inc(raised[1], 1)

            pool.wait_ge(m_yw[0], 16 * ((MT + 1) // 2) + 16)
            pool.wait_ge(m_yw[1], 16 * (MT // 2) + 16)
            pool.wait_ge(l1_ld, 80)
            slot_rows(0)
            with pool.Fori(0, NB) as b:
                pool.sem_clear(pch)
                done[0] = 0
                for half in range(2):
                    inverse_root(half, b * 2 + half + 1, (n_var, n_pow))
                for half in range(2):
                    pool.wait_ge(n_hs, b * 2 + half + 1)
                    ht = h[:, bass.ds(b * 2 + half, 1), :].rearrange("p a b -> p (a b)")
                    nc.gpsimd.tensor_tensor(ht, ht, bias_bc[:, 3 * D:4 * D], ALU.add).then_inc(n_hb, 1)
                slot_rows(b + 1)
                for half in range(2):
                    inverse_root(half, b * 2 + half + 1, (n_var2, n_pow2))
            for k in range(2):
                for half in range(2):
                    pool.wait_ge(n_y[k][half], 16 * (NB + 1))

        @block.scalar
        def _(act):
            act.wait_ge(ld_w, 48)
            nc.scalar.activation(wA[:, :, 0, :], wst, ACT.Copy, scale=WS).then_inc(w_hi, 1)
            nc.scalar.activation(wB[:, :, 0, :], wst2, ACT.Copy, scale=WS).then_inc(w_hi, 1)
            nc.scalar.activation(wR[:, :, 0, :], wst3, ACT.Copy, scale=WS).then_inc(w_hi, 1)
            for t in range(TAB):
                act.wait_ge(t_mm, t + 1)
                wait(act, t_wr, 32 * t)
                nc.scalar.activation(u, psS[:, 0, :], ACT.Copy, scale=1.0 / WS).then_inc(t_u, 1)
                nc.scalar.activation(tv[:, :, 0:HD], psS[:, 1, 0:D].rearrange("p (a b) -> p a b", b=HD),
                                     ACT.Copy, scale=1.0 / WS).then_inc(t_v, 1)
            act.wait_ge(t_wr, 32 * TAB)
            act.sem_inc(ex_r, 1)
            with act.Fori(0, NB) as b:
                for p in range(8):
                    act.wait_ge(sc_r, b * 8 + p + 1)
                    act.wait_ge(av_r, b * 8 + max(p - 1, 0) + 1)
                    nc.scalar.activation(E[:, p % 2, :, :], psS[:, 2 * (p % 2):2 * (p % 2) + 2, :], ACT.Exp,
                                         scale=HD ** -0.5).then_inc(ex_r, 1)
                    if p % 2:
                        q = p // 2
                        act.wait_ge(st_ld[q % 2], b * 32 + 16 * (q // 2) + 16)
                        nc.scalar.activation(WX[:, bass.ds(b, 1), q, 0, :].rearrange("p e n -> p (e n)"),
                                             stage[:, q % 2, :], ACT.Copy, scale=WS).then_inc(st_hi, 1)

            act.wait_ge(rt_d, 1)
            nc.scalar.activation(pe8, pe8, ACT.Exp).then_inc(rt_e, 1)
            nc.scalar.activation(rqm, rqm, ACT.Exp).then_inc(rt_e, 1)
            act.wait_ge(f_m, 1)
            nc.scalar.activation(wM[:, :, 0, :], psS[:, 0:2, 0:D], ACT.Copy, scale=WS / D).then_inc(f_mh, 1)
            act.wait_ge(w1_ld, 32)
            nc.scalar.activation(wB[:, :, 0, :], wst1o, ACT.Copy, scale=WS).then_inc(w1_hi, 1)
            nc.scalar.activation(wA[:, :, 0, :], wst1, ACT.Copy, scale=WS).then_inc(w1_hi, 1)
            act.wait_ge(rt_idx, 1)
            act.wait_ge(f_ml, 1)

            def gelu(j, i):
                e = act.value_load(ej[0:1, bass.ds(j, 1)], min_val=0, max_val=NE - 1)
                for q in range(2):
                    act.wait_ge(m_g1, j * 2 + q + 3)
                    act.wait_ge(m_gs, j * 2 + q + 1)
                    for c in range(4 * q, 4 * q + 4):
                        last = nc.scalar.activation(g[:, i, c, :], psS[:, 2 * i + q, (c % 4) * P:(c % 4 + 1) * P],
                                                    ACT.Gelu_apprx_tanh, bias=b1s[:, bass.ds(e, 1), c], scale=1.0 / WS)
                    last.then_inc(m_act, 1)

            with act.Fori(0, MT // 2) as jj:
                for i in range(2):
                    gelu(jj * 2 + i, i)
            gelu(MT - 1, 0)
            with act.Fori(0, NB) as b:
                for half in range(2):
                    act.wait_ge(n_min, b * 2 + half + 1)
                    nc.scalar.activation(mn, mn, ACT.Exp).then_inc(n_exp, 1)

        @block.vector
        def _(dve):
            done = [0]

            def link(ins):
                ins.then_inc(dch, 1)
                done[0] = done[0] + 1
                dve.wait_ge(dch, done[0])

            V = nc.vector
            link(V.memset(pos_i[:], 0))
            dve.wait_ge(ld_x, 32)
            tk, tj = tokf[0:NB, :], jrow[0:NB, :]
            link(V.tensor_copy(tk, tokx_i[0:NB, :]))
            V.tensor_scalar(tm[0:NB, :], tk, 1.0, None, ALU.not_equal)
            link(V.scalar_tensor_tensor(tsp[0:NB, :], tk, 4.0, tj, ALU.is_equal, ALU.mult))
            V.tensor_tensor_scan(tva[0:NB, :], tm[0:NB, :], tm[0:NB, :], 1.0, ALU.mult, ALU.mult)
            link(V.tensor_tensor_scan(tls[0:NB, :], tsp[0:NB, :], tsp[0:NB, :], 0.0, ALU.max, ALU.max))
            link(V.tensor_tensor(tls[0:NB, :], tj, tls[0:NB, :], ALU.subtract))
            link(V.scalar_tensor_tensor(tls[0:NB, :], tls[0:NB, :], 1.0, tva[0:NB, :], ALU.add, ALU.mult))
            V.tensor_scalar(tls[0:NB, :], tls[0:NB, :], 1.0, None, ALU.add).then_inc(pos_r, 1)
            dve.wait_ge(ld_tab, 16)
            for t in range(TAB):
                last = V.bn_stats(st_t[:, t, :], tb[:, t, :])
            link(last)
            for t in range(TAB):
                last = V.bn_aggr(mv_t[:, t, :], st_t[:, t, :])
            last.then_inc(t_var, 1)
            dve.wait_ge(posT_r, 1)
            V.tensor_copy(pos_i[:, 0:NT].rearrange("p (b s) -> p s b", s=2),
                          psT[1][:, 0:NT].rearrange("p (s b) -> p s b", s=2)).then_inc(posi_r, 2)
            for w, st, n in ((wA, wst, 1), (wB, wst2, 2), (wR, wst3, 3)):
                dve.wait_ge(w_hi, n)
                V.scalar_tensor_tensor(w[:, :, 1, :], st, WS, w[:, :, 0, :], ALU.mult, ALU.subtract).then_inc(w_lo, 1)
            dve.wait_ge(t_pow, 1)
            for t in range(TAB):
                link(V.tensor_scalar(thn, tb[:, t, :], mv_t[:, t, 0:1], small[:, 26 + t:27 + t], ALU.subtract, ALU.mult))
                wait(dve, t_T, t)
                link(V.tensor_copy(ths[:, 0, :], thn))
                V.tensor_tensor(ths[:, 1, :], thn, ths[:, 0, :], ALU.subtract).then_inc(t_split, 1)
                dve.wait_ge(t_T, t + 1)
                wait(dve, t_mm, t)
                V.tensor_copy(txT.rearrange("p a b c -> p (a b) c"), psTh[0]).then_inc(t_xT, 1)
                dve.wait_ge(t_u, t + 1)
                link(V.tensor_tensor(usq, u, u, ALU.mult))
                wait(dve, t_rn, t)
                V.tensor_reduce(small[:, 32:64], usq.rearrange("p (a b) -> p a b", b=HD), AX.X, ALU.add).then_inc(t_sum, 1)
                dve.wait_ge(t_rn, t + 1)
                V.tensor_tensor(u.rearrange("p (a b) -> p a b", b=HD), u.rearrange("p (a b) -> p a b", b=HD),
                                small[:, 32:64].unsqueeze(2).to_broadcast([P, 2 * H, HD]), ALU.mult).then_inc(t_out, 1)
            dve.wait_ge(t_wr, 32 * TAB)
            V.memset(small[:, 0:1], 0.0).then_inc(st_free, 2)

            def split_row(ready):
                rv = r.rearrange("p (a b) -> p a b", b=HD)
                link(V.tensor_copy(hl[:, :, 0, :], rv))
                link(V.tensor_tensor(hl[:, :, 1, :], rv, hl[:, :, 0, :], ALU.subtract))
                V.tensor_copy(hl[:, 0:H, 2:4, :], hl[:, 0:H, 0:2, :])
                V.tensor_copy(hl[:, H:2 * H, 2, :], hl[:, H:2 * H, 1, :])
                V.tensor_copy(hl[:, H:2 * H, 3, :], hl[:, H:2 * H, 0, :]).then_inc(ready, 1)

            def split_heads(b, half):
                dve.wait_ge(rope_r, b * 2 + half + 1)
                split_row(split_r)

            def stage_low(b, q):
                dve.wait_ge(st_hi, b * 4 + q + 1)
                hi = WX[:, bass.ds(b, 1), q, 0, :].rearrange("p e n -> p (e n)")
                lo = WX[:, bass.ds(b, 1), q, 1, :].rearrange("p e n -> p (e n)")
                V.scalar_tensor_tensor(lo, stage[:, q % 2, :], WS, hi, ALU.mult, ALU.subtract).then_inc(st_free, 1)

            split_heads(0, 0)
            dve.sem_inc(no_r, 1)
            dve.sem_inc(lgs_r, 1)
            dve.sem_inc(xn_w[0], 16)
            dve.sem_inc(xn_w[1], 16)
            with dve.Fori(0, NB) as b:
                dve.sem_clear(dch)
                done[0] = 0
                for half in range(2):
                    for pg in range(4):
                        dve.wait_ge(tr_r, b * 8 + half * 4 + pg + 1)
                        V.tensor_copy(qkT[:, 2 * pg:2 * pg + 2, :, half * P:(half + 1) * P],
                                      psTh[pg % 2].rearrange("p (a b) c -> p a b c", a=2)).then_inc(qk_r, 1)
                    split_heads(b + half, 1 - half)
                for gp in range(2):
                    stage_low(b, 2 * gp)
                    stage_low(b, 2 * gp + 1)
                    dve.wait_ge(av_r, b * 8 + 4 * gp + 5)
                    av = psO[gp][:, 0:8 * 2 * VW].rearrange("p (a b c) -> p a b c", a=8, b=2)
                    ov = o[:, :, gp * P:(gp + 1) * P].rearrange("p b (a c) -> p a b c", c=HD)
                    link(V.reciprocal(rden, av[:, :, :, HD]))
                    V.tensor_tensor(ov, av[:, :, :, 0:HD], rden.unsqueeze(3).to_broadcast([P, 8, 2, HD]),
                                    ALU.mult).then_inc(no_r, 1)
                    dve.wait_ge(no_r, b * 2 + gp + 2)
                    og = o[:, :, gp * P:(gp + 1) * P]
                    link(V.tensor_copy(osp[:, :, 0, gp * P:(gp + 1) * P], og))
                    V.tensor_tensor(osp[:, :, 1, gp * P:(gp + 1) * P], og, osp[:, :, 0, gp * P:(gp + 1) * P],
                                    ALU.subtract).then_inc(osp_r, 1)
                for half in range(2):
                    dve.wait_ge(ot_r, b * 2 + half + 1)
                    V.tensor_copy(xT[half].rearrange("p a b c -> p (a b) c"), psTh[half]).then_inc(otc_r, 1)
                for half in range(2):
                    ht = h[:, bass.ds(b * 2 + half, 1), :].rearrange("p a b -> p (a b)")
                    dve.wait_ge(wo_r, b * 2 + half + 1)
                    dve.wait_ge(h_r, b * 2 + half + 1)
                    link(V.scalar_tensor_tensor(ht, psT[half][:, 0:D], 1.0 / WS, ht, ALU.mult, ALU.add))
                    link(V.bn_stats(bst[half], ht))
                    V.bn_aggr(small[:, 4 * half:4 * half + 2], bst[half]).then_inc(var_r, 1)
                for half in range(2):
                    ht = h[:, bass.ds(b * 2 + half, 1), :].rearrange("p a b -> p (a b)")
                    dve.wait_ge(pw_r, b * 2 + half + 1)
                    link(V.tensor_scalar(hn, ht, small[:, 4 * half:4 * half + 1], small[:, 4 * half + 2:4 * half + 3],
                                         ALU.subtract, ALU.mult))
                    dve.wait_ge(xn_w[half], b * 16 + 16)
                    link(V.tensor_copy(hs[half][:, 0, :], hn))
                    V.tensor_tensor(hs[half][:, 1, :], hn, hs[half][:, 0, :], ALU.subtract).then_inc(hs_r, 1)
                    dve.wait_ge(hs_r, b * 2 + half + 1)
                for half in range(2):
                    dve.wait_ge(ht_r, b * 2 + half + 1)
                    V.tensor_copy(xT[half].rearrange("p a b c -> p (a b) c"), psTh[half]).then_inc(htc_r, 1)
                for half in range(2):
                    dve.wait_ge(lgp_r, b * 2 + half + 1)
                    link(V.tensor_scalar(lg[:], psT[half][:, 0:NE], 1.0 / WS, None, ALU.mult))
                    link(V.max(mx8[:], lg[:]))
                    link(V.max_index(ix8[:], mx8[:], lg[:]))
                    V.tensor_copy(lgt[:, bass.ds(b * 2 + half, 1), :].rearrange("p a b -> p (a b)"), lg[:])
                    V.tensor_copy(mxt[:, bass.ds(b * 2 + half, 1), :].rearrange("p a b -> p (a b)"), mx8[:, 0:2])
                    V.tensor_copy(ixt[:, bass.ds(b * 2 + half, 1), :].rearrange("p a b -> p (a b)"),
                                  ix8[:, 0:2]).then_inc(lgs_r, 1)
                    dve.wait_ge(lgs_r, b * 2 + half + 2)
            dve.sem_clear(dch)
            done[0] = 0

            dve.wait_ge(rt_ld, 64)
            mx0 = mxt[:, :, 0]
            V.memset(onec, 1.0)
            V.memset(e8[:, 3, :], 0.0)
            V.memset(slot_i[:], 0)
            V.tensor_tensor(m0, ioe.unsqueeze(1).to_broadcast([P, NT, NE]), ixt[:, :, 0:1].to_broadcast([P, NT, NE]), ALU.is_equal)
            link(V.tensor_tensor(m1, ioe.unsqueeze(1).to_broadcast([P, NT, NE]), ixt[:, :, 1:2].to_broadcast([P, NT, NE]), ALU.is_equal))
            V.tensor_tensor(mc, m0, m1, ALU.add).then_inc(rt_c, 1)
            V.tensor_tensor(rqm, mxt[:, :, 1], mx0, ALU.subtract)
            V.tensor_tensor(pe8, lgt[:], mxt[:, :, 0:1].to_broadcast([P, NT, NE]), ALU.subtract).then_inc(rt_d, 1)
            dve.wait_ge(rt_tot, 1)
            V.tensor_copy(totb, psO[0][:, 0:1].to_broadcast([P, P])).then_inc(rt_totc, 1)
            dve.wait_ge(rt_e, 2)
            link(V.tensor_reduce(rqs, pe8, AX.X, ALU.add))
            link(V.reciprocal(gate[:, :, 0], rqs))
            V.tensor_tensor(gate[:, :, 1], gate[:, :, 0], rqm, ALU.mult)
            dve.wait_ge(rt_pre, 1)
            link(V.tensor_scalar(e8i, psT[0][:, 0:NE], float(P - 1), None, ALU.add))
            link(V.tensor_scalar(e8i, e8i, 7, None, ALU.logical_shift_right))
            link(V.tensor_copy(e8[:, 1, :], e8i))
            link(V.tensor_tensor_scan(e8[:, 2, :], e8[:, 1, :], e8[:, 3, :], 0.0, ALU.add, ALU.add))
            link(V.tensor_tensor(e8[:, 4, :], e8[:, 2, :], e8[:, 1, :], ALU.subtract))
            link(V.tensor_scalar(e8[:, 5, :], e8[:, 4, :], float(P), None, ALU.mult))
            link(V.tensor_tensor(p1, psO[1][:, 0:P].rearrange("p (a b) -> p a b", b=NE),
                                 e8[:, 5:6, :].to_broadcast([P, NT, NE]), ALU.add))
            V.tensor_tensor(m0, m0, p1, ALU.mult)
            link(V.tensor_tensor(m1, m1, p1, ALU.mult))
            V.tensor_reduce(sf[:, :, 0], m0, AX.X, ALU.add)
            link(V.tensor_reduce(sf[:, :, 1], m1, AX.X, ALU.add))
            link(V.tensor_copy(slot_i[:, 0:NT, :], sf))
            si = slot_i[:, 0:NT, :].rearrange("p a b -> p (a b)")
            V.tensor_scalar(ri, si, 7, None, ALU.logical_shift_right)
            link(V.tensor_scalar(ri2, si, P - 1, None, ALU.bitwise_and))
            V.tensor_copy(ra, ri)
            link(V.tensor_copy(rb, ri2))
            V.tensor_tensor(ohb, iob.unsqueeze(1).to_broadcast([P, 2 * NT, P]), rb.unsqueeze(2).to_broadcast([P, 2 * NT, P]), ALU.is_equal)
            link(V.tensor_tensor(oha, ioa.unsqueeze(1).to_broadcast([P, 2 * NT, MT]), ra.unsqueeze(2).to_broadcast([P, 2 * NT, MT]), ALU.is_equal))
            oh2 = oha.rearrange("p (a b) c -> p a (b c)", b=2)
            V.tensor_tensor(oh2, oh2, tokid.unsqueeze(2).to_broadcast([P, NT, 2 * MT]), ALU.mult).then_inc(rt_oh, 1)
            link(V.tensor_tensor(ecmp[0:1], ioa[0:1].unsqueeze(2).to_broadcast([1, MT, NE]),
                                 e8[0:1, 2:3, :].to_broadcast([1, MT, NE]), ALU.is_ge))
            link(V.tensor_reduce(rq_e[0:1], ecmp[0:1], AX.X, ALU.add))
            V.tensor_scalar(ej[:], rq_e[0:1], float(NE - 1), None, ALU.min)
            dve.wait_ge(rt_inv, 1)
            V.tensor_copy(inv_i[:], psT[1][:, 0:MT]).then_inc(rt_idx, 1)
            dve.wait_ge(f_ac, 1)
            V.tensor_copy(fa.rearrange("p a b c -> p (a b) c"), psS[:, :, 0:D]).then_inc(f_ac, 1)
            dve.wait_ge(f_mh, 1)
            V.scalar_tensor_tensor(wM[:, :, 1, :], psS[:, 0:2, 0:D], WS / D, wM[:, :, 0, :], ALU.mult, ALU.subtract).then_inc(f_ml, 1)
            for w, st, n in ((wB, wst1o, 1), (wA, wst1, 2)):
                dve.wait_ge(w1_hi, n)
                V.scalar_tensor_tensor(w[:, :, 1, :], st, WS, w[:, :, 0, :], ALU.mult, ALU.subtract).then_inc(w1_lo, 1)
            dve.sem_inc(m_y, 2)
            dve.sem_inc(m_yw[0], 16)
            dve.sem_inc(m_yw[1], 16)
            dve.sem_inc(m_gs, 4)
            dve.wait_ge(m_b2, 16)

            def rows_in(j, i):
                dve.wait_ge(m_T, j + 3)
                V.tensor_copy(exT[:, i, :, :, :].rearrange("p a b c -> p (a b) c"), psTh[i]).then_inc(m_Tc, 1)

            def split_hidden(j, i):
                for q in range(2):
                    c = slice(4 * q, 4 * q + 4)
                    dve.wait_ge(m_act, j * 2 + q + 1)
                    dve.wait_ge(m_g2, j + 1)
                    V.tensor_copy(gs[:, i, 0, c, :], g[:, i, c, :]).then_inc(m_hi, 1)
                    dve.wait_ge(m_hi, j * 2 + q + 1)
                    V.tensor_tensor(gs[:, i, 1, c, :], g[:, i, c, :], gs[:, i, 0, c, :], ALU.subtract).then_inc(m_gs, 1)

            def y_in(j, i):
                e = dve.value_load(ej[0:1, bass.ds(j, 1)], min_val=0, max_val=NE - 1)
                dve.wait_ge(m_g2, j + 3)
                V.scalar_tensor_tensor(y[:, i, :], psO[i][:, 0:D], 1.0 / WS, b2bc[:, bass.ds(e, 1), :].rearrange("p a b -> p (a b)"),
                                       ALU.mult, ALU.add).then_inc(m_y, 1)

            def y_free(i, n):
                dve.wait_ge(m_yw[i], n)

            rows_in(0, 0)
            rows_in(1, 1)
            split_hidden(0, 0)
            with dve.Fori(0, MT // 2 - 1) as jj:
                for i in (1, 0):
                    j = jj * 2 + (1 if i else 2)
                    rows_in(j + 1, 1 - i)
                    split_hidden(j, i)
                    dve.wait_ge(m_yw[1 - i], jj * 16 + 16)
                    y_in(j - 1, 1 - i)
            for j in (MT - 2, MT - 1):
                i = j % 2
                if j + 1 < MT:
                    rows_in(j + 1, 1 - i)
                split_hidden(j, i)
                dve.wait_ge(m_yw[1 - i], 16 * ((j - 1) // 2) + 16)
                y_in(j - 1, 1 - i)
            dve.wait_ge(m_yw[0], 16 * ((MT - 1) // 2) + 16)
            y_in(MT - 1, 0)

            dve.wait_ge(m_yw[0], 16 * ((MT + 1) // 2) + 16)
            dve.wait_ge(m_yw[1], 16 * (MT // 2) + 16)
            dve.wait_ge(l1_ld, 80)
            V.memset(mask3[:, 1, :], 1.0)
            link(V.memset(vaug[:, :, :, HD:VW], 1.0))

            def row(b, half):
                return h[:, bass.ds(b * 2 + half, 1), :].rearrange("p a b -> p (a b)")

            def normalised(b, half, powered, ready):
                dve.wait_ge(powered, b * 2 + half + 1)
                link(V.tensor_scalar(hn, row(b, half), small[:, 4 * half:4 * half + 1], small[:, 4 * half + 2:4 * half + 3],
                                     ALU.subtract, ALU.mult))
                link(V.tensor_copy(hs1[half][:, 0, :], hn))
                V.tensor_tensor(hs1[half][:, 1, :], hn, hs1[half][:, 0, :], ALU.subtract).then_inc(ready, 1)
                dve.wait_ge(ready, b * 2 + half + 1)

            with dve.Fori(0, NB) as b:
                dve.sem_clear(dch)
                done[0] = 0
                for half in range(2):
                    ht = row(b, half)
                    gt = gate[:, bass.ds(b * 2 + half, 1), :].rearrange("p a b -> p (a b)")
                    dve.wait_ge(n_y[0][half], b * 16 + 16)
                    dve.wait_ge(n_y[1][half], b * 16 + 16)
                    link(V.scalar_tensor_tensor(ht, yg[:, 0, half, :], gt[:, 0:1], ht, ALU.mult, ALU.add))
                    link(V.scalar_tensor_tensor(ht, yg[:, 1, half, :], gt[:, 1:2], ht, ALU.mult, ALU.add))
                    link(V.bn_stats(bst[half], ht))
                    V.bn_aggr(small[:, 4 * half:4 * half + 2], bst[half]).then_inc(n_var, 1)
                for half in range(2):
                    normalised(b, half, n_pow, n_hs)
                for half in range(2):
                    dve.wait_ge(n_hT, b * 2 + half + 1)
                    V.tensor_copy(xT[half].rearrange("p a b c -> p (a b) c"), psTh[half]).then_inc(n_hTc, 1)
                for half in range(2):
                    dve.wait_ge(n_qkv, b * 2 + half + 1)
                    V.scalar_tensor_tensor(x1[:, 0:2 * D], psS[:, 2 * half, :], 1.0 / WS, bias_bc[:, 0:2 * D],
                                           ALU.mult, ALU.add).then_inc(n_x1, 1)
                    V.scalar_tensor_tensor(vaug[:, half, :, 0:HD], psS[:, 2 * half + 1, 0:D].rearrange("p (a b) -> p a b", b=HD),
                                           1.0 / WS, bias_bc[:, 2 * D:3 * D].rearrange("p (a b) -> p a b", b=HD),
                                           ALU.mult, ALU.add).then_inc(n_v, 1)
                    dve.wait_ge(n_x1, b * 2 + half + 1)
                    V.tensor_scalar(mn, x1[:, 0:2 * D], 0.0, None, ALU.min).then_inc(n_min, 1)
                    dve.wait_ge(n_exp, b * 2 + half + 1)
                    link(V.scalar_tensor_tensor(r, x1[:, 0:2 * D], 0.0, mn, ALU.max, ALU.add))
                    split_row(n_spl)
                    for pg in range(4):
                        dve.wait_ge(n_tr, b * 8 + half * 4 + pg + 1)
                        V.tensor_copy(qkT[:, 2 * pg:2 * pg + 2, :, half * P:(half + 1) * P],
                                      psTh[pg % 2].rearrange("p (a b) c -> p a b c", a=2)).then_inc(n_qk, 1)
                for p in range(8):
                    dve.wait_ge(n_sc, b * 8 + p + 1)
                    if p >= 2:
                        dve.wait_ge(n_av, b * 8 + p - 1)
                    ev = E[:, p % 2, :, 0:3 * P]
                    for e in range(2):
                        last = V.tensor_tensor(ev[:, e, :], psS[:, 2 * (p % 2) + e, 0:3 * P],
                                               mask3[:].rearrange("p a b -> p (a b)"), ALU.mult)
                    last.then_inc(n_ms, 1)
                    if p in (4, 7):
                        gp = 0 if p == 4 else 1
                        dve.wait_ge(n_av, b * 8 + 4 * gp + 4)
                        av = psO[gp][:, 0:8 * 2 * VW].rearrange("p (a b c) -> p a b c", a=8, b=2)
                        ov = o[:, :, gp * P:(gp + 1) * P].rearrange("p b (a c) -> p a b c", c=HD)
                        link(V.tensor_scalar(rden, av[:, :, :, HD], EPS_L1, None, ALU.add))
                        link(V.reciprocal(rden, rden))
                        link(V.tensor_tensor(ov, av[:, :, :, 0:HD], rden.unsqueeze(3).to_broadcast([P, 8, 2, HD]), ALU.mult))
                        og = o[:, :, gp * P:(gp + 1) * P]
                        link(V.tensor_copy(osp[:, :, 0, gp * P:(gp + 1) * P], og))
                        V.tensor_tensor(osp[:, :, 1, gp * P:(gp + 1) * P], og, osp[:, :, 0, gp * P:(gp + 1) * P],
                                        ALU.subtract).then_inc(n_osp, 1)
                for half in range(2):
                    dve.wait_ge(n_oT, b * 2 + half + 1)
                    V.tensor_copy(xT[half].rearrange("p a b c -> p (a b) c"), psTh[half]).then_inc(n_oTc, 1)
                for half in range(2):
                    ht = row(b, half)
                    dve.wait_ge(n_wo, b * 2 + half + 1)
                    dve.wait_ge(n_hb, b * 2 + half + 1)
                    link(V.scalar_tensor_tensor(ht, psT[half][:, 0:D], 1.0 / WS, ht, ALU.mult, ALU.add))
                    link(V.bn_stats(bst[half], ht))
                    V.bn_aggr(small[:, 4 * half:4 * half + 2], bst[half]).then_inc(n_var2, 1)
                for half in range(2):
                    normalised(b, half, n_pow2, n_hs2)
                    V.tensor_tensor(row(b, half), row(b, half), bias_bc[:, 4 * D:5 * D], ALU.add).then_inc(n_fb, 1)
                for half in range(2):
                    dve.wait_ge(n_gT, b * 2 + half + 1)
                    V.tensor_copy(xT[half].rearrange("p a b c -> p (a b) c"), psTh[half]).then_inc(n_gTc, 1)
                for half in range(2):
                    ht = row(b, half)
                    dve.wait_ge(n_ff, b * 2 + half + 1)
                    dve.wait_ge(n_fb, b * 2 + half + 1)
                    V.scalar_tensor_tensor(ht, psT[half][:, 0:D], 1.0 / WS, ht, ALU.mult, ALU.add).then_inc(n_out, 1)
                dve.wait_ge(n_out, b * 2 + 2)

        @block.tensor
        def _(pe):
            M, TR = nc.tensor.matmul, nc.tensor.transpose

            def transpose_rows(ps, rows):
                for a in range(2):
                    for c in range(KC):
                        last = TR(ps[:, a * KC + c, :], rows[:, a, c * P:(c + 1) * P], identh[:])
                return last

            pe.wait_ge(ld_ident, 32)
            pe.wait_ge(pos_r, 1)
            for sq in range(2):
                last = TR(psT[1][:, sq * NB:(sq + 1) * NB], tls[0:NB, sq * P:(sq + 1) * P], ident[:])
            last.then_inc(posT_r, 1)
            pe.wait_ge(w_lo, 3)
            for t in range(TAB):
                pe.wait_ge(t_split, t + 1)
                transpose_rows(psTh[0], ths).then_inc(t_T, 1)
                pe.wait_ge(t_xT, t + 1)
                wait(pe, t_v, t)
                split3(psS[:, 0, :], txT, wA, 0, 2 * D)
                split3(psS[:, 1, :], txT, wA, 2 * D, 3 * D).then_inc(t_mm, 1)
            pe.wait_ge(posi_r, 2)
            pe.sem_inc(av_r, 1)
            with pe.Fori(0, NB) as b:
                pe.wait_ge(lgs_r, b * 2 + 1)
                for half in range(2):
                    pe.wait_ge(split_r, b * 2 + half + 1)
                    for pg in range(4):
                        if half or pg >= 2:
                            pe.wait_ge(qk_r, b * 8 + half * 4 + pg - 1)
                        for a in range(2):
                            for qk in range(2):
                                hd = qk * H + 4 * pg + 2 * a
                                last = TR(psTh[pg % 2][:, 2 * a + qk, :],
                                          hl[:, hd:hd + 2, :, :].rearrange("p a b c -> p (a b c)"), identh[:])
                        last.then_inc(tr_r, 1)
                for p in range(9):
                    if p < 8:
                        pe.wait_ge(qk_r, b * 8 + 5 + p // 2)
                        pe.wait_ge(ex_r, b * 8 + max(p - 1, 0) + 1)
                        for e in range(2):
                            rows = slice(64 * e, 64 * e + 64)
                            for st in range(2):
                                last = M(psS[:, 2 * (p % 2) + e, st * T:(st + 1) * T],
                                         qkT[rows, p, 1, st * P:(st + 1) * P], qkT[rows, p, 0, :], start=True, stop=True)
                        last.then_inc(sc_r, 1)
                    if p:
                        pp = p - 1
                        pe.wait_ge(ex_r, b * 8 + pp + 2)
                        if pp == 0:
                            pe.wait_ge(g_v[0], b * 16 + 16)
                            pe.wait_ge(g_v[1], b * 16 + 16)
                            pe.wait_ge(no_r, b * 2 + 1)
                        for e in range(2):
                            hd = 2 * (pp % 4) + e
                            for tt in range(2):
                                col = (hd * 2 + tt) * VW
                                for st in range(2):
                                    last = M(psO[pp // 4][:, col:col + VW],
                                             E[:, pp % 2, e, st * T + tt * P:st * T + (tt + 1) * P],
                                             vaug[:, st, 2 * pp + e, :], start=(st == 0), stop=(st == 1))
                        last.then_inc(av_r, 1)
                pe.wait_ge(osp_r, b * 2 + 2)
                for half in range(2):
                    transpose_rows(psTh[half], osp[:, half, :, :]).then_inc(ot_r, 1)
                for half in range(2):
                    pe.wait_ge(otc_r, b * 2 + half + 1)
                    split3(psT[half], xT[half], wB, 0, D).then_inc(wo_r, 1)
                for half in range(2):
                    pe.wait_ge(hs_r, b * 2 + half + 1)
                    transpose_rows(psTh[half], hs[half]).then_inc(ht_r, 1)
                for half in range(2):
                    pe.wait_ge(htc_r, b * 2 + half + 1)
                    split3(psT[half], xT[half], wR, 0, NE).then_inc(lgp_r, 1)

            pe.wait_ge(rt_c, 1)
            M(psO[0][:, 0:1], mc.rearrange("p a b -> p (a b)"), onec, start=True, stop=True).then_inc(rt_tot, 1)
            pe.wait_ge(rt_totc, 1)
            M(psO[1][:, 0:P], totb, tpre, start=True, stop=False)
            M(psO[1][:, 0:P], ltri, mc.rearrange("p a b -> p (a b)"), start=False, stop=True)
            M(psT[0][:, 0:NE], totb, tsum, start=True, stop=True).then_inc(rt_pre, 1)
            pe.wait_ge(f_a, 48)
            for part in range(2):
                for m in range(KC):
                    for k in range(KC):
                        for w in range(2):
                            tab = ((0, 1), (1, 2))[part][w]
                            last = M(psS[:, part * KC + m, 0:D], fw[:, w, k, m * P:(m + 1) * P], dft[:, tab, k, :],
                                     start=(k == 0 and w == 0), stop=(k == KC - 1 and w == 1))
            last.then_inc(f_ac, 1)
            pe.wait_ge(rt_oh, 1)
            for k in range(2 * NT):
                last = M(psT[1][:, 0:MT], ohb[:, k, :], oha[:, k, :], start=(k == 0), stop=(k == 2 * NT - 1))
            last.then_inc(rt_inv, 1)
            pe.wait_ge(f_ac, 2)
            for m in range(KC):
                for n in range(KC):
                    for part in range(2):
                        last = M(psS[:, m, 0:D], fa[:, part, n, m * P:(m + 1) * P], dft[:, part, n, :],
                                 start=(n == 0 and part == 0), stop=(n == KC - 1 and part == 1))
            last.then_inc(f_m, 1)

            pe.wait_ge(rt_idx, 1)
            pe.wait_ge(f_ml, 1)
            pe.sem_inc(m_g1, 2)
            pe.sem_inc(m_g2, 2)

            def expert(j):
                return pe.value_load(ej[0:1, bass.ds(j, 1)], min_val=0, max_val=NE - 1)

            def rows_T(j, i, n):
                pe.wait_ge(m_x[i], n * 16 + 16)
                transpose_rows(psTh[i], xs[:, i, :, :]).then_inc(m_T, 1)

            def hidden(j, i):
                e = expert(j)
                pe.wait_ge(m_Tc, j + 1)
                for q in range(2):
                    pe.wait_ge(m_gs, j * 2 + q + 1)
                    for c in range(4 * q, 4 * q + 4):
                        k = 0
                        for kc in range(KC):
                            for wp, xp in ((0, 0), (0, 1), (1, 0)):
                                w = WX[:, bass.ds(e, 1), kc, wp, c * P:(c + 1) * P].rearrange("p a b -> p (a b)")
                                last = M(psS[:, 2 * i + q, (c % 4) * P:(c % 4 + 1) * P], w, exT[:, i, xp, kc, :],
                                         start=(k == 0), stop=(k == 5))
                                k += 1
                    last.then_inc(m_g1, 1)

            def outputs(j, i):
                e = expert(j)
                k = 0
                for c in range(CH):
                    if c % 4 == 0:
                        pe.wait_ge(m_gs, j * 2 + c // 4 + 5)
                    if c == 0:
                        pe.wait_ge(m_y, j + 1)
                    for xp, wp in ((0, 0), (0, 1), (1, 0)):
                        w = WX[:, bass.ds(e, 1), 2 + c // 4, wp, (c % 4) * D:(c % 4 + 1) * D].rearrange("p a b -> p (a b)")
                        last = M(psO[i][:, 0:D], gs[:, i, xp, c, :], w, start=(k == 0), stop=(k == 3 * CH - 1))
                        k += 1
                last.then_inc(m_g2, 1)

            rows_T(0, 0, 0)
            hidden(0, 0)
            rows_T(1, 1, 0)
            with pe.Fori(0, MT // 2 - 1) as jj:
                for i in (1, 0):
                    j = jj * 2 + (1 if i else 2)
                    hidden(j, i)
                    rows_T(j + 1, 1 - i, jj + 1)
                    outputs(j - 1, 1 - i)
            hidden(MT - 2, 1)
            rows_T(MT - 1, 0, MT // 2)
            outputs(MT - 3, 0)
            hidden(MT - 1, 0)
            outputs(MT - 2, 1)
            outputs(MT - 1, 0)

            pe.wait_ge(m_y, MT + 2)
            pe.wait_ge(w1_lo, 2)
            with pe.Fori(0, NB) as b:
                for half in range(2):
                    pe.wait_ge(n_hs, b * 2 + half + 1)
                    transpose_rows(psTh[half], hs1[half]).then_inc(n_hT, 1)
                for half in range(2):
                    pe.wait_ge(n_hTc, b * 2 + half + 1)
                    split3(psS[:, 2 * half, :], xT[half], wA, 0, 2 * D)
                    split3(psS[:, 2 * half + 1, :], xT[half], wA, 2 * D, 3 * D).then_inc(n_qkv, 1)
                for half in range(2):
                    pe.wait_ge(n_spl, b * 2 + half + 1)
                    for pg in range(4):
                        if half or pg >= 2:
                            pe.wait_ge(n_qk, b * 8 + half * 4 + pg - 1)
                        for a in range(2):
                            for qk in range(2):
                                hd = qk * H + 4 * pg + 2 * a
                                last = TR(psTh[pg % 2][:, 2 * a + qk, :],
                                          hl[:, hd:hd + 2, :, :].rearrange("p a b c -> p (a b c)"), identh[:])
                        last.then_inc(n_tr, 1)
                for p in range(9):
                    if p < 8:
                        pe.wait_ge(n_qk, b * 8 + 5 + p // 2)
                        if p >= 2:
                            pe.wait_ge(n_ms, b * 8 + p - 1)
                        else:
                            pe.wait_ge(n_v, b * 2 + 2)
                        for e in range(2):
                            rows = slice(64 * e, 64 * e + 64)
                            ps = psS[:, 2 * (p % 2) + e, :]
                            M(ps[:, 0:T], qkT[rows, p, 1, 0:P], qkT[rows, p, 0, :], start=True, stop=True)
                            last = M(ps[:, T:T + P], qkT[rows, p, 1, P:T], qkT[rows, p, 0, P:T], start=True, stop=True)
                        last.then_inc(n_sc, 1)
                    if p:
                        pp = p - 1
                        pe.wait_ge(n_ms, b * 8 + pp + 1)
                        for e in range(2):
                            hd = 2 * (pp % 4) + e
                            for tt in range(2):
                                col = (hd * 2 + tt) * VW
                                blocks = ((0, 0),) if tt == 0 else ((1, 0), (2, 1))
                                for n, (bl, st) in enumerate(blocks):
                                    last = M(psO[pp // 4][:, col:col + VW], E[:, pp % 2, e, bl * P:(bl + 1) * P],
                                             vaug[:, st, 2 * pp + e, :], start=(n == 0), stop=(n == len(blocks) - 1))
                        last.then_inc(n_av, 1)
                pe.wait_ge(n_osp, b * 2 + 2)
                for half in range(2):
                    transpose_rows(psTh[half], osp[:, half, :, :]).then_inc(n_oT, 1)
                for half in range(2):
                    pe.wait_ge(n_oTc, b * 2 + half + 1)
                    split3(psT[half], xT[half], wB, 0, D).then_inc(n_wo, 1)
                for half in range(2):
                    pe.wait_ge(n_hs2, b * 2 + half + 1)
                    transpose_rows(psTh[half], hs1[half]).then_inc(n_gT, 1)
                for half in range(2):
                    pe.wait_ge(n_gTc, b * 2 + half + 1)
                    split3(psT[half], xT[half], wM, 0, D).then_inc(n_ff, 1)


_HOST = ["x", "L0_tok_weights", "L0_attn_Wqkv", "L0_attn_Wo", "L0_attn_bo", "L0_ffn_w_router", "L0_ffn_w1", "L0_ffn_b1",
         "L0_ffn_w2", "L0_ffn_b2", "L1_attn_w_qkv", "L1_attn_b_qkv", "L1_attn_w_out", "L1_attn_b_out",
         "L1_ffn_w_freq_real", "L1_ffn_w_freq_imag", "L1_ffn_bias"]


def constants():
    import numpy as np
    f = np.float32
    pos = np.arange(T, dtype=f)
    inv = (1.0 / np.power(f(10000.0), np.arange(HD // 2, dtype=f) / f(HD // 2))).astype(f)
    ang = pos[:, None] * inv[None, :]
    cos = np.concatenate([np.cos(ang), np.cos(ang)], 1)
    sin = np.concatenate([-np.sin(ang), np.sin(ang)], 1)
    rope = np.stack([cos, sin], 1).reshape(2, P, 2, HD).transpose(1, 0, 2, 3)
    te = np.arange(P)
    tile, ex = te // NE, te % NE
    lt = (te[:, None] < te[None, :])
    k = np.arange(D)
    ang2 = 2.0 * np.pi * ((k[:, None] * k[None, :]) % D) / D
    dft = np.stack([np.cos(ang2), np.sin(ang2), -np.cos(ang2)]).reshape(3, KC, P, D).transpose(2, 0, 1, 3)
    iota = np.concatenate([np.tile(np.arange(P), (P, 1)), np.tile(np.arange(MT), (P, 1)), np.tile(np.arange(NE), (P, 1)),
                           np.arange(NT)[None, :] * P + te[:, None]], 1)
    c = {
        "c_ident": np.eye(NB, dtype=f), "c_identh": np.eye(P, dtype=np.float16), "c_rope": rope,
        "c_j": np.tile(np.arange(T), (NB, 1)),
        "c_ltri": lt, "c_tpre": (ex[:, None] == ex[None, :]) & (tile[:, None] < tile[None, :]),
        "c_tsum": ex[:, None] == np.arange(NE)[None, :],
        "c_causal": te[:, None] <= te[None, :], "c_dft": dft, "c_iota": iota,
    }
    return {n: np.ascontiguousarray(a if a.dtype == np.float16 else a.astype(f)) for n, a in c.items()}


def kernel(**inputs):
    import numpy as _np
    import concourse.bacc as _bacc
    from concourse.bass_utils import run_bass_kernel_spmd as _run

    nc = _bacc.Bacc("TRN2", target_bir_lowering=False, num_devices=1)
    arrays, args = {}, []
    given = {n: _np.asarray(inputs[n]) for n in _HOST}
    given["L0_ffn_b1"] = given["L0_ffn_b1"].reshape(NE, CH, P).transpose(2, 0, 1)
    given["L1_attn_w_qkv"] = given["L1_attn_w_qkv"].T
    given["L1_attn_w_out"] = given["L1_attn_w_out"].T
    given.update(constants())
    for name, a in given.items():
        a = _np.ascontiguousarray(a)
        arrays["in_" + name] = a
        args.append(nc.dram_tensor("in_" + name, a.shape, mybir.dt.from_np(a.dtype), kind="ExternalInput").ap())
    out = nc.dram_tensor("out_0", (NB, T, D), fp32, kind="ExternalOutput").ap()
    lm_tower(nc, *args, out)
    r = _run(nc, [arrays], core_ids=[0])
    return r.results[0]["out_0"]
```

```python
import concourse.bass as bass
from concourse import mybir
from contextlib import ExitStack

fp32 = mybir.dt.float32
fp16 = mybir.dt.float16
i32 = mybir.dt.int32
u32 = mybir.dt.uint32
ALU = mybir.AluOpType
ACT = mybir.ActivationFunctionType
AX = mybir.AxisListType

P = 128
NB, T, D = 8, 256, 256
NT = NB * T // P
H, HD = 16, 16
NE, HID, TOPK = 8, 1024, 2
VW = HD + 1
TAB = 3
MT = (TOPK * NB * T + NE * (P - 1)) // P
CH = HID // P
WS = 64.0
EPS_LN, EPS_QK, EPS_L1 = 1e-5, 1e-6, 1e-6
KC = D // P


def wait(eng, sem, value):
    if isinstance(value, int) and value <= 0:
        return
    eng.wait_ge(sem, value)


def lm_tower(nc, x, table, wqkv0, wo0, bo0, wr, w1, b1, w2, b2, wqkv1, bqkv1, wout1, bout1,
             fre, fim, fbias, c_ident, c_identh, c_rope, c_j, c_ltri, c_tpre, c_tsum, c_causal,
             c_dft, c_iota, out):
    ctx = ExitStack()
    with ctx:
        def sb(name, shape, dt):
            return ctx.enter_context(nc.sbuf_tensor(name, shape, dt))

        def sem(name):
            return ctx.enter_context(nc.semaphore(name))

        tab_qk = nc.dram_tensor("tab_qk", (TAB * P, 2 * D), fp32).ap()
        tab_v = [nc.dram_tensor(f"tab_v{i}", (TAB * P, H * VW // 2), fp32).ap() for i in range(2)]
        xn_d = nc.dram_tensor("xn_d", (NT * P, 2 * D), fp16).ap()
        y_d = nc.dram_tensor("y_d", (MT * P, D), fp32).ap()

        WX = sb("expert_weights", [P, NE, 4, 2, 1024], fp16)
        h = sb("h", [P, NT, D], fp32)
        wA = sb("w_qkv_split", [P, KC, 2, 3 * D], fp16)
        wB = sb("w_o_split", [P, KC, 2, D], fp16)
        wM = sb("w_fft_split", [P, KC, 2, D], fp16)
        wR = sb("w_router_split", [P, KC, 2, NE], fp16)
        ident = sb("ident", [P, P], fp32)
        identh = sb("identh", [P, P], fp16)
        rope = sb("rope", [P, 2, 2, HD], fp32)
        pos_i = sb("pos_i", [P, NT + 4], i32)
        posx = sb("posx", [P, 3, 2, 1], i32)
        bias_bc = sb("bias_bc", [P, 5 * D], fp32)
        stage = sb("stage", [P, 2, 1024], fp32)
        lgt = sb("lgt", [P, NT, NE], fp32)
        mxt = sb("mxt", [P, NT, 2], fp32)
        ixt = sb("ixt", [P, NT, 2], fp32)
        gate = sb("gate", [P, NT, 2], fp32)
        slot_i = sb("slot_i", [P, NT + 2, 2], i32)
        inv_i = sb("inv_i", [P, MT], i32)
        ej = sb("ej", [1, MT], i32)
        posy = sb("posy", [P, 2, 2, 1], i32)
        b1s = sb("b1s", [P, NE, CH], fp32)
        small = sb("small", [P, 64], fp32)
        mexp = sb("minus_half", [P, 32], fp32)
        epsc = sb("epsc", [P, 1], fp32)
        lg = sb("lg", [P, 2, NE], fp32)
        mx8 = sb("mx8", [P, 2, 8], fp32)
        ix8 = sb("ix8", [P, 2, 8], u32)
        AW = 9536
        arena = sb("arena", [P, AW], fp32)

        def view(at, shape, dt=fp32, memory=None):
            n = 1
            for s in shape:
                n *= s
            words = n if dt in (fp32, i32, u32) else n // 2
            a = (arena[:] if memory is None else memory)[:, at:at + words]
            if dt != fp32:
                a = a.bitcast(dt)
            names = " ".join("abcdef"[i] for i in range(len(shape)))
            if len(shape) > 1:
                a = a.rearrange(f"p ({names}) -> p {names}", **{"abcdef"[i]: shape[i] for i in range(1, len(shape))})
            return a, at + words

        at = 0
        qkg, at = view(at, [2, 4, 2 * 4, HD])
        rp, at = view(at, [2, 2, 8, HD])
        rp2, at = view(at, [2, 8, HD])
        hl, at = view(at, [2, 2, 2, 4, 4, HD], fp16)
        qkT, at = view(at, [8, 2, T], fp16)
        vaug, at = view(at, [2, 2, H // 2, VW])
        E, at = view(at, [2, 2, 2 * T])
        o, at = view(at, [2, P])
        hnx, at = view(at, [D])
        osp, at = view(at, [2, 2, D], fp16)
        oTs, at = view(at, [2 * T])
        hn2 = arena[:, at - 4 * D - 2 * D:at - 4 * D].rearrange("p (a b) -> p a b", a=2)
        assert at <= AW, at
        xTa = bias_bc[:, 3 * D:5 * D].bitcast(fp16).rearrange("p (a b c d) -> p a b c d", a=2, b=2, c=KC)
        hsa = wM.rearrange("p a b c -> p a b c")
        big = WX[:].rearrange("p a b c d -> p (a b c d)").bitcast(fp32)

        def late(at, shape, dt=fp32):
            return view(at, shape, dt, big)

        at = 0
        lx, at = late(at, [2, 2 * D])
        lmn, at = late(at, [2, 2 * D])
        lr, at = late(at, [2, 2, H, HD])
        lhl, at = late(at, [2, 2, 2, 4, 4, HD], fp16)
        lqkT, at = late(at, [8, 2, T], fp16)
        lv, at = late(at, [NB, 2, 2 * (H // 2) * HD])
        lvaug, at = late(at, [2, 2, H // 2, VW])
        lE, at = late(at, [2, 2, 3, P])
        lo, at = late(at, [2, P])
        lhn, at = late(at, [2, D])
        losp, at = late(at, [2, 2, D], fp16)
        loTs, at = late(at, [2 * T])
        lhs, at = late(at, [2, 2, D], fp16)
        lps, at = late(at, [2, 2, D], fp16)
        lxT, at = late(at, [2, 2, KC, P], fp16)
        lyT, at = late(at, [2, 2, KC, P], fp16)
        mask3, at = late(at, [3, P])
        at = 0
        wst, at = view(at, [KC, 3 * D])
        tb, at = view(at, [TAB, D])
        u, at = view(at, [2 * D])
        usq, at = view(at, [2 * D])
        txT, at = view(at, [2, KC, P], fp16)
        ths, at = view(at, [2, D], fp16)
        tv, at = view(at, [H, VW])
        tokx_i, at = view(at, [T], i32)
        tokf, at = view(at, [T])
        jrow, at = view(at, [T])
        tm, at = view(at, [T])
        tsp, at = view(at, [T])
        tls, at = view(at, [T])
        tva, at = view(at, [T])
        thn, at = view(at, [D])
        wst2, at = view(at, [KC, D])
        wst3, at = view(at, [KC, NE])
        at = 0
        ltri, at = view(at, [P])
        tpre, at = view(at, [P])
        tsum, at = view(at, [NE])
        iota, at = view(at, [P + MT + NE + NT])
        iob, ioa, ioe, tokid = iota[:, 0:P], iota[:, P:P + MT], iota[:, P + MT:P + MT + NE], iota[:, P + MT + NE:]
        m0, at = view(at, [NT, NE])
        m1, at = view(at, [NT, NE])
        mc, at = view(at, [NT, NE])
        totb, at = view(at, [P])
        ohb, at = view(at, [2 * NT, P], fp16)
        oha, at = view(at, [2 * NT, MT], fp16)
        ra, at = view(at, [2 * NT])
        rb, at = view(at, [2 * NT])
        ri, at = view(at, [2 * NT], i32)
        ri2, at = view(at, [2 * NT], i32)
        ecmp, at = view(at, [MT, NE])
        e8, at = view(at, [8, NE])
        e8i, at = view(at, [NE], i32)
        pe8, at = view(at, [NT, NE])
        p1, at = view(at, [NT, NE])
        sf, at = view(at, [NT, 2])
        rq, at = view(at, [4 * NT])
        rqm, rqs, rqr = rq[:, 0:NT], rq[:, NT:2 * NT], rq[:, 2 * NT:3 * NT]
        onec, at = view(at, [1])
        rq_e, at = view(at, [MT])
        dft, at = view(at, [3, KC, D])
        fw, at = view(at, [2, KC, D])
        fa, at = view(at, [2, KC, D])
        assert at <= AW, at
        at = 0
        xs, at = view(at, [2, 2, D], fp16)
        exT, at = view(at, [2, 2, KC, P], fp16)
        g, at = view(at, [2, CH, P])
        gs, at = view(at, [2, 2, CH, P], fp16)
        y, at = view(at, [2, D])
        b2bc, at = view(at, [NE, D])
        mixr, at = view(at, [2, 1], i32)
        wst1, at = view(at, [KC, 3 * D])
        assert at <= AW, at
        wst1o = stage[:, 0, 0:KC * D].rearrange("p (a b) -> p a b", a=KC)
        sflat = stage[:].rearrange("p a b -> p (a b)")
        yg = sflat[:, 0:4 * D].rearrange("p (a b c) -> p a b c", a=2, b=2)

        psT = [ctx.enter_context(nc.psum_tensor(f"psT{i}", [P, 512], fp32)) for i in range(2)]
        psS = ctx.enter_context(nc.psum_tensor("psS", [P, 4, 512], fp32))
        psO = [ctx.enter_context(nc.psum_tensor(f"psO{i}", [P, 512], fp32)) for i in range(2)]
        psW = psT[1][:]
        psWh = psW.bitcast(fp16).rearrange("p (a b c) -> p a b c", a=2, b=4)
        psTb = psT[0][:].bitcast(fp16).rearrange("p (a b c) -> p a b c", a=2, b=4)
        psTf = psT[0][:].bitcast(fp16).rearrange("p (s q t) -> p s q t", s=2, q=4)
        psTh = [t[:, 0:256].bitcast(fp16).rearrange("p (a b) -> p a b", a=4) for t in psT]


        ld_x, ld_ident, ld_small = sem("ld_x"), sem("ld_ident"), sem("ld_small")
        ld_w = sem("ld_w")
        ld_tab = sem("ld_tab")
        w_hi, w_lo = sem("w_hi"), sem("w_lo")
        pos_r, posT_r, posi_r = sem("pos_r"), sem("posT_r"), sem("posi_r")
        mexp_r, ones_r = sem("mexp_r"), sem("ones_r")
        t_var, t_pow, t_split, t_T, t_xT, t_mm = (sem(n) for n in ("t_var", "t_pow", "t_split", "t_T", "t_xT", "t_mm"))
        t_u, t_sum, t_rn, t_out, t_v, t_wr = (sem(n) for n in ("t_u", "t_sum", "t_rn", "t_out", "t_v", "t_wr"))
        g_qk = sem("g_qk")
        g_h = sem("g_h")
        g_v = [sem("g_v0"), sem("g_v1")]
        pos_x = sem("pos_x")
        rope_r, split_r = sem("rope_r"), sem("split_r")
        tr_r, qk_r = sem("tr_r"), sem("qk_r")
        oc_r, oT_r, ob_r = sem("oc_r"), sem("oT_r"), sem("ob_r")
        sc_r, ex_r, av_r = sem("sc_r"), sem("ex_r"), sem("av_r")
        no_r, osp_r = sem("no_r"), sem("osp_r")
        ot_r, otc_r, wo_r = sem("ot_r"), sem("otc_r"), sem("wo_r")
        var_r, pw_r, hs_r = sem("var_r"), sem("pw_r"), sem("hs_r")
        xn_w = sem("xn_w")
        ht_r, htc_r, lgp_r, lgs_r = sem("ht_r"), sem("htc_r"), sem("lgp_r"), sem("lgs_r")
        h_r = sem("h_r")
        st_ld = [sem("st_ld0"), sem("st_ld1")]
        st_hi, st_free = sem("st_hi"), sem("st_free")
        dch, ach, pch = sem("dch"), sem("ach"), sem("pch")
        rt_a = sem("rt_a")
        w1_hi, w1_lo, w1_ld, l1_ld = sem("w1_hi"), sem("w1_lo"), sem("w1_ld"), sem("l1_ld")
        f_a, f_ac, f_m, f_mh, f_ml = (sem(n) for n in ("f_a", "f_ac", "f_m", "f_mh", "f_ml"))
        n_y = sem("n_y")
        n_var, n_pow = sem("n_var"), sem("n_pow")
        n_hs, n_hT, n_hTc = sem("n_hs"), sem("n_hT"), sem("n_hTc")
        n_qkv, n_x = sem("n_qkv"), sem("n_x")
        n_min, n_exp, n_hl, n_spl = sem("n_min"), sem("n_exp"), sem("n_hl"), sem("n_spl")
        n_tr, n_qk = sem("n_tr"), sem("n_qk")
        n_sc, n_av = sem("n_sc"), sem("n_av")
        n_ms, n_mid, n_pm = sem("n_ms"), sem("n_mid"), sem("n_pm")
        n_vc, n_oc, n_oT, n_osp = sem("n_vc"), sem("n_oc"), sem("n_oT"), sem("n_osp")
        n_lT, n_lTc, n_wo = sem("n_lT"), sem("n_lTc"), sem("n_wo")
        n_var2, n_pow2, n_hs2, n_gT, n_gTc = sem("n_var2"), sem("n_pow2"), sem("n_hs2"), sem("n_gT"), sem("n_gTc")
        n_ff, n_out, n_hb, n_fb = sem("n_ff"), sem("n_out"), sem("n_hb"), sem("n_fb")
        rt_ld, rt_d, rt_e, rt_c, rt_tot, rt_totc, rt_pre, rt_oh, rt_inv, rt_idx = (
            sem(n) for n in ("rt_ld", "rt_d", "rt_e", "rt_c", "rt_tot", "rt_totc", "rt_pre", "rt_oh", "rt_inv", "rt_idx"))
        m_w = [sem("m_w0"), sem("m_w1")]
        m_x = [sem("m_x0"), sem("m_x1")]
        m_T, m_Tc, m_g1, m_act, m_gs, m_g2, m_y = (sem(n) for n in ("m_T", "m_Tc", "m_g1", "m_act", "m_gs", "m_g2", "m_y"))
        m_b2, m_hi = sem("m_b2"), sem("m_hi")
        m_yw = [sem("m_yw0"), sem("m_yw1")]
        out_w = sem("out_w")
        mv_t = small[:, 0:6].rearrange("p (a b) -> p a b", b=2)
        st_t = small[:, 8:26].rearrange("p (a b) -> p a b", b=6)
        bst = [small[:, 8:14], small[:, 14:20]]
        mvq = small[:, 20:24].rearrange("p (a b) -> p a b", b=2)
        mvp = small[:, 0:4].rearrange("p (a b) -> p a b", b=2)
        rden2 = small[:, 32:48].rearrange("p (a b) -> p a b", a=2)
        block = ctx.enter_context(nc.Block())

        def split3(ps, xhl, w, n0, n1, out0=0):
            k, last = 0, 3 * KC - 1
            for c in range(KC):
                for a, b in ((0, 0), (0, 1), (1, 0)):
                    m = nc.tensor.matmul(ps[:, out0:out0 + n1 - n0], xhl[:, a, c, :], w[:, c, b, n0:n1],
                                         start=(k == 0), stop=(k == last))
                    k += 1
            return m


        def table_view(a):
            return a.rearrange("(t p) n -> p t n", p=P)

        w1_v = w1.rearrange("e (c p) n -> p e c n", p=P)
        w2_v = w2.rearrange("e (g c p) n -> p e g c n", p=P, g=2)

        @block.sync
        def _(sp):
            sp.dma_start(tokx_i[0:NB, :], x).then_inc(ld_x, 16)
            sp.dma_start(jrow[0:NB, :], c_j).then_inc(ld_x, 16)
            sp.dma_start(tb, table_view(table[0:TAB * P, :])).then_inc(ld_tab, 16)
            sp.dma_start(ident[:], c_ident).then_inc(ld_ident, 16)
            sp.dma_start(identh[:], c_identh).then_inc(ld_ident, 16)
            sp.dma_start(wst, wqkv0.rearrange("(c p) n -> p c n", p=P)).then_inc(ld_w, 16)
            sp.dma_start(wst2, wo0.rearrange("(c p) n -> p c n", p=P)).then_inc(ld_w, 16)
            sp.dma_start(wst3, wr.rearrange("(c p) n -> p c n", p=P)).then_inc(ld_w, 16)
            sp.dma_start(rope[:], c_rope).then_inc(ld_small, 16)
            sp.dma_start(bias_bc[:, 0:D], bo0.partition_broadcast(P)).then_inc(ld_small, 16)
            sp.dma_start(b1s[:], b1).then_inc(ld_small, 16)
            for t in range(TAB):
                sp.wait_ge(t_out, t + 1)
                sp.dma_start(tab_qk[t * P:(t + 1) * P, :], u).then_inc(t_wr, 16)
                sp.wait_ge(t_v, t + 1)
                sp.wait_ge(ones_r, 1)
                for i in range(2):
                    sp.dma_start(tab_v[i][t * P:(t + 1) * P, :], tv[:, i * H // 2:(i + 1) * H // 2, :].rearrange("p a b -> p (a b)")
                                 ).then_inc(t_wr, 16)
            def rows_out(b):
                sp.wait_ge(hs_r, b + 1)
                sp.dma_start(table_view(xn_d)[:, bass.ds(b * 2, 2), :], hsa.rearrange("p a b c -> p a (b c)")).then_inc(xn_w, 16)

            def expert_in(b):
                for q in range(4):
                    sp.wait_ge(st_free, b * 4 + q + 1)
                    if q < 2:
                        sp.dma_start(stage[:, q % 2, :], w1_v[:, bass.ds(b, 1), q, :].rearrange("p e n -> p (e n)")
                                     ).then_inc(st_ld[q % 2], 16)
                    else:
                        sp.dma_start(stage[:, q % 2, :].rearrange("p (c n) -> p c n", c=4),
                                     w2_v[:, bass.ds(b, 1), q - 2, :, :].rearrange("p e c n -> p (e c) n")
                                     ).then_inc(st_ld[q % 2], 16)

            expert_in(0)
            with sp.Fori(0, NB - 1) as bb:
                expert_in(bb + 1)
                rows_out(bb)
            rows_out(NB - 1)
            sp.wait_ge(xn_w, 16 * NB)
            sp.wait_ge(lgs_r, NB)
            sp.wait_ge(g_qk, 32 * (NB + 2))
            sp.wait_ge(g_v[0], 32 * (NB + 1))
            sp.wait_ge(ex_r, 8 * NB + 1)
            sp.wait_ge(qk_r, 4 * (NB + 1) - 1)
            sp.wait_ge(tr_r, 4 * (NB + 1))
            for dst, src in ((ltri, c_ltri), (tpre, c_tpre), (tsum, c_tsum), (iota, c_iota)):
                sp.dma_start(dst, src).then_inc(rt_ld, 16)
            sp.dma_start(dft, c_dft).then_inc(f_a, 16)
            sp.dma_start(fw[:, 0, :, :], fre.rearrange("(c p) n -> p c n", p=P)).then_inc(f_a, 16)
            sp.dma_start(fw[:, 1, :, :], fim.rearrange("(c p) n -> p c n", p=P)).then_inc(f_a, 16)
            sp.dma_start(wst1o, wout1.rearrange("(c p) n -> p c n", p=P)).then_inc(w1_ld, 16)
            sp.dma_start(bias_bc[:, 0:3 * D], bqkv1.partition_broadcast(P)).then_inc(l1_ld, 16)
            sp.dma_start(bias_bc[:, 3 * D:4 * D], bout1.partition_broadcast(P)).then_inc(l1_ld, 16)
            sp.dma_start(bias_bc[:, 4 * D:5 * D], fbias.partition_broadcast(P)).then_inc(l1_ld, 16)
            sp.wait_ge(rt_idx, 1)
            sp.wait_ge(f_ml, 1)
            sp.dma_start(b2bc.rearrange("p a b -> p (a b)"), b2.rearrange("a b -> (a b)").partition_broadcast(P)).then_inc(m_b2, 16)
            sp.dma_start(wst1, wqkv1.rearrange("(c p) n -> p c n", p=P)).then_inc(w1_ld, 16)

            def y_out(j, i):
                sp.wait_ge(m_y, j + 3)
                sp.dma_start(table_view(y_d)[:, bass.ds(j, 1), :].rearrange("p t n -> p (t n)"), y[:, i, :]).then_inc(m_yw[i], 16)

            with sp.Fori(0, MT // 2) as jj:
                for i in range(2):
                    y_out(jj * 2 + i, i)
            y_out(MT - 1, 0)
            sp.wait_ge(m_y, MT + 2)
            for k in (0, 2):
                sp.dma_start(mask3[:, k, :], c_causal).then_inc(l1_ld, 16)
            with sp.Fori(0, NB) as b:
                sp.wait_ge(n_out, b + 1)
                sp.dma_start(out.rearrange("b (s p) d -> p (b s) d", p=P)[:, bass.ds(b * 2, 2), :],
                             h[:, bass.ds(b * 2, 2), :]).then_inc(out_w, 16)
            sp.wait_ge(out_w, 16 * NB)

        @block.gpsimd
        def _(pool):
            done = [0]

            def link(ins):
                ins.then_inc(pch, 1)
                done[0] = done[0] + 1
                pool.wait_ge(pch, done[0])

            nc.gpsimd.memset(tv[:, :, HD:VW], 1.0).then_inc(ones_r, 1)
            nc.gpsimd.memset(epsc[:], EPS_LN)
            nc.gpsimd.memset(mexp[:], -0.5).then_inc(mexp_r, 1)
            pool.wait_ge(mexp_r, 1)
            pool.wait_ge(t_var, 1)
            link(nc.gpsimd.tensor_scalar(small[:, 26:26 + TAB], mv_t[:, :, 1], EPS_LN, None, ALU.add))
            nc.gpsimd.tensor_tensor(small[:, 26:26 + TAB], small[:, 26:26 + TAB], mexp[:, 0:TAB], ALU.pow).then_inc(t_pow, 1)
            pool.wait_ge(posi_r, 2)

            def embeddings(t0, t1):
                for t in range(t0, t1):
                    nc.gpsimd.indirect_dma_start(h[:, t, :], None, table, bass.IndirectOffsetOnAxis(
                        ap=pos_i[:, t:t + 1], axis=0)).then_inc(g_h, 16)

            embeddings(0, 4)
            for t in range(TAB):
                pool.wait_ge(t_sum, t + 1)
                link(nc.gpsimd.tensor_scalar(small[:, 32:64], small[:, 32:64], EPS_QK, None, ALU.add))
                nc.gpsimd.tensor_tensor(small[:, 32:64], small[:, 32:64], mexp[:], ALU.pow).then_inc(t_rn, 1)
                embeddings(4 + 4 * t, 8 + 4 * t)

            def gather_qk(b):
                link(nc.gpsimd.tensor_copy(posx[:, 0, :, 0], pos_i[:, bass.ds(b * 2, 2)]))
                for half in range(2):
                    nc.gpsimd.indirect_dma_start(qkg[:, half].rearrange("p a b c -> p (a b c)"), None, tab_qk,
                                                 bass.IndirectOffsetOnAxis(ap=posx[:, 0, half, :], axis=0)).then_inc(g_qk, 16)

            def gather_v(b, gp):
                link(nc.gpsimd.tensor_copy(posx[:, 1 + gp, :, 0], pos_i[:, bass.ds(b * 2, 2)]))
                for half in range(2):
                    nc.gpsimd.indirect_dma_start(vaug[:, gp, half].rearrange("p a b -> p (a b)"), None, tab_v[gp],
                                                 bass.IndirectOffsetOnAxis(ap=posx[:, 1 + gp, half, :], axis=0)
                                                 ).then_inc(g_v[gp], 16)

            def turn(b, pg):
                x, y = qkg[:, :, pg], rp[:, pg % 2]
                cs = rope[:, :, 0:1, :].to_broadcast([P, 2, 8, HD])
                sn = rope[:, :, 1:2, :].to_broadcast([P, 2, 8, HD])
                if pg == 0:
                    pool.wait_ge(g_qk, b * 32 + 32)
                wait(pool, split_r, b * 4 + pg - 1)
                nc.gpsimd.tensor_tensor(y, x, cs, ALU.mult)
                nc.gpsimd.tensor_tensor(rp2[:, :, :, 0:8], x[:, :, :, 8:16], sn[:, :, :, 0:8], ALU.mult)
                link(nc.gpsimd.tensor_tensor(rp2[:, :, :, 8:16], x[:, :, :, 0:8], sn[:, :, :, 8:16], ALU.mult))
                link2(nc.gpsimd.tensor_tensor(y, y, rp2, ALU.add), b * 4 + pg + 1)

            def link2(ins, count):
                ins.then_inc(rope_r, 1)
                pool.wait_ge(rope_r, count)

            def root(b):
                pool.wait_ge(var_r, b + 1)
                link(nc.gpsimd.tensor_tensor(small[:, 4:6], mvp[:, :, 1], epsc[:].to_broadcast([P, 2]), ALU.add))
                nc.gpsimd.tensor_tensor(small[:, 4:6], small[:, 4:6], mexp[:, 0:2], ALU.pow).then_inc(pw_r, 1)

            def pool_body(b, first=False):
                wait(pool, av_r, b * 8)
                gather_v(b, 1)
                turn(b + 1, 0)
                turn(b + 1, 1)
                hb = h[:, bass.ds(b * 2, 2), :]
                nc.gpsimd.tensor_tensor(hb, hb, bias_bc[:, 0:D].unsqueeze(1).to_broadcast([P, 2, D]), ALU.add).then_inc(ob_r, 1)
                turn(b + 1, 2)
                if not first:
                    root(b - 1)
                turn(b + 1, 3)
                gather_qk(b + 2)
                pool.wait_ge(av_r, b * 8 + 4)
                gather_v(b + 1, 0)

            pool.wait_ge(t_wr, 48 * TAB)
            pool.wait_ge(ld_small, 48)
            gather_qk(0)
            gather_v(0, 0)
            for pg in range(4):
                turn(0, pg)
            gather_qk(1)
            pool.wait_ge(g_h, 16 * NT)
            pool_body(0, True)
            with pool.Fori(0, NB - 1) as bb:
                pool.sem_clear(pch)
                done[0] = 0
                pool_body(bb + 1)
            pool.sem_clear(pch)
            done[0] = 0
            root(NB - 1)

            pool.wait_ge(rt_idx, 1)
            pool.wait_ge(f_ml, 1)
            pool.wait_ge(xn_w, 16 * NB)
            pool.sem_inc(m_T, 2)

            def token_rows(j, i):
                pool.wait_ge(m_T, j + 1)
                link(nc.gpsimd.tensor_copy(mixr[:, i, :], inv_i[:, bass.ds(j, 1)]))
                nc.gpsimd.indirect_dma_start(xs[:, i, :, :].rearrange("p a b -> p (a b)"), None, xn_d,
                                             bass.IndirectOffsetOnAxis(ap=mixr[:, i, :], axis=0)).then_inc(m_x[i], 16)

            with pool.Fori(0, MT // 2) as jj:
                pool.sem_clear(pch)
                done[0] = 0
                for i in range(2):
                    token_rows(jj * 2 + i, i)
            token_rows(MT - 1, 0)

            def slot_rows(b, halves=(0, 1)):
                if 0 in halves:
                    link(nc.gpsimd.tensor_copy(posy[:, :, :, 0], slot_i[:, bass.ds(b * 2, 2), :]))
                for half in halves:
                    for k in range(2):
                        nc.gpsimd.indirect_dma_start(yg[:, k, half, :], None, y_d, bass.IndirectOffsetOnAxis(
                            ap=posy[:, half, k, :], axis=0)).then_inc(n_y, 16)

            def inverse_root(b, stats, root, ready, done_sem):
                pool.wait_ge(ready, b + 1)
                link(nc.gpsimd.tensor_tensor(root, stats[:, :, 1], epsc[:].to_broadcast([P, 2]), ALU.add))
                nc.gpsimd.tensor_tensor(root, root, mexp[:, 0:2], ALU.pow).then_inc(done_sem, 1)

            def add_bias(b, bias, ready, done_sem):
                pool.wait_ge(ready, b + 1)
                hb = h[:, bass.ds(b * 2, 2), :]
                nc.gpsimd.tensor_tensor(hb, hb, bias.unsqueeze(1).to_broadcast([P, 2, D]), ALU.add).then_inc(done_sem, 1)

            def mask_second(b, p):
                pool.wait_ge(n_mid, b * 8 + p + 1)
                e = lE[:, p % 2, 1, 0:3:2, :]
                nc.gpsimd.tensor_tensor(e, e, mask3[:, 0:3:2, :], ALU.mult).then_inc(n_pm, 1)

            def next_rows(b):
                inverse_root(b, mvp, small[:, 4:6], n_var, n_pow)

            def pool_late(b, tail=True, group=True, prep=True, ahead=True, ahead2=True):
                mask_second(b, 1)
                if prep:
                    add_bias(b + 2, bias_bc[:, 3 * D:4 * D], n_hs, n_hb)
                mask_second(b, 2)
                mask_second(b, 3)
                if ahead:
                    next_rows(b + 3)
                if ahead2:
                    slot_rows(b + 4, (0,))
                mask_second(b, 4)
                if tail:
                    inverse_root(b - 1, mvq, small[:, 24:26], n_var2, n_pow2)
                mask_second(b, 5)
                if ahead2:
                    slot_rows(b + 4, (1,))
                mask_second(b, 6)
                if tail:
                    add_bias(b - 1, bias_bc[:, 4 * D:5 * D], n_hs2, n_fb)
                mask_second(b, 7)
                if group:
                    mask_second(b + 1, 0)

            pool.wait_ge(m_yw[0], 16 * ((MT + 1) // 2) + 16)
            pool.wait_ge(m_yw[1], 16 * (MT // 2) + 16)
            pool.wait_ge(l1_ld, 80)
            for c in range(3):
                slot_rows(c)
                next_rows(c)
                if c < 2:
                    add_bias(c, bias_bc[:, 3 * D:4 * D], n_hs, n_hb)
            slot_rows(3)
            mask_second(0, 0)
            pool_late(0, tail=False)
            with pool.Fori(0, NB - 5) as bb:
                pool.sem_clear(pch)
                done[0] = 0
                pool_late(bb + 1)
            pool_late(NB - 4, ahead2=False)
            pool_late(NB - 3, ahead=False, ahead2=False)
            pool_late(NB - 2, prep=False, ahead=False, ahead2=False)
            pool_late(NB - 1, group=False, prep=False, ahead=False, ahead2=False)
            inverse_root(NB - 1, mvq, small[:, 24:26], n_var2, n_pow2)
            add_bias(NB - 1, bias_bc[:, 4 * D:5 * D], n_hs2, n_fb)

        @block.scalar
        def _(act):
            act.wait_ge(ld_w, 48)
            nc.scalar.activation(wA[:, :, 0, :], wst, ACT.Copy, scale=WS).then_inc(w_hi, 1)
            nc.scalar.activation(wB[:, :, 0, :], wst2, ACT.Copy, scale=WS).then_inc(w_hi, 1)
            nc.scalar.activation(wR[:, :, 0, :], wst3, ACT.Copy, scale=WS).then_inc(w_hi, 1)
            for t in range(TAB):
                act.wait_ge(t_mm, t + 1)
                wait(act, t_wr, 48 * t)
                nc.scalar.activation(u.rearrange("p (g a n) -> p a g n", g=4, a=2),
                                     psS[:, 0, :].rearrange("p (a g n) -> p a g n", a=2, g=4),
                                     ACT.Copy, scale=1.0 / WS).then_inc(t_u, 1)
                nc.scalar.activation(tv[:, :, 0:HD], psS[:, 1, 0:D].rearrange("p (a b) -> p a b", b=HD),
                                     ACT.Copy, scale=1.0 / WS).then_inc(t_v, 1)
            act.wait_ge(t_wr, 48 * TAB)

            def exponentials(b, p):
                act.wait_ge(sc_r, b * 8 + p + 1)
                wait(act, av_r, b * 8 + p - 1)
                nc.scalar.activation(E[:, p % 2, :, :], psS[:, 2 * (p % 2):2 * (p % 2) + 2, :], ACT.Exp,
                                     scale=HD ** -0.5).then_inc(ex_r, 1)

            def rows_from(b, pg):
                act.wait_ge(tr_r, b * 4 + pg + 1)
                qk = qkT[:, 2 * pg:2 * pg + 2].rearrange("p a b t -> p (a b) t")
                nc.scalar.activation(qk.rearrange("p q (s t) -> p s q t", s=2), psTf, ACT.Copy).then_inc(qk_r, 1)

            def sums_out(b, gp):
                act.wait_ge(av_r, b * 8 + 4 * gp + 4)
                wait(act, oT_r, b * 2 + gp)
                nc.scalar.activation(oTs, psO[gp][:], ACT.Copy).then_inc(oc_r, 1)

            def act_body(b, first=False):
                for p in range(8):
                    if p == 0 and not first:
                        sums_out(b - 1, 1)
                    if p < 7:
                        exponentials(b, p + 1)
                    else:
                        exponentials(b + 1, 0)
                    if p == 4:
                        sums_out(b, 0)
                    if p == 0:
                        if not first:
                            rows_from(b, 3)
                    elif p % 2 == 0:
                        rows_from(b + 1, p // 2 - 1)
                    else:
                        q = p // 2
                        act.wait_ge(st_ld[q % 2], b * 32 + 16 * (q // 2) + 16)
                        nc.scalar.activation(WX[:, bass.ds(b, 1), q, 0, :].rearrange("p e n -> p (e n)"),
                                             stage[:, q % 2, :], ACT.Copy, scale=WS).then_inc(st_hi, 1)

            for pg in range(4):
                rows_from(0, pg)
            exponentials(0, 0)
            act_body(0, True)
            with act.Fori(0, NB - 1) as bb:
                act_body(bb + 1)
            sums_out(NB - 1, 1)

            act.wait_ge(rt_d, 1)
            nc.scalar.activation(pe8, pe8, ACT.Exp).then_inc(rt_e, 1)
            nc.scalar.activation(rqm, rqm, ACT.Exp).then_inc(rt_e, 1)
            act.wait_ge(f_m, 1)
            nc.scalar.activation(wM[:, :, 0, :], psS[:, 0:2, 0:D], ACT.Copy, scale=WS / D).then_inc(f_mh, 1)
            act.wait_ge(w1_ld, 32)
            nc.scalar.activation(wB[:, :, 0, :], wst1o, ACT.Copy, scale=WS).then_inc(w1_hi, 1)
            nc.scalar.activation(wA[:, :, 0, :], wst1, ACT.Copy, scale=WS).then_inc(w1_hi, 1)
            act.wait_ge(rt_idx, 1)
            act.wait_ge(f_ml, 1)

            def gelu(j, i):
                e = act.value_load(ej[0:1, bass.ds(j, 1)], min_val=0, max_val=NE - 1)
                for q in range(2):
                    act.wait_ge(m_g1, j * 2 + q + 3)
                    act.wait_ge(m_gs, j * 2 + q + 1)
                    for c in range(4 * q, 4 * q + 4):
                        last = nc.scalar.activation(g[:, i, c, :], psS[:, 2 * i + q, (c % 4) * P:(c % 4 + 1) * P],
                                                    ACT.Gelu_apprx_tanh, bias=b1s[:, bass.ds(e, 1), c], scale=1.0 / WS)
                    last.then_inc(m_act, 1)

            with act.Fori(0, MT // 2) as jj:
                for i in range(2):
                    gelu(jj * 2 + i, i)
            gelu(MT - 1, 0)
            def second_head(b, p):
                act.wait_ge(n_sc, b * 8 + p + 1)
                wait(act, n_av, b * 8 + p - 1)
                nc.scalar.activation(lE[:, p % 2, 1].rearrange("p a b -> p (a b)"), psS[:, 2 * (p % 2) + 1, 0:3 * P], ACT.Copy).then_inc(n_mid, 1)

            def late_exp(b, half):
                act.wait_ge(n_min, b * 2 + half + 1)
                nc.scalar.activation(lmn[:, half], lmn[:, half], ACT.Exp).then_inc(n_exp, 1)

            def late_parts(b, pg):
                z = lhl[:, pg % 2]
                act.wait_ge(n_hl, b * 4 + pg + 1)
                nc.scalar.activation(z[:, :, 0, :, 2:4, :].rearrange("p a c d e -> p a c (d e)"),
                                     z[:, :, 0, :, 0:2, :].rearrange("p a c d e -> p a c (d e)"), ACT.Copy)
                nc.scalar.activation(z[:, :, 1, :, 2, :], z[:, :, 1, :, 1, :], ACT.Copy)
                nc.scalar.activation(z[:, :, 1, :, 3, :], z[:, :, 1, :, 0, :], ACT.Copy).then_inc(n_spl, 1)

            def late_rows_from(b, pg):
                act.wait_ge(n_tr, b * 4 + pg + 1)
                qk = lqkT[:, 2 * pg:2 * pg + 2].rearrange("p a b t -> p (a b) t")
                nc.scalar.activation(qk.rearrange("p q (s t) -> p s q t", s=2), psTf, ACT.Copy).then_inc(n_qk, 1)

            def late_sums_out(b, gp):
                act.wait_ge(n_av, b * 8 + 4 * gp + 4)
                wait(act, n_oT, b * 2 + gp)
                nc.scalar.activation(loTs, psO[gp][:], ACT.Copy).then_inc(n_oc, 1)

            def values_in(b, gp):
                act.wait_ge(n_x, b * 3 + 3)
                wait(act, n_av, b * 8 - 4 + 4 * gp)
                src = lv[:, bass.ds(b, 1), :, gp * P:(gp + 1) * P].rearrange("p a s (h c) -> p (a s) h c", c=HD)
                nc.scalar.activation(lvaug[:, gp, :, :, 0:HD], src, ACT.Copy).then_inc(n_vc, 1)

            def act_late(b, tail=True, group=True, prep=True):
                for p in range(8):
                    if p == 0 and tail:
                        late_sums_out(b - 1, 1)
                    if p < 7:
                        second_head(b, p + 1)
                    elif group:
                        second_head(b + 1, 0)
                    if p == 0:
                        if tail:
                            late_rows_from(b, 3)
                        values_in(b, 1)
                    if p == 4:
                        late_sums_out(b, 0)
                    if group and p % 2 == 0:
                        if p:
                            late_rows_from(b + 1, p // 2 - 1)
                        late_parts(b + 1, p // 2)
                    if prep and p in (3, 5):
                        late_exp(b + 2, (p - 3) // 2)
                    if group and p == 5:
                        values_in(b + 1, 0)

            for half in range(2):
                late_exp(0, half)
            values_in(0, 0)
            for pg in range(4):
                late_parts(0, pg)
                late_rows_from(0, pg)
            for half in range(2):
                late_exp(1, half)
            second_head(0, 0)
            act_late(0, tail=False)
            with act.Fori(0, NB - 3) as bb:
                act_late(bb + 1)
            act_late(NB - 2, prep=False)
            act_late(NB - 1, group=False, prep=False)
            late_sums_out(NB - 1, 1)

        @block.vector
        def _(dve):
            done = [0]

            def link(ins):
                ins.then_inc(dch, 1)
                done[0] = done[0] + 1
                dve.wait_ge(dch, done[0])

            V = nc.vector
            link(V.memset(pos_i[:], 0))
            for i in range(2):
                V.memset(psO[i][:], 0.0)
            dve.wait_ge(ld_x, 32)
            tk, tj = tokf[0:NB, :], jrow[0:NB, :]
            link(V.tensor_copy(tk, tokx_i[0:NB, :]))
            V.tensor_scalar(tm[0:NB, :], tk, 1.0, None, ALU.not_equal)
            link(V.scalar_tensor_tensor(tsp[0:NB, :], tk, 4.0, tj, ALU.is_equal, ALU.mult))
            V.tensor_tensor_scan(tva[0:NB, :], tm[0:NB, :], tm[0:NB, :], 1.0, ALU.mult, ALU.mult)
            link(V.tensor_tensor_scan(tls[0:NB, :], tsp[0:NB, :], tsp[0:NB, :], 0.0, ALU.max, ALU.max))
            link(V.tensor_tensor(tls[0:NB, :], tj, tls[0:NB, :], ALU.subtract))
            link(V.scalar_tensor_tensor(tls[0:NB, :], tls[0:NB, :], 1.0, tva[0:NB, :], ALU.add, ALU.mult))
            V.tensor_scalar(tls[0:NB, :], tls[0:NB, :], 1.0, None, ALU.add).then_inc(pos_r, 1)
            dve.wait_ge(ld_tab, 16)
            for t in range(TAB):
                last = V.bn_stats(st_t[:, t, :], tb[:, t, :])
            link(last)
            for t in range(TAB):
                last = V.bn_aggr(mv_t[:, t, :], st_t[:, t, :])
            last.then_inc(t_var, 1)
            dve.wait_ge(posT_r, 1)
            V.tensor_copy(pos_i[:, 0:NT].rearrange("p (b s) -> p s b", s=2),
                          psT[1][:, 0:NT].rearrange("p (s b) -> p s b", s=2)).then_inc(posi_r, 2)
            for w, st, n in ((wA, wst, 1), (wB, wst2, 2), (wR, wst3, 3)):
                dve.wait_ge(w_hi, n)
                V.scalar_tensor_tensor(w[:, :, 1, :], st, WS, w[:, :, 0, :], ALU.mult, ALU.subtract).then_inc(w_lo, 1)
            dve.wait_ge(t_pow, 1)
            for t in range(TAB):
                link(V.tensor_scalar(thn, tb[:, t, :], mv_t[:, t, 0:1], small[:, 26 + t:27 + t], ALU.subtract, ALU.mult))
                wait(dve, t_T, t)
                link(V.tensor_copy(ths[:, 0, :], thn))
                V.tensor_tensor(ths[:, 1, :], thn, ths[:, 0, :], ALU.subtract).then_inc(t_split, 1)
                dve.wait_ge(t_T, t + 1)
                wait(dve, t_mm, t)
                V.tensor_copy(txT.rearrange("p a b c -> p (a b) c"), psTh[0]).then_inc(t_xT, 1)
                dve.wait_ge(t_u, t + 1)
                link(V.tensor_tensor(usq, u, u, ALU.mult))
                wait(dve, t_rn, t)
                V.tensor_reduce(small[:, 32:64], usq.rearrange("p (a b) -> p a b", b=HD), AX.X, ALU.add).then_inc(t_sum, 1)
                dve.wait_ge(t_rn, t + 1)
                V.tensor_tensor(u.rearrange("p (a b) -> p a b", b=HD), u.rearrange("p (a b) -> p a b", b=HD),
                                small[:, 32:64].unsqueeze(2).to_broadcast([P, 2 * H, HD]), ALU.mult).then_inc(t_out, 1)
            dve.wait_ge(t_wr, 48 * TAB)
            V.memset(small[:, 0:1], 0.0).then_inc(st_free, 2)

            def split_group(b, pg):
                y, z = rp[:, pg % 2].rearrange("p a b c -> p (a b) c"), hl[:, pg % 2]
                zv = z.rearrange("p a b c d e -> p (a b c) d e")
                dve.wait_ge(rope_r, b * 4 + pg + 1)
                wait(dve, tr_r, b * 4 + pg - 1)
                link(V.tensor_copy(zv[:, :, 0, :], y))
                link(V.tensor_tensor(zv[:, :, 1, :], y, zv[:, :, 0, :], ALU.subtract))
                V.tensor_copy(z[:, :, 0, :, 2:4, :].rearrange("p a c d e -> p a c (d e)"),
                              z[:, :, 0, :, 0:2, :].rearrange("p a c d e -> p a c (d e)"))
                V.tensor_copy(z[:, :, 1, :, 2, :], z[:, :, 1, :, 1, :])
                V.tensor_copy(z[:, :, 1, :, 3, :], z[:, :, 1, :, 0, :]).then_inc(split_r, 1)

            def head_outputs(b, gp):
                dve.wait_ge(oT_r, b * 2 + gp + 1)
                av = psW.rearrange("p (t h c) -> p t h c", t=2, c=32)
                link(V.reciprocal(rden2, av[:, :, :, HD]))
                link(V.tensor_tensor(o.rearrange("p t (h c) -> p t h c", c=HD), av[:, :, :, 0:HD],
                                     rden2.unsqueeze(3).to_broadcast([P, 2, 8, HD]), ALU.mult))
                hi = osp[:, :, 0, gp * P:(gp + 1) * P]
                link(V.tensor_copy(hi, o))
                V.tensor_tensor(osp[:, :, 1, gp * P:(gp + 1) * P], o, hi, ALU.subtract).then_inc(osp_r, 1)

            def rows_back(sem_in, sem_out, b):
                dve.wait_ge(sem_in, b + 1)
                V.tensor_copy(xTa.rearrange("p a b c d -> p (a b c d)"), psW.bitcast(fp16)).then_inc(sem_out, 1)

            def residual(b):
                hb = h[:, bass.ds(b * 2, 2), :]
                dve.wait_ge(wo_r, b + 1)
                dve.wait_ge(ob_r, b + 1)
                link(V.scalar_tensor_tensor(hb, psW.rearrange("p (a b) -> p a b", a=2), 1.0 / WS, hb, ALU.mult, ALU.add))
                for half in range(2):
                    last = V.bn_stats(bst[half], h[:, bass.ds(b * 2 + half, 1), :].rearrange("p a b -> p (a b)"))
                link(last)
                for half in range(2):
                    last = V.bn_aggr(mvp[:, half, :], bst[half])
                last.then_inc(var_r, 1)

            def normalise(b):
                dve.wait_ge(pw_r, b + 1)
                for half in range(2):
                    last = V.tensor_scalar(hn2[:, half, :], h[:, bass.ds(b * 2 + half, 1), :].rearrange("p a b -> p (a b)"),
                                           mvp[:, half, 0:1], small[:, 4 + half:5 + half], ALU.subtract, ALU.mult)
                link(last)
                wait(dve, xn_w, b * 16)
                link(V.tensor_copy(hsa[:, :, 0, :], hn2))
                V.tensor_tensor(hsa[:, :, 1, :], hn2, hsa[:, :, 0, :], ALU.subtract).then_inc(hs_r, 1)

            def top2(b):
                dve.wait_ge(lgp_r, b + 1)
                link(V.tensor_scalar(lg[:], psW.rearrange("p (a b) -> p a b", a=2)[:, :, 0:NE], 1.0 / WS, None, ALU.mult))
                V.max(mx8[:, 0, :], lg[:, 0, :])
                link(V.max(mx8[:, 1, :], lg[:, 1, :]))
                V.max_index(ix8[:, 0, :], mx8[:, 0, :], lg[:, 0, :])
                link(V.max_index(ix8[:, 1, :], mx8[:, 1, :], lg[:, 1, :]))
                V.tensor_copy(lgt[:, bass.ds(b * 2, 2), :], lg[:])
                V.tensor_copy(mxt[:, bass.ds(b * 2, 2), :], mx8[:, :, 0:2])
                V.tensor_copy(ixt[:, bass.ds(b * 2, 2), :], ix8[:, :, 0:2]).then_inc(lgs_r, 1)
                dve.wait_ge(lgs_r, b + 1)

            def stage_low(b, q):
                dve.wait_ge(st_hi, b * 4 + q + 1)
                hi = WX[:, bass.ds(b, 1), q, 0, :].rearrange("p e n -> p (e n)")
                lo = WX[:, bass.ds(b, 1), q, 1, :].rearrange("p e n -> p (e n)")
                V.scalar_tensor_tensor(lo, stage[:, q % 2, :], WS, hi, ALU.mult, ALU.subtract).then_inc(st_free, 1)

            def dve_body(b, first=False):
                split_group(b + 1, 0)
                if not first:
                    head_outputs(b - 1, 1)
                split_group(b + 1, 1)
                if not first:
                    rows_back(ot_r, otc_r, b - 1)
                stage_low(b, 0)
                if not first:
                    residual(b - 1)
                split_group(b + 1, 2)
                stage_low(b, 1)
                if not first:
                    normalise(b - 1)
                head_outputs(b, 0)
                split_group(b + 1, 3)
                if not first:
                    rows_back(ht_r, htc_r, b - 1)
                stage_low(b, 2)
                if not first:
                    top2(b - 1)
                stage_low(b, 3)

            for pg in range(4):
                split_group(0, pg)
            dve_body(0, True)
            with dve.Fori(0, NB - 1) as bb:
                dve.sem_clear(dch)
                done[0] = 0
                dve_body(bb + 1)
            dve.sem_clear(dch)
            done[0] = 0
            head_outputs(NB - 1, 1)
            rows_back(ot_r, otc_r, NB - 1)
            residual(NB - 1)
            normalise(NB - 1)
            rows_back(ht_r, htc_r, NB - 1)
            top2(NB - 1)

            dve.wait_ge(rt_ld, 64)
            mx0 = mxt[:, :, 0]
            V.memset(onec, 1.0)
            V.memset(e8[:, 3, :], 0.0)
            V.memset(slot_i[:], 0)
            V.tensor_tensor(m0, ioe.unsqueeze(1).to_broadcast([P, NT, NE]), ixt[:, :, 0:1].to_broadcast([P, NT, NE]), ALU.is_equal)
            link(V.tensor_tensor(m1, ioe.unsqueeze(1).to_broadcast([P, NT, NE]), ixt[:, :, 1:2].to_broadcast([P, NT, NE]), ALU.is_equal))
            V.tensor_tensor(mc, m0, m1, ALU.add).then_inc(rt_c, 1)
            V.tensor_tensor(rqm, mxt[:, :, 1], mx0, ALU.subtract)
            V.tensor_tensor(pe8, lgt[:], mxt[:, :, 0:1].to_broadcast([P, NT, NE]), ALU.subtract).then_inc(rt_d, 1)
            dve.wait_ge(rt_tot, 1)
            V.tensor_copy(totb, psO[0][:, 0:1].to_broadcast([P, P])).then_inc(rt_totc, 1)
            dve.wait_ge(rt_e, 2)
            link(V.tensor_reduce(rqs, pe8, AX.X, ALU.add))
            link(V.reciprocal(gate[:, :, 0], rqs))
            V.tensor_tensor(gate[:, :, 1], gate[:, :, 0], rqm, ALU.mult)
            dve.wait_ge(rt_pre, 1)
            link(V.tensor_scalar(e8i, psT[0][:, 0:NE], float(P - 1), None, ALU.add))
            link(V.tensor_scalar(e8i, e8i, 7, None, ALU.logical_shift_right))
            link(V.tensor_copy(e8[:, 1, :], e8i))
            link(V.tensor_tensor_scan(e8[:, 2, :], e8[:, 1, :], e8[:, 3, :], 0.0, ALU.add, ALU.add))
            link(V.tensor_tensor(e8[:, 4, :], e8[:, 2, :], e8[:, 1, :], ALU.subtract))
            link(V.tensor_scalar(e8[:, 5, :], e8[:, 4, :], float(P), None, ALU.mult))
            link(V.tensor_tensor(p1, psO[1][:, 0:P].rearrange("p (a b) -> p a b", b=NE),
                                 e8[:, 5:6, :].to_broadcast([P, NT, NE]), ALU.add))
            V.tensor_tensor(m0, m0, p1, ALU.mult)
            link(V.tensor_tensor(m1, m1, p1, ALU.mult))
            V.tensor_reduce(sf[:, :, 0], m0, AX.X, ALU.add)
            link(V.tensor_reduce(sf[:, :, 1], m1, AX.X, ALU.add))
            link(V.tensor_copy(slot_i[:, 0:NT, :], sf))
            si = slot_i[:, 0:NT, :].rearrange("p a b -> p (a b)")
            V.tensor_scalar(ri, si, 7, None, ALU.logical_shift_right)
            link(V.tensor_scalar(ri2, si, P - 1, None, ALU.bitwise_and))
            V.tensor_copy(ra, ri)
            link(V.tensor_copy(rb, ri2))
            V.tensor_tensor(ohb, iob.unsqueeze(1).to_broadcast([P, 2 * NT, P]), rb.unsqueeze(2).to_broadcast([P, 2 * NT, P]), ALU.is_equal)
            link(V.tensor_tensor(oha, ioa.unsqueeze(1).to_broadcast([P, 2 * NT, MT]), ra.unsqueeze(2).to_broadcast([P, 2 * NT, MT]), ALU.is_equal))
            oh2 = oha.rearrange("p (a b) c -> p a (b c)", b=2)
            V.tensor_tensor(oh2, oh2, tokid.unsqueeze(2).to_broadcast([P, NT, 2 * MT]), ALU.mult).then_inc(rt_oh, 1)
            link(V.tensor_tensor(ecmp[0:1], ioa[0:1].unsqueeze(2).to_broadcast([1, MT, NE]),
                                 e8[0:1, 2:3, :].to_broadcast([1, MT, NE]), ALU.is_ge))
            link(V.tensor_reduce(rq_e[0:1], ecmp[0:1], AX.X, ALU.add))
            V.tensor_scalar(ej[:], rq_e[0:1], float(NE - 1), None, ALU.min)
            dve.wait_ge(rt_inv, 1)
            V.tensor_copy(inv_i[:], psT[1][:, 0:MT]).then_inc(rt_idx, 1)
            dve.wait_ge(f_ac, 1)
            V.tensor_copy(fa.rearrange("p a b c -> p (a b) c"), psS[:, :, 0:D]).then_inc(f_ac, 1)
            dve.wait_ge(f_mh, 1)
            V.scalar_tensor_tensor(wM[:, :, 1, :], psS[:, 0:2, 0:D], WS / D, wM[:, :, 0, :], ALU.mult, ALU.subtract).then_inc(f_ml, 1)
            for w, st, n in ((wB, wst1o, 1), (wA, wst1, 2)):
                dve.wait_ge(w1_hi, n)
                V.scalar_tensor_tensor(w[:, :, 1, :], st, WS, w[:, :, 0, :], ALU.mult, ALU.subtract).then_inc(w1_lo, 1)
            dve.sem_inc(m_y, 2)
            dve.sem_inc(m_yw[0], 16)
            dve.sem_inc(m_yw[1], 16)
            dve.sem_inc(m_gs, 4)
            dve.wait_ge(m_b2, 16)

            def rows_in(j, i):
                dve.wait_ge(m_T, j + 3)
                V.tensor_copy(exT[:, i, :, :, :].rearrange("p a b c -> p (a b) c"), psTh[i]).then_inc(m_Tc, 1)

            def split_hidden(j, i):
                for q in range(2):
                    c = slice(4 * q, 4 * q + 4)
                    dve.wait_ge(m_act, j * 2 + q + 1)
                    dve.wait_ge(m_g2, j + 1)
                    V.tensor_copy(gs[:, i, 0, c, :], g[:, i, c, :]).then_inc(m_hi, 1)
                    dve.wait_ge(m_hi, j * 2 + q + 1)
                    V.tensor_tensor(gs[:, i, 1, c, :], g[:, i, c, :], gs[:, i, 0, c, :], ALU.subtract).then_inc(m_gs, 1)

            def y_in(j, i):
                e = dve.value_load(ej[0:1, bass.ds(j, 1)], min_val=0, max_val=NE - 1)
                dve.wait_ge(m_g2, j + 3)
                V.scalar_tensor_tensor(y[:, i, :], psO[i][:, 0:D], 1.0 / WS, b2bc[:, bass.ds(e, 1), :].rearrange("p a b -> p (a b)"),
                                       ALU.mult, ALU.add).then_inc(m_y, 1)

            def y_free(i, n):
                dve.wait_ge(m_yw[i], n)

            rows_in(0, 0)
            rows_in(1, 1)
            split_hidden(0, 0)
            with dve.Fori(0, MT // 2 - 1) as jj:
                for i in (1, 0):
                    j = jj * 2 + (1 if i else 2)
                    rows_in(j + 1, 1 - i)
                    split_hidden(j, i)
                    dve.wait_ge(m_yw[1 - i], jj * 16 + 16)
                    y_in(j - 1, 1 - i)
            for j in (MT - 2, MT - 1):
                i = j % 2
                if j + 1 < MT:
                    rows_in(j + 1, 1 - i)
                split_hidden(j, i)
                dve.wait_ge(m_yw[1 - i], 16 * ((j - 1) // 2) + 16)
                y_in(j - 1, 1 - i)
            dve.wait_ge(m_yw[0], 16 * ((MT - 1) // 2) + 16)
            y_in(MT - 1, 0)

            dve.wait_ge(m_yw[0], 16 * ((MT + 1) // 2) + 16)
            dve.wait_ge(m_yw[1], 16 * (MT // 2) + 16)
            dve.wait_ge(l1_ld, 80)
            V.memset(mask3[:, 1, :], 1.0)
            link(V.memset(lvaug[:, :, :, :, HD:VW], 1.0))
            for i in range(2):
                V.memset(psO[i][:], 0.0)

            def seq(b):
                return h[:, bass.ds(b * 2, 2), :]

            def row(b, half):
                return h[:, bass.ds(b * 2 + half, 1), :].rearrange("p a b -> p (a b)")

            def statistics(b, stats, ready):
                for half in range(2):
                    last = V.bn_stats(bst[half], row(b, half))
                link(last)
                for half in range(2):
                    last = V.bn_aggr(stats[:, half, :], bst[half])
                last.then_inc(ready, 1)

            def combine(b):
                dve.wait_ge(n_y, b * 64 + 64)
                for k in range(2):
                    for half in range(2):
                        gt = gate[:, bass.ds(b * 2 + half, 1), :].rearrange("p a b -> p (a b)")
                        last = V.scalar_tensor_tensor(row(b, half), yg[:, k, half, :], gt[:, k:k + 1], row(b, half), ALU.mult, ALU.add)
                    link(last)
                statistics(b, mvp, n_var)

            def late_normalise(b, stats, root, powered, rows, ready):
                dve.wait_ge(powered, b + 1)
                for half in range(2):
                    last = V.tensor_scalar(lhn[:, half, :], row(b, half), stats[:, half, 0:1], small[:, root + half:root + half + 1],
                                           ALU.subtract, ALU.mult)
                link(last)
                link(V.tensor_copy(rows[:, :, 0, :], lhn))
                V.tensor_tensor(rows[:, :, 1, :], lhn, rows[:, :, 0, :], ALU.subtract).then_inc(ready, 1)

            def prep_rows(b):
                late_normalise(b, mvp, 4, n_pow, lps, n_hs)

            def tail_rows(b):
                late_normalise(b, mvq, 24, n_pow2, lhs, n_hs2)

            def late_rows_back(b, ready, bank, dst, done_sem):
                dve.wait_ge(ready, b + 1)
                V.tensor_copy(dst.rearrange("p a b c d -> p (a b c d)"), bank.bitcast(fp16)).then_inc(done_sem, 1)

            def q_and_k(b, half):
                dve.wait_ge(n_qkv, b * 3 + half + 1)
                V.scalar_tensor_tensor(lx[:, half], psT[0][:], 1.0 / WS, bias_bc[:, 0:2 * D], ALU.mult, ALU.add).then_inc(n_x, 1)
                dve.wait_ge(n_x, b * 3 + half + 1)
                V.tensor_scalar(lmn[:, half], lx[:, half], 0.0, None, ALU.min).then_inc(n_min, 1)

            def values(b):
                dve.wait_ge(n_qkv, b * 3 + 3)
                V.scalar_tensor_tensor(lv[:, bass.ds(b, 1), :, :].rearrange("p a s n -> p (a s) n"),
                                       psT[0][:].rearrange("p (s n) -> p s n", s=2),
                                       1.0 / WS, bias_bc[:, 2 * D:3 * D].unsqueeze(1).to_broadcast([P, 2, D]),
                                       ALU.mult, ALU.add).then_inc(n_x, 1)

            def elu1(b, half):
                dve.wait_ge(n_exp, b * 2 + half + 1)
                return V.scalar_tensor_tensor(lr[:, half].rearrange("p a b c -> p (a b c)"), lx[:, half], 0.0, lmn[:, half],
                                              ALU.max, ALU.add)

            def late_split(b, pg):
                z = lhl[:, pg % 2].rearrange("p a b c d e -> p (a b) c d e")
                y = lr[:, :, :, 4 * pg:4 * pg + 4, :].rearrange("p a b c e -> p (a b) c e")
                wait(dve, n_tr, b * 4 + pg - 1)
                link(V.tensor_copy(z[:, :, :, 0, :], y))
                V.tensor_tensor(z[:, :, :, 1, :], y, z[:, :, :, 0, :], ALU.subtract).then_inc(n_hl, 1)

            def first_head(b, p):
                dve.wait_ge(n_sc, b * 8 + p + 1)
                wait(dve, n_av, b * 8 + p - 1)
                V.tensor_tensor(lE[:, p % 2, 0], psS[:, 2 * (p % 2), 0:3 * P].rearrange("p (a b) -> p a b", b=P),
                                mask3, ALU.mult).then_inc(n_ms, 1)

            def late_heads(b, gp):
                dve.wait_ge(n_oT, b * 2 + gp + 1)
                av = psW.rearrange("p (t h c) -> p t h c", t=2, c=32)
                link(V.tensor_scalar(rden2, av[:, :, :, HD], EPS_L1, None, ALU.add))
                link(V.reciprocal(rden2, rden2))
                link(V.tensor_tensor(lo.rearrange("p t (h c) -> p t h c", c=HD), av[:, :, :, 0:HD],
                                     rden2.unsqueeze(3).to_broadcast([P, 2, 8, HD]), ALU.mult))
                hi = losp[:, :, 0, gp * P:(gp + 1) * P]
                link(V.tensor_copy(hi, lo))
                V.tensor_tensor(losp[:, :, 1, gp * P:(gp + 1) * P], lo, hi, ALU.subtract).then_inc(n_osp, 1)

            def late_residual(b):
                dve.wait_ge(n_wo, b + 1)
                dve.wait_ge(n_hb, b + 1)
                link(V.scalar_tensor_tensor(seq(b), psW.rearrange("p (a b) -> p a b", a=2), 1.0 / WS, seq(b), ALU.mult, ALU.add))
                statistics(b, mvq, n_var2)

            def result(b):
                dve.wait_ge(n_ff, b + 1)
                dve.wait_ge(n_fb, b + 1)
                V.scalar_tensor_tensor(seq(b), psW.rearrange("p (a b) -> p a b", a=2), 1.0 / WS, seq(b), ALU.mult, ALU.add).then_inc(n_out, 1)

            def dve_late(b, tail=True, group=True, prep=True, ahead=True):
                first_head(b, 1)
                if tail:
                    late_heads(b - 1, 1)
                if group:
                    late_split(b + 1, 0)
                first_head(b, 2)
                if prep:
                    late_rows_back(b + 2, n_hT, psT[0][:], lxT, n_hTc)
                first_head(b, 3)
                if tail:
                    late_rows_back(b - 1, n_lT, psW, lyT, n_lTc)
                if group:
                    late_split(b + 1, 1)
                if ahead:
                    combine(b + 3)
                first_head(b, 4)
                if prep:
                    q_and_k(b + 2, 0)
                if tail:
                    late_residual(b - 1)
                first_head(b, 5)
                if group:
                    late_split(b + 1, 2)
                if prep:
                    q_and_k(b + 2, 1)
                first_head(b, 6)
                if tail:
                    tail_rows(b - 1)
                late_heads(b, 0)
                first_head(b, 7)
                if group:
                    late_split(b + 1, 3)
                if tail:
                    late_rows_back(b - 1, n_gT, psW, lyT, n_gTc)
                if prep:
                    dve.wait_ge(n_hl, b * 4 + 8)
                    elu1(b + 2, 0)
                    values(b + 2)
                if group:
                    first_head(b + 1, 0)
                if prep:
                    link(elu1(b + 2, 1))
                if ahead:
                    prep_rows(b + 3)
                if tail:
                    result(b - 1)

            def to_elu(b):
                late_rows_back(b, n_hT, psT[0][:], lxT, n_hTc)
                q_and_k(b, 0)
                q_and_k(b, 1)
                values(b)

            combine(0)
            prep_rows(0)
            combine(1)
            to_elu(0)
            prep_rows(1)
            elu1(0, 0)
            link(elu1(0, 1))
            combine(2)
            for pg in range(4):
                late_split(0, pg)
            to_elu(1)
            elu1(1, 0)
            link(elu1(1, 1))
            prep_rows(2)
            first_head(0, 0)
            dve_late(0, tail=False)
            with dve.Fori(0, NB - 4) as bb:
                dve.sem_clear(dch)
                done[0] = 0
                dve_late(bb + 1)
            dve_late(NB - 3, ahead=False)
            dve_late(NB - 2, prep=False, ahead=False)
            dve_late(NB - 1, group=False, prep=False, ahead=False)
            late_heads(NB - 1, 1)
            late_rows_back(NB - 1, n_lT, psW, lyT, n_lTc)
            late_residual(NB - 1)
            tail_rows(NB - 1)
            late_rows_back(NB - 1, n_gT, psW, lyT, n_gTc)
            result(NB - 1)

        @block.tensor
        def _(pe):
            M, TR = nc.tensor.matmul, nc.tensor.transpose

            def transpose_rows(ps, rows):
                for a in range(2):
                    for c in range(KC):
                        last = TR(ps[:, a * KC + c, :], rows[:, a, c * P:(c + 1) * P], identh[:])
                return last

            pe.wait_ge(ld_ident, 32)
            pe.wait_ge(pos_r, 1)
            for sq in range(2):
                last = TR(psT[1][:, sq * NB:(sq + 1) * NB], tls[0:NB, sq * P:(sq + 1) * P], ident[0:NB, 0:NB])
            last.then_inc(posT_r, 1)
            pe.wait_ge(w_lo, 3)
            for t in range(TAB):
                pe.wait_ge(t_split, t + 1)
                transpose_rows(psTh[0], ths).then_inc(t_T, 1)
                pe.wait_ge(t_xT, t + 1)
                wait(pe, t_v, t)
                split3(psS[:, 0, :], txT, wA, 0, 2 * D)
                split3(psS[:, 1, :], txT, wA, 2 * D, 3 * D).then_inc(t_mm, 1)
            pe.wait_ge(posi_r, 2)

            def group_T(b, pg):
                pe.wait_ge(split_r, b * 4 + pg + 1)
                wait(pe, qk_r, b * 4 + pg)
                for half in range(2):
                    for a in range(2):
                        for qk in range(2):
                            last = TR(psTf[:, half, 2 * a + qk, :],
                                      hl[:, pg % 2, half, qk, 2 * a:2 * a + 2].rearrange("p a b c -> p (a b c)"), identh[:])
                last.then_inc(tr_r, 1)

            def scores(b, p):
                pe.wait_ge(qk_r, b * 4 + p // 2 + 1)
                wait(pe, ex_r, b * 8 + p - 1)
                for e in range(2):
                    rows = slice(64 * e, 64 * e + 64)
                    for st in range(2):
                        last = M(psS[:, 2 * (p % 2) + e, st * T:(st + 1) * T],
                                 qkT[rows, p, 1, st * P:(st + 1) * P], qkT[rows, p, 0, :], start=True, stop=True)
                last.then_inc(sc_r, 1)

            def weighted(b, p):
                gp = p // 4
                pe.wait_ge(ex_r, b * 8 + p + 1)
                if p % 4 == 0:
                    pe.wait_ge(g_v[gp], b * 32 + 32)
                    wait(pe, oc_r, b * 2 + gp - 1)
                for e in range(2):
                    hd = 2 * (p % 4) + e
                    for st in range(2):
                        last = M(psO[gp][32 * (hd % 4):32 * (hd % 4) + VW, (hd // 4) * T:(hd // 4 + 1) * T],
                                 vaug[:, gp, st, hd, :], E[:, p % 2, e, st * T:(st + 1) * T], start=(st == 0), stop=(st == 1))
                last.then_inc(av_r, 1)

            def sums_T(b, gp):
                pe.wait_ge(oc_r, b * 2 + gp + 1)
                if gp:
                    wait(pe, lgs_r, b)
                    pe.wait_ge(osp_r, b * 2 + 1)
                else:
                    wait(pe, var_r, b)
                for tt in range(2):
                    for st in range(2):
                        last = TR(psW[:, (2 * tt + st) * P:(2 * tt + st + 1) * P], oTs[:, st * T + tt * P:st * T + (tt + 1) * P], ident[:])
                last.then_inc(oT_r, 1)

            def out_T(b):
                pe.wait_ge(osp_r, b * 2 + 2)
                for half in range(2):
                    last = transpose_rows(psWh[:, half], osp[:, half, :, :])
                last.then_inc(ot_r, 1)

            def project(b):
                pe.wait_ge(otc_r, b + 1)
                for half in range(2):
                    last = split3(psW[:, half * D:], xTa[:, half], wB, 0, D)
                last.then_inc(wo_r, 1)

            def norm_T(b):
                pe.wait_ge(hs_r, b + 1)
                for half in range(2):
                    last = transpose_rows(psWh[:, half], hsa[:, half, :, :])
                last.then_inc(ht_r, 1)

            def route(b):
                pe.wait_ge(htc_r, b + 1)
                for half in range(2):
                    last = split3(psW[:, half * D:], xTa[:, half], wR, 0, NE)
                last.then_inc(lgp_r, 1)

            def pe_body(b, first=False):
                for p in range(8):
                    if p < 7:
                        scores(b, p + 1)
                    else:
                        scores(b + 1, 0)
                    weighted(b, p)
                    if p % 2:
                        group_T(b + 1, p // 2)
                    if not first:
                        if p == 0:
                            sums_T(b - 1, 1)
                        if p == 1:
                            out_T(b - 1)
                        if p == 3:
                            project(b - 1)
                        if p == 6:
                            pe.wait_ge(osp_r, b * 2 + 1)
                            norm_T(b - 1)
                        if p == 7:
                            route(b - 1)
                    if p == 5:
                        sums_T(b, 0)

            for pg in range(4):
                group_T(0, pg)
            scores(0, 0)
            pe_body(0, True)
            with pe.Fori(0, NB - 1) as bb:
                pe_body(bb + 1)
            sums_T(NB - 1, 1)
            out_T(NB - 1)
            project(NB - 1)
            norm_T(NB - 1)
            route(NB - 1)

            pe.wait_ge(rt_c, 1)
            M(psO[0][:, 0:1], mc.rearrange("p a b -> p (a b)"), onec, start=True, stop=True).then_inc(rt_tot, 1)
            pe.wait_ge(rt_totc, 1)
            M(psO[1][:, 0:P], totb, tpre, start=True, stop=False)
            M(psO[1][:, 0:P], ltri, mc.rearrange("p a b -> p (a b)"), start=False, stop=True)
            M(psT[0][:, 0:NE], totb, tsum, start=True, stop=True).then_inc(rt_pre, 1)
            pe.wait_ge(f_a, 48)
            for part in range(2):
                for m in range(KC):
                    for k in range(KC):
                        for w in range(2):
                            tab = ((0, 1), (1, 2))[part][w]
                            last = M(psS[:, part * KC + m, 0:D], fw[:, w, k, m * P:(m + 1) * P], dft[:, tab, k, :],
                                     start=(k == 0 and w == 0), stop=(k == KC - 1 and w == 1))
            last.then_inc(f_ac, 1)
            pe.wait_ge(rt_oh, 1)
            for k in range(2 * NT):
                last = M(psT[1][:, 0:MT], ohb[:, k, :], oha[:, k, :], start=(k == 0), stop=(k == 2 * NT - 1))
            last.then_inc(rt_inv, 1)
            pe.wait_ge(f_ac, 2)
            for m in range(KC):
                for n in range(KC):
                    for part in range(2):
                        last = M(psS[:, m, 0:D], fa[:, part, n, m * P:(m + 1) * P], dft[:, part, n, :],
                                 start=(n == 0 and part == 0), stop=(n == KC - 1 and part == 1))
            last.then_inc(f_m, 1)

            pe.wait_ge(rt_idx, 1)
            pe.wait_ge(f_ml, 1)
            pe.sem_inc(m_g1, 2)
            pe.sem_inc(m_g2, 2)

            def expert(j):
                return pe.value_load(ej[0:1, bass.ds(j, 1)], min_val=0, max_val=NE - 1)

            def rows_T(j, i, n):
                pe.wait_ge(m_x[i], n * 16 + 16)
                transpose_rows(psTh[i], xs[:, i, :, :]).then_inc(m_T, 1)

            def hidden(j, i):
                e = expert(j)
                pe.wait_ge(m_Tc, j + 1)
                for q in range(2):
                    pe.wait_ge(m_gs, j * 2 + q + 1)
                    for c in range(4 * q, 4 * q + 4):
                        k = 0
                        for kc in range(KC):
                            for wp, xp in ((0, 0), (0, 1), (1, 0)):
                                w = WX[:, bass.ds(e, 1), kc, wp, c * P:(c + 1) * P].rearrange("p a b -> p (a b)")
                                last = M(psS[:, 2 * i + q, (c % 4) * P:(c % 4 + 1) * P], w, exT[:, i, xp, kc, :],
                                         start=(k == 0), stop=(k == 5))
                                k += 1
                    last.then_inc(m_g1, 1)

            def outputs(j, i):
                e = expert(j)
                k = 0
                for c in range(CH):
                    if c % 4 == 0:
                        pe.wait_ge(m_gs, j * 2 + c // 4 + 5)
                    if c == 0:
                        pe.wait_ge(m_y, j + 1)
                    for xp, wp in ((0, 0), (0, 1), (1, 0)):
                        w = WX[:, bass.ds(e, 1), 2 + c // 4, wp, (c % 4) * D:(c % 4 + 1) * D].rearrange("p a b -> p (a b)")
                        last = M(psO[i][:, 0:D], gs[:, i, xp, c, :], w, start=(k == 0), stop=(k == 3 * CH - 1))
                        k += 1
                last.then_inc(m_g2, 1)

            rows_T(0, 0, 0)
            hidden(0, 0)
            rows_T(1, 1, 0)
            with pe.Fori(0, MT // 2 - 1) as jj:
                for i in (1, 0):
                    j = jj * 2 + (1 if i else 2)
                    hidden(j, i)
                    rows_T(j + 1, 1 - i, jj + 1)
                    outputs(j - 1, 1 - i)
            hidden(MT - 2, 1)
            rows_T(MT - 1, 0, MT // 2)
            outputs(MT - 3, 0)
            hidden(MT - 1, 0)
            outputs(MT - 2, 1)
            outputs(MT - 1, 0)

            pe.wait_ge(m_y, MT + 2)
            pe.wait_ge(w1_lo, 2)

            def late_norm_T(b, free, count):
                pe.wait_ge(n_hs, b + 1)
                wait(pe, free, count)
                for half in range(2):
                    last = transpose_rows(psTb[:, half], lps[:, half, :, :])
                last.then_inc(n_hT, 1)

            def late_qkv(b, part, free, count):
                pe.wait_ge(n_hTc, b + 1)
                wait(pe, free, count)
                if part < 2:
                    last = split3(psT[0], lxT[:, part], wA, 0, 2 * D)
                else:
                    for half in range(2):
                        last = split3(psT[0], lxT[:, half], wA, 2 * D, 3 * D, half * D)
                last.then_inc(n_qkv, 1)

            def late_group_T(b, pg, free, count):
                pe.wait_ge(n_spl, b * 4 + pg + 1)
                wait(pe, free, count)
                for half in range(2):
                    for a in range(2):
                        for qk in range(2):
                            last = TR(psTf[:, half, 2 * a + qk, :],
                                      lhl[:, pg % 2, half, qk, 2 * a:2 * a + 2].rearrange("p a b c -> p (a b c)"), identh[:])
                last.then_inc(n_tr, 1)

            def late_scores(b, p):
                pe.wait_ge(n_qk, b * 4 + p // 2 + 1)
                wait(pe, n_ms, b * 8 + p - 1)
                wait(pe, n_mid, b * 8 + p - 1)
                for e in range(2):
                    rows = slice(64 * e, 64 * e + 64)
                    ps = psS[:, 2 * (p % 2) + e, :]
                    M(ps[:, 0:T], lqkT[rows, p, 1, 0:P], lqkT[rows, p, 0, :], start=True, stop=True)
                    last = M(ps[:, T:T + P], lqkT[rows, p, 1, P:T], lqkT[rows, p, 0, P:T], start=True, stop=True)
                last.then_inc(n_sc, 1)

            def late_weighted(b, p):
                gp = p // 4
                pe.wait_ge(n_ms, b * 8 + p + 1)
                pe.wait_ge(n_pm, b * 8 + p + 1)
                if p % 4 == 0:
                    pe.wait_ge(n_vc, b * 2 + gp + 1)
                    wait(pe, n_oc, b * 2 + gp - 1)
                for e in range(2):
                    hd = 2 * (p % 4) + e
                    rows, c0 = slice(32 * (hd % 4), 32 * (hd % 4) + VW), (hd // 4) * T
                    M(psO[gp][rows, c0:c0 + T], lvaug[:, gp, 0, hd, :], lE[:, p % 2, e, 0:2, :].rearrange("p a b -> p (a b)"),
                      start=True, stop=False)
                    last = M(psO[gp][rows, c0 + P:c0 + T], lvaug[:, gp, 1, hd, :], lE[:, p % 2, e, 2, :], start=False, stop=True)
                last.then_inc(n_av, 1)

            def late_sums_T(b, gp):
                pe.wait_ge(n_oc, b * 2 + gp + 1)
                if gp:
                    wait(pe, n_out, b)
                    pe.wait_ge(n_osp, b * 2 + 1)
                else:
                    wait(pe, n_var2, b)
                for tt in range(2):
                    for st in range(2):
                        last = TR(psW[:, (2 * tt + st) * P:(2 * tt + st + 1) * P], loTs[:, st * T + tt * P:st * T + (tt + 1) * P], ident[:])
                last.then_inc(n_oT, 1)

            def late_T(b, ready, rows, value, done_sem):
                pe.wait_ge(ready, value)
                for half in range(2):
                    last = transpose_rows(psWh[:, half], rows[:, half, :, :])
                last.then_inc(done_sem, 1)

            def late_product(b, ready, w, done_sem):
                pe.wait_ge(ready, b + 1)
                for half in range(2):
                    last = split3(psW[:, half * D:], lyT[:, half], w, 0, D)
                last.then_inc(done_sem, 1)

            def pe_late(b, tail=True, group=True, prep=True):
                for p in range(8):
                    if p < 7:
                        late_scores(b, p + 1)
                    elif group:
                        late_scores(b + 1, 0)
                    late_weighted(b, p)
                    if tail:
                        if p == 0:
                            late_sums_T(b - 1, 1)
                        if p == 1:
                            late_T(b - 1, n_osp, losp, b * 2, n_lT)
                        if p == 3:
                            late_product(b - 1, n_lTc, wB, n_wo)
                        if p == 6:
                            pe.wait_ge(n_osp, b * 2 + 1)
                            late_T(b - 1, n_hs2, lhs, b, n_gT)
                        if p == 7:
                            late_product(b - 1, n_gTc, wM, n_ff)
                    if p == 5:
                        late_sums_T(b, 0)
                    if p == 0 and prep:
                        if tail:
                            late_norm_T(b + 2, n_qk, b * 4 + 4)
                        else:
                            late_norm_T(b + 2, n_x, b * 3 + 6)
                    if p and p % 2 == 0 and prep:
                        late_qkv(b + 2, p // 2 - 1, n_qk, b * 4 + 4 + p // 2)
                    if p % 2 and group:
                        if not prep:
                            late_group_T(b + 1, p // 2, n_qk, b * 4 + 4 + p // 2)
                        elif p == 1:
                            late_group_T(b + 1, 0, n_hTc, b + 3)
                        else:
                            late_group_T(b + 1, p // 2, n_x, b * 3 + 6 + p // 2)

            for c in range(2):
                late_norm_T(c, n_qk, c * 4)
                for part in range(3):
                    late_qkv(c, part, n_x, (c * 3 + part) if part else 0)
                if c == 0:
                    for pg in range(4):
                        late_group_T(0, pg, n_qk if pg else n_x, pg if pg else 3)
            late_scores(0, 0)
            pe_late(0, tail=False)
            with pe.Fori(0, NB - 3) as bb:
                pe_late(bb + 1)
            pe_late(NB - 2, prep=False)
            pe_late(NB - 1, group=False, prep=False)
            late_sums_T(NB - 1, 1)
            late_T(NB - 1, n_osp, losp, NB * 2, n_lT)
            late_product(NB - 1, n_lTc, wB, n_wo)
            late_T(NB - 1, n_hs2, lhs, NB, n_gT)
            late_product(NB - 1, n_gTc, wM, n_ff)


_HOST = ["x", "L0_tok_weights", "L0_attn_Wqkv", "L0_attn_Wo", "L0_attn_bo", "L0_ffn_w_router", "L0_ffn_w1", "L0_ffn_b1",
         "L0_ffn_w2", "L0_ffn_b2", "L1_attn_w_qkv", "L1_attn_b_qkv", "L1_attn_w_out", "L1_attn_b_out",
         "L1_ffn_w_freq_real", "L1_ffn_w_freq_imag", "L1_ffn_bias"]


def constants():
    import numpy as np
    f = np.float32
    pos = np.arange(T, dtype=f)
    inv = (1.0 / np.power(f(10000.0), np.arange(HD // 2, dtype=f) / f(HD // 2))).astype(f)
    ang = pos[:, None] * inv[None, :]
    cos = np.concatenate([np.cos(ang), np.cos(ang)], 1)
    sin = np.concatenate([-np.sin(ang), np.sin(ang)], 1)
    rope = np.stack([cos, sin], 1).reshape(2, P, 2, HD).transpose(1, 0, 2, 3)
    te = np.arange(P)
    tile, ex = te // NE, te % NE
    lt = (te[:, None] < te[None, :])
    k = np.arange(D)
    ang2 = 2.0 * np.pi * ((k[:, None] * k[None, :]) % D) / D
    dft = np.stack([np.cos(ang2), np.sin(ang2), -np.cos(ang2)]).reshape(3, KC, P, D).transpose(2, 0, 1, 3)
    iota = np.concatenate([np.tile(np.arange(P), (P, 1)), np.tile(np.arange(MT), (P, 1)), np.tile(np.arange(NE), (P, 1)),
                           np.arange(NT)[None, :] * P + te[:, None]], 1)
    c = {
        "c_ident": np.eye(P, dtype=f), "c_identh": np.eye(P, dtype=np.float16), "c_rope": rope,
        "c_j": np.tile(np.arange(T), (NB, 1)),
        "c_ltri": lt, "c_tpre": (ex[:, None] == ex[None, :]) & (tile[:, None] < tile[None, :]),
        "c_tsum": ex[:, None] == np.arange(NE)[None, :],
        "c_causal": te[:, None] <= te[None, :], "c_dft": dft, "c_iota": iota,
    }
    return {n: np.ascontiguousarray(a if a.dtype == np.float16 else a.astype(f)) for n, a in c.items()}


def kernel(**inputs):
    import numpy as _np
    import concourse.bacc as _bacc
    from concourse.bass_utils import run_bass_kernel_spmd as _run

    nc = _bacc.Bacc("TRN2", target_bir_lowering=False, num_devices=1)
    arrays, args = {}, []
    given = {n: _np.asarray(inputs[n]) for n in _HOST}
    given["L0_ffn_b1"] = given["L0_ffn_b1"].reshape(NE, CH, P).transpose(2, 0, 1)
    given["L1_attn_w_qkv"] = given["L1_attn_w_qkv"].T
    given["L1_attn_w_out"] = given["L1_attn_w_out"].T
    given.update(constants())
    for name, a in given.items():
        a = _np.ascontiguousarray(a)
        arrays["in_" + name] = a
        args.append(nc.dram_tensor("in_" + name, a.shape, mybir.dt.from_np(a.dtype), kind="ExternalInput").ap())
    out = nc.dram_tensor("out_0", (NB, T, D), fp32, kind="ExternalOutput").ap()
    lm_tower(nc, *args, out)
    r = _run(nc, [arrays], core_ids=[0])
    return r.results[0]["out_0"]
```

```python
import concourse.bass as bass
from concourse import mybir
from contextlib import ExitStack

fp32 = mybir.dt.float32
fp16 = mybir.dt.float16
i32 = mybir.dt.int32
u32 = mybir.dt.uint32
ALU = mybir.AluOpType
ACT = mybir.ActivationFunctionType
AX = mybir.AxisListType

P = 128
NB, T, D = 8, 256, 256
NT = NB * T // P
H, HD = 16, 16
NE, HID, TOPK = 8, 1024, 2
VW = HD + 1
TAB = 3
MT = (TOPK * NB * T + NE * (P - 1)) // P
CH = HID // P
WS = 64.0
EPS_LN, EPS_QK, EPS_L1 = 1e-5, 1e-6, 1e-6
KC = D // P


def wait(eng, sem, value):
    if isinstance(value, int) and value <= 0:
        return
    eng.wait_ge(sem, value)


def lm_tower(nc, x, table, wqkv0, wo0, bo0, wr, w1, b1, w2, b2, wqkv1, bqkv1, wout1, bout1,
             fre, fim, fbias, c_ident, c_identh, c_rope, c_j, c_ltri, c_tpre, c_tsum, c_causal,
             c_dft, c_iota, out):
    ctx = ExitStack()
    with ctx:
        def sb(name, shape, dt):
            return ctx.enter_context(nc.sbuf_tensor(name, shape, dt))

        def sem(name):
            return ctx.enter_context(nc.semaphore(name))

        tab_qk = nc.dram_tensor("tab_qk", (TAB * P, 2 * D), fp32).ap()
        tab_v = [nc.dram_tensor(f"tab_v{i}", (TAB * P, H * VW // 2), fp32).ap() for i in range(2)]
        xn_d = nc.dram_tensor("xn_d", (NT * P, 2 * D), fp16).ap()
        y_d = nc.dram_tensor("y_d", (MT * P, D), fp32).ap()

        WX = sb("expert_weights", [P, NE, 4, 2, 1024], fp16)
        h = sb("h", [P, NT, D], fp32)
        wA = sb("w_qkv_split", [P, KC, 2, 3 * D], fp16)
        wB = sb("w_o_split", [P, KC, 2, D], fp16)
        wM = sb("w_fft_split", [P, KC, 2, D], fp16)
        wR = sb("w_router_split", [P, KC, 2, NE], fp16)
        ident = sb("ident", [P, P], fp32)
        identh = sb("identh", [P, P], fp16)
        rope = sb("rope", [P, 2, 2, HD], fp32)
        pos_i = sb("pos_i", [P, NT + 4], i32)
        posx = sb("posx", [P, 3, 2, 1], i32)
        bias_bc = sb("bias_bc", [P, 5 * D], fp32)
        stage = sb("stage", [P, 2, 1024], fp32)
        lgt = sb("lgt", [P, NT, NE], fp32)
        mxt = sb("mxt", [P, NT, 2], fp32)
        ixt = sb("ixt", [P, NT, 2], fp32)
        gate = sb("gate", [P, NT, 2], fp32)
        slot_i = sb("slot_i", [P, NT + 2, 2], i32)
        inv_i = sb("inv_i", [P, MT], i32)
        ej = sb("ej", [1, MT], i32)
        UN = 4
        GR = MT // UN + 1
        epk = sb("epk", [1, GR], i32)
        posy = sb("posy", [P, 4, 2, 2, 1], i32)
        b1s = sb("b1s", [P, NE, CH], fp32)
        small = sb("small", [P, 64], fp32)
        mexp = sb("minus_half", [P, 32], fp32)
        epsc = sb("epsc", [P, 1], fp32)
        neg1 = sb("minus_one", [P, 1], fp32)
        lg = sb("lg", [P, 2, NE], fp32)
        mx8 = sb("mx8", [P, 2, 8], fp32)
        ix8 = sb("ix8", [P, 2, 8], u32)
        AW = 9536
        arena = sb("arena", [P, AW], fp32)

        def view(at, shape, dt=fp32, memory=None):
            n = 1
            for s in shape:
                n *= s
            words = n if dt in (fp32, i32, u32) else n // 2
            a = (arena[:] if memory is None else memory)[:, at:at + words]
            if dt != fp32:
                a = a.bitcast(dt)
            names = " ".join("abcdef"[i] for i in range(len(shape)))
            if len(shape) > 1:
                a = a.rearrange(f"p ({names}) -> p {names}", **{"abcdef"[i]: shape[i] for i in range(1, len(shape))})
            return a, at + words

        at = 0
        qkg, at = view(at, [2, 4, 2 * 4, HD])
        rp, at = view(at, [2, 2, 8, HD])
        rp2, at = view(at, [2, 8, HD])
        hl, at = view(at, [2, 2, 2, 4, 4, HD], fp16)
        qkT, at = view(at, [8, 2, T], fp16)
        vaug, at = view(at, [2, 2, H // 2, VW])
        E, at = view(at, [2, 2, 2 * T])
        hn2, _ = view(at, [2, D])
        o, at = view(at, [2, P])
        at += D
        osp, at = view(at, [2, 2, D], fp16)
        oTs, at = view(at, [2 * T])
        assert at <= AW, at
        xTa = bias_bc[:, 3 * D:5 * D].bitcast(fp16).rearrange("p (a b c d) -> p a b c d", a=2, b=2, c=KC)
        hsa = bias_bc[:, D:3 * D].bitcast(fp16).rearrange("p (a b c) -> p a b c", a=2, b=2)
        big = WX[:].rearrange("p a b c d -> p (a b c d)").bitcast(fp32)
        EW = 4 * 1024

        def late(at, shape, dt=fp32):
            return view(at, shape, dt, big)

        at = 0
        lx, at = late(at, [2, 2 * D])
        lmn, at = late(at, [2, 2 * D])
        lr, at = late(at, [2, 2, H, HD])
        lhl, at = late(at, [2, 2, 2, 4, 4, HD], fp16)
        lqkT, at = late(at, [8, 2, T], fp16)
        lv, at = late(at, [NB, 2, 2 * (H // 2) * HD])
        lvaug, at = late(at, [2, 2, H // 2, VW])
        lE, at = late(at, [2, 2, 3, P])
        lo, at = late(at, [2, P])
        lhn, at = late(at, [2, D])
        losp, at = late(at, [2, 2, D], fp16)
        loTs, at = late(at, [2 * T])
        lhs, at = late(at, [2, 2, D], fp16)
        lps, at = late(at, [2, 2, D], fp16)
        lxT, at = late(at, [2, 2, KC, P], fp16)
        lyT, at = late(at, [2, 2, KC, P], fp16)
        ygp, at = late(at, [3, 2, 2, D])
        at = 4 * EW
        wst, at = late(at, [KC, 3 * D])
        wst2, at = late(at, [KC, D])
        wst3, at = late(at, [KC, NE])
        tb, at = late(at, [TAB, D])
        thn, at = late(at, [TAB, D])
        ths, at = late(at, [TAB, 2, D], fp16)
        txT, at = late(at, [TAB, 2, KC, P], fp16)
        u, at = late(at, [TAB, 2 * D])
        usq, at = late(at, [TAB, 2 * D])
        ssq, at = late(at, [TAB, 2 * H])
        srt, at = late(at, [TAB, 2 * H])
        sin_, at = late(at, [TAB, 2 * H])
        scr, at = late(at, [TAB, 2 * H])
        tv, at = late(at, [TAB, H, VW])
        tokx_i, at = late(at, [T], i32)
        tokf, at = late(at, [T])
        jrow, at = late(at, [T])
        tm, at = late(at, [T])
        tsp, at = late(at, [T])
        tls, at = late(at, [T])
        tva, at = late(at, [T])
        dft, at = late(at, [3, KC, D])
        fw, at = late(at, [2, KC, D])
        fa, at = late(at, [2, KC, D])
        assert at <= NE * EW, at
        at = 0
        ltri, at = view(at, [P])
        tpre, at = view(at, [P])
        tsum, at = view(at, [NE])
        iota, at = view(at, [P + MT + NE + NT])
        ioa, ioe, tokid = iota[:, P:P + MT], iota[:, P + MT:P + MT + NE], iota[:, P + MT + NE:]
        assert at <= 4 * D, at
        m0, at = view(at, [NT, NE])
        m1, at = view(at, [NT, NE])
        mc, at = view(at, [NT, NE])
        totb, at = view(at, [P])
        ohb, at = view(at, [2 * NT, P], fp16)
        oha, at = view(at, [2 * NT, MT], fp16)
        ioh, at = view(at, [P + MT + 1], fp16)
        tokh, at = view(at, [NT], fp16)
        ra, at = view(at, [2 * NT], fp16)
        rb, at = view(at, [2 * NT], fp16)
        ri, at = view(at, [2 * NT], i32)
        ri2, at = view(at, [2 * NT], i32)
        ecmp, at = view(at, [MT, NE])
        e8, at = view(at, [8, NE])
        e8i, at = view(at, [NE], i32)
        pe8, at = view(at, [NT, NE])
        p1, at = view(at, [NT, NE])
        sf, at = view(at, [NT, 2])
        rq, at = view(at, [2 * NT])
        rqm, rqs = rq[:, 0:NT], rq[:, NT:2 * NT]
        onec, at = view(at, [1])
        rq_e, at = view(at, [UN * GR + 1])
        pkf, at = view(at, [GR])
        assert at <= AW, at
        at = 0
        xs, at = view(at, [2, 2, D], fp16)
        exT, at = view(at, [2, 2, KC, P], fp16)
        g, at = view(at, [2, CH, P])
        gs, at = view(at, [2, 2, CH, P], fp16)
        y, at = view(at, [2, D])
        b2bc, at = view(at, [NE, D])
        mixr, at = view(at, [2, 1], i32)
        wst1, at = view(at, [KC, 3 * D])
        wst1o = stage[:, 1, 0:KC * D].rearrange("p (a b) -> p a b", a=KC)
        assert at <= AW, at
        sflat = stage[:].rearrange("p a b -> p (a b)")
        yg = sflat[:, 0:4 * D].rearrange("p (a b c) -> p a b c", a=2, b=2)
        mask3 = sflat[:, 6 * D:6 * D + 3 * P].rearrange("p (a b) -> p a b", a=3)

        psT = [ctx.enter_context(nc.psum_tensor(f"psT{i}", [P, 512], fp32)) for i in range(2)]
        psS = ctx.enter_context(nc.psum_tensor("psS", [P, 4, 512], fp32))
        psO = [ctx.enter_context(nc.psum_tensor(f"psO{i}", [P, 512], fp32)) for i in range(2)]
        psW = psT[1][:]
        psWh = psW.bitcast(fp16).rearrange("p (a b c) -> p a b c", a=2, b=4)
        psTb = psT[0][:].bitcast(fp16).rearrange("p (a b c) -> p a b c", a=2, b=4)
        psTf = psT[0][:].bitcast(fp16).rearrange("p (s q t) -> p s q t", s=2, q=4)
        psTh = [t[:, 0:256].bitcast(fp16).rearrange("p (a b) -> p a b", a=4) for t in psT]

        ld_x, ld_ident, ld_small = sem("ld_x"), sem("ld_ident"), sem("ld_small")
        ld_w = sem("ld_w")
        ld_tab = sem("ld_tab")
        w_hi, w_lo = sem("w_hi"), sem("w_lo")
        pos_r, posT_r, posi_r = sem("pos_r"), sem("posT_r"), sem("posi_r")
        mexp_r, ones_r = sem("mexp_r"), sem("ones_r")
        t_var, t_pow, t_split, t_T, t_xT, t_mm = (sem(n) for n in ("t_var", "t_pow", "t_split", "t_T", "t_xT", "t_mm"))
        t_u, t_v, t_sum, t_root, t_out, t_wr = (sem(n) for n in ("t_u", "t_v", "t_sum", "t_root", "t_out", "t_wr"))
        g_qk = sem("g_qk")
        g_h = sem("g_h")
        g_v = [sem("g_v0"), sem("g_v1")]
        rope_r, split_r = sem("rope_r"), sem("split_r")
        tr_r, qk_r = sem("tr_r"), sem("qk_r")
        oc_r, oT_r, ob_r = sem("oc_r"), sem("oT_r"), sem("ob_r")
        sc_r, ex_r, av_r = sem("sc_r"), sem("ex_r"), sem("av_r")
        osp_r = sem("osp_r")
        ot_r, otc_r, wo_r = sem("ot_r"), sem("otc_r"), sem("wo_r")
        var_r, pw_r, hs_r = sem("var_r"), sem("pw_r"), sem("hs_r")
        xn_w = sem("xn_w")
        ht_r, htc_r = sem("ht_r"), sem("htc_r")
        lgp_r, lgs_r = sem("lgp_r"), sem("lgs_r")
        st_ld = [sem("st_ld0"), sem("st_ld1")]
        st_hi, st_free = sem("st_hi"), sem("st_free")
        dch, pch = sem("dch"), sem("pch")
        w1_hi, w1_lo, w1_ld, l1_ld = sem("w1_hi"), sem("w1_lo"), sem("w1_ld"), sem("l1_ld")
        f_a, f_ac, f_m, f_mh, f_ml = (sem(n) for n in ("f_a", "f_ac", "f_m", "f_mh", "f_ml"))
        n_y = sem("n_y")
        n_yp = [sem(f"n_yp{i}") for i in range(3)]
        n_var, n_pow = sem("n_var"), sem("n_pow")
        n_hs, n_hT, n_hTc = sem("n_hs"), sem("n_hT"), sem("n_hTc")
        n_qkv, n_x = sem("n_qkv"), sem("n_x")
        n_exp, n_hl, n_spl = sem("n_exp"), sem("n_hl"), sem("n_spl")
        n_tr, n_qk = sem("n_tr"), sem("n_qk")
        n_sc, n_av = sem("n_sc"), sem("n_av")
        n_ms, n_mid, n_pm = sem("n_ms"), sem("n_mid"), sem("n_pm")
        n_vc, n_oc, n_oT, n_osp = sem("n_vc"), sem("n_oc"), sem("n_oT"), sem("n_osp")
        n_lT, n_lTc, n_wo = sem("n_lT"), sem("n_lTc"), sem("n_wo")
        n_var2, n_pow2, n_hs2, n_gT, n_gTc = sem("n_var2"), sem("n_pow2"), sem("n_hs2"), sem("n_gT"), sem("n_gTc")
        n_ff, n_out, n_hb, n_fb = sem("n_ff"), sem("n_out"), sem("n_hb"), sem("n_fb")
        rt_ld, rt_d, rt_e, rt_c, rt_tot, rt_totc, rt_pre, rt_oh, rt_inv, rt_idx = (
            sem(n) for n in ("rt_ld", "rt_d", "rt_e", "rt_c", "rt_tot", "rt_totc", "rt_pre", "rt_oh", "rt_inv", "rt_idx"))
        m_x = [sem("m_x0"), sem("m_x1")]
        m_T, m_Tc, m_g1, m_act, m_gs, m_g2, m_y = (sem(n) for n in ("m_T", "m_Tc", "m_g1", "m_act", "m_gs", "m_g2", "m_y"))
        m_b2, m_hi = sem("m_b2"), sem("m_hi")
        m_yw = [sem("m_yw0"), sem("m_yw1")]
        out_w = sem("out_w")
        mv_t = small[:, 0:6].rearrange("p (a b) -> p a b", b=2)
        st_t = small[:, 8:26].rearrange("p (a b) -> p a b", b=6)
        bst = [small[:, 8:14], small[:, 14:20]]
        mvq = small[:, 20:24].rearrange("p (a b) -> p a b", b=2)
        mvp = small[:, 0:4].rearrange("p (a b) -> p a b", b=2)
        rden2 = small[:, 32:48].rearrange("p (a b) -> p a b", a=2)
        block = ctx.enter_context(nc.Block())

        def split3(ps, xhl, w, n0, n1, out0=0):
            k, last = 0, 3 * KC - 1
            for c in range(KC):
                for a, b in ((0, 0), (0, 1), (1, 0)):
                    m = nc.tensor.matmul(ps[:, out0:out0 + n1 - n0], xhl[:, a, c, :], w[:, c, b, n0:n1],
                                         start=(k == 0), stop=(k == last))
                    k += 1
            return m

        def table_view(a):
            return a.rearrange("(t p) n -> p t n", p=P)

        w1_v = w1.rearrange("e (c p) n -> p e c n", p=P)
        w2_v = w2.rearrange("e (g c p) n -> p e g c n", p=P, g=2)

        @block.sync
        def _(sp):
            sp.dma_start(tokx_i[0:NB, :], x).then_inc(ld_x, 16)
            sp.dma_start(jrow[0:NB, :], c_j).then_inc(ld_x, 16)
            sp.dma_start(tb, table_view(table[0:TAB * P, :])).then_inc(ld_tab, 16)
            sp.dma_start(ident[:], c_ident).then_inc(ld_ident, 16)
            sp.dma_start(identh[:], c_identh).then_inc(ld_ident, 16)
            sp.dma_start(wst, wqkv0.rearrange("(c p) n -> p c n", p=P)).then_inc(ld_w, 16)
            sp.dma_start(wst2, wo0.rearrange("(c p) n -> p c n", p=P)).then_inc(ld_w, 16)
            sp.dma_start(wst3, wr.rearrange("(c p) n -> p c n", p=P)).then_inc(ld_w, 16)
            sp.dma_start(rope[:], c_rope).then_inc(ld_small, 16)
            sp.dma_start(bias_bc[:, 0:D], bo0.partition_broadcast(P)).then_inc(ld_small, 16)
            sp.dma_start(b1s[:], b1).then_inc(ld_small, 16)
            sp.dma_start(dft, c_dft).then_inc(f_a, 16)
            sp.dma_start(fw[:, 0, :, :], fre.rearrange("(c p) n -> p c n", p=P)).then_inc(f_a, 16)
            sp.dma_start(fw[:, 1, :, :], fim.rearrange("(c p) n -> p c n", p=P)).then_inc(f_a, 16)
            sp.wait_ge(ones_r, 1)
            for t in range(TAB):
                sp.wait_ge(t_v, t + 1)
                for i in range(2):
                    sp.dma_start(tab_v[i][t * P:(t + 1) * P, :], tv[:, t, i * H // 2:(i + 1) * H // 2, :].rearrange("p a b -> p (a b)")
                                 ).then_inc(t_wr, 16)
            for t in range(TAB):
                sp.wait_ge(t_out, t + 1)
                sp.dma_start(tab_qk[t * P:(t + 1) * P, :], u[:, t, :]).then_inc(t_wr, 16)

            def rows_out(b):
                sp.wait_ge(hs_r, b + 1)
                sp.dma_start(table_view(xn_d)[:, bass.ds(b * 2, 2), :], hsa.rearrange("p a b c -> p a (b c)")).then_inc(xn_w, 16)

            def expert_in(b):
                for q in range(4):
                    sp.wait_ge(st_free, b * 4 + q + 1)
                    if q < 2:
                        sp.dma_start(stage[:, q % 2, :], w1_v[:, bass.ds(b, 1), q, :].rearrange("p e n -> p (e n)")
                                     ).then_inc(st_ld[q % 2], 16)
                    else:
                        sp.dma_start(stage[:, q % 2, :].rearrange("p (c n) -> p c n", c=4),
                                     w2_v[:, bass.ds(b, 1), q - 2, :, :].rearrange("p e c n -> p (e c) n")
                                     ).then_inc(st_ld[q % 2], 16)

            expert_in(0)
            with sp.Fori(0, NB - 1) as bb:
                expert_in(bb + 1)
                rows_out(bb)
            sp.wait_ge(g_qk, 32 * (NB + 2))
            sp.wait_ge(rope_r, 4 * (NB + 1))
            for dst, src in ((ltri, c_ltri), (tpre, c_tpre), (tsum, c_tsum), (iota, c_iota)):
                sp.dma_start(dst, src).then_inc(rt_ld, 16)
            rows_out(NB - 1)
            sp.wait_ge(xn_w, 16 * NB)
            sp.wait_ge(lgs_r, NB)
            sp.wait_ge(st_free, 4 * NB + 2)
            for k in (0, 2):
                sp.dma_start(mask3[:, k, :], c_causal).then_inc(l1_ld, 16)
            sp.dma_start(bias_bc[:, 0:3 * D], bqkv1.partition_broadcast(P)).then_inc(l1_ld, 16)
            sp.dma_start(bias_bc[:, 3 * D:4 * D], bout1.partition_broadcast(P)).then_inc(l1_ld, 16)
            sp.dma_start(bias_bc[:, 4 * D:5 * D], fbias.partition_broadcast(P)).then_inc(l1_ld, 16)
            sp.wait_ge(m_T, 4)
            sp.dma_start(b2bc.rearrange("p a b -> p (a b)"), b2.rearrange("a b -> (a b)").partition_broadcast(P)).then_inc(m_b2, 16)
            sp.dma_start(wst1, wqkv1.rearrange("(c p) n -> p c n", p=P)).then_inc(w1_ld, 16)
            sp.dma_start(wst1o, wout1.rearrange("(c p) n -> p c n", p=P)).then_inc(w1_ld, 16)

            def y_out(j, i):
                sp.wait_ge(m_y, j + 3)
                sp.dma_start(table_view(y_d)[:, bass.ds(j, 1), :].rearrange("p t n -> p (t n)"), y[:, i, :]).then_inc(m_yw[i], 16)

            with sp.Fori(0, MT // 2) as jj:
                for i in range(2):
                    y_out(jj * 2 + i, i)
            y_out(MT - 1, 0)
            with sp.Fori(0, NB) as b:
                sp.wait_ge(n_out, b + 1)
                sp.dma_start(out.rearrange("b (s p) d -> p (b s) d", p=P)[:, bass.ds(b * 2, 2), :],
                             h[:, bass.ds(b * 2, 2), :]).then_inc(out_w, 16)
            sp.wait_ge(out_w, 16 * NB)

        @block.gpsimd
        def _(pool):
            done = [0]

            def link(ins):
                ins.then_inc(pch, 1)
                done[0] = done[0] + 1
                pool.wait_ge(pch, done[0])

            nc.gpsimd.memset(tv[:, :, :, HD:VW], 1.0).then_inc(ones_r, 1)
            nc.gpsimd.memset(epsc[:], EPS_LN)
            nc.gpsimd.memset(neg1[:], -1.0)
            nc.gpsimd.memset(mexp[:], -0.5).then_inc(mexp_r, 1)
            pool.wait_ge(mexp_r, 1)
            pool.wait_ge(t_var, 1)
            link(nc.gpsimd.tensor_scalar(small[:, 26:26 + TAB], mv_t[:, :, 1], EPS_LN, None, ALU.add))
            nc.gpsimd.tensor_tensor(small[:, 26:26 + TAB], small[:, 26:26 + TAB], mexp[:, 0:TAB], ALU.pow).then_inc(t_pow, 1)
            pool.wait_ge(posi_r, 2)

            def embeddings(t0, t1):
                for t in range(t0, t1):
                    nc.gpsimd.indirect_dma_start(h[:, t, :], None, table, bass.IndirectOffsetOnAxis(
                        ap=pos_i[:, t:t + 1], axis=0)).then_inc(g_h, 16)

            embeddings(0, NT)

            def gather_qk(b):
                link(nc.gpsimd.tensor_copy(posx[:, 0, :, 0], pos_i[:, bass.ds(b * 2, 2)]))
                for half in range(2):
                    nc.gpsimd.indirect_dma_start(qkg[:, half].rearrange("p a b c -> p (a b c)"), None, tab_qk,
                                                 bass.IndirectOffsetOnAxis(ap=posx[:, 0, half, :], axis=0)).then_inc(g_qk, 16)

            def gather_v(b, gp):
                link(nc.gpsimd.tensor_copy(posx[:, 1 + gp, :, 0], pos_i[:, bass.ds(b * 2, 2)]))
                for half in range(2):
                    nc.gpsimd.indirect_dma_start(vaug[:, gp, half].rearrange("p a b -> p (a b)"), None, tab_v[gp],
                                                 bass.IndirectOffsetOnAxis(ap=posx[:, 1 + gp, half, :], axis=0)
                                                 ).then_inc(g_v[gp], 16)

            def turn(b, pg):
                x, y = qkg[:, :, pg], rp[:, pg % 2]
                cs = rope[:, :, 0:1, :].to_broadcast([P, 2, 8, HD])
                sn = rope[:, :, 1:2, :].to_broadcast([P, 2, 8, HD])
                if pg == 0:
                    pool.wait_ge(g_qk, b * 32 + 32)
                wait(pool, split_r, b * 4 + pg - 1)
                nc.gpsimd.tensor_tensor(y, x, cs, ALU.mult)
                nc.gpsimd.tensor_tensor(rp2[:, :, :, 0:8], x[:, :, :, 8:16], sn[:, :, :, 0:8], ALU.mult)
                link(nc.gpsimd.tensor_tensor(rp2[:, :, :, 8:16], x[:, :, :, 0:8], sn[:, :, :, 8:16], ALU.mult))
                link2(nc.gpsimd.tensor_tensor(y, y, rp2, ALU.add), b * 4 + pg + 1)

            def link2(ins, count):
                ins.then_inc(rope_r, 1)
                pool.wait_ge(rope_r, count)

            def root(b):
                pool.wait_ge(var_r, b + 1)
                link(nc.gpsimd.tensor_tensor(small[:, 4:6], mvp[:, :, 1], epsc[:].to_broadcast([P, 2]), ALU.add))
                nc.gpsimd.tensor_tensor(small[:, 4:6], small[:, 4:6], mexp[:, 0:2], ALU.pow).then_inc(pw_r, 1)

            def pool_body(b, first=False):
                wait(pool, av_r, b * 8)
                gather_v(b, 1)
                turn(b + 1, 0)
                turn(b + 1, 1)
                turn(b + 1, 2)
                hb = h[:, bass.ds(b * 2, 2), :]
                nc.gpsimd.tensor_tensor(hb, hb, bias_bc[:, 0:D].unsqueeze(1).to_broadcast([P, 2, D]), ALU.add).then_inc(ob_r, 1)
                pool.wait_ge(av_r, b * 8 + 4)
                gather_v(b + 1, 0)
                if not first:
                    root(b - 1)
                turn(b + 1, 3)
                gather_qk(b + 2)

            pool.wait_ge(t_wr, 48 * TAB)
            pool.wait_ge(ld_small, 48)
            gather_qk(0)
            gather_v(0, 0)
            for pg in range(4):
                turn(0, pg)
            gather_qk(1)
            pool.wait_ge(g_h, 16 * NT)
            pool_body(0, True)
            with pool.Fori(0, NB - 1) as bb:
                pool.sem_clear(pch)
                done[0] = 0
                pool_body(bb + 1)
            pool.sem_clear(pch)
            done[0] = 0
            root(NB - 1)

            pool.wait_ge(rt_idx, 1)
            pool.wait_ge(xn_w, 16 * NB)
            pool.sem_inc(m_T, 2)

            def token_rows(j, i):
                pool.wait_ge(m_T, j + 1)
                link(nc.gpsimd.tensor_copy(mixr[:, i, :], inv_i[:, bass.ds(j, 1)]))
                nc.gpsimd.indirect_dma_start(xs[:, i, :, :].rearrange("p a b -> p (a b)"), None, xn_d,
                                             bass.IndirectOffsetOnAxis(ap=mixr[:, i, :], axis=0)).then_inc(m_x[i], 16)

            with pool.Fori(0, MT // 2) as jj:
                pool.sem_clear(pch)
                done[0] = 0
                for i in range(2):
                    token_rows(jj * 2 + i, i)
            token_rows(MT - 1, 0)

            def slot_rows(b, parts=range(4), pre=None):
                buf, ready, ix = (yg, n_y, 3) if pre is None else (ygp[:, pre], n_yp[pre], pre)
                if 0 in parts:
                    link(nc.gpsimd.tensor_copy(posy[:, ix, :, :, 0], slot_i[:, bass.ds(b * 2, 2), :]))
                for part in parts:
                    half, k = part // 2, part % 2
                    nc.gpsimd.indirect_dma_start(buf[:, k, half, :], None, y_d, bass.IndirectOffsetOnAxis(
                        ap=posy[:, ix, half, k, :], axis=0)).then_inc(ready, 16)

            def inverse_root(b, stats, root, ready, done_sem):
                pool.wait_ge(ready, b + 1)
                link(nc.gpsimd.tensor_tensor(root, stats[:, :, 1], epsc[:].to_broadcast([P, 2]), ALU.add))
                nc.gpsimd.tensor_tensor(root, root, mexp[:, 0:2], ALU.pow).then_inc(done_sem, 1)

            def add_bias(b, bias, ready, done_sem):
                pool.wait_ge(ready, b + 1)
                hb = h[:, bass.ds(b * 2, 2), :]
                nc.gpsimd.tensor_tensor(hb, hb, bias.unsqueeze(1).to_broadcast([P, 2, D]), ALU.add).then_inc(done_sem, 1)

            def mask_second(b, p):
                pool.wait_ge(n_mid, b * 8 + p + 1)
                e = lE[:, p % 2, 1, 0:3:2, :]
                nc.gpsimd.tensor_tensor(e, e, mask3[:, 0:3:2, :], ALU.mult).then_inc(n_pm, 1)

            def first_root(b):
                inverse_root(b, mvp, small[:, 4:6], n_var, n_pow)

            def pool_late(b, tail=True, group=True, prep=True, ahead=True, ahead2=True):
                mask_second(b, 1)
                if prep:
                    add_bias(b + 2, bias_bc[:, 3 * D:4 * D], n_hs, n_hb)
                mask_second(b, 2)
                mask_second(b, 3)
                mask_second(b, 4)
                if ahead:
                    first_root(b + 3)
                if tail:
                    inverse_root(b - 1, mvq, small[:, 24:26], n_var2, n_pow2)
                mask_second(b, 5)
                if ahead2:
                    slot_rows(b + 4, (0, 1))
                mask_second(b, 6)
                if tail:
                    add_bias(b - 1, bias_bc[:, 4 * D:5 * D], n_hs2, n_fb)
                mask_second(b, 7)
                if ahead2:
                    slot_rows(b + 4, (2,))
                if group:
                    mask_second(b + 1, 0)
                if ahead2:
                    slot_rows(b + 4, (3,))

            pool.wait_ge(m_yw[0], 16 * ((MT + 1) // 2) + 16)
            pool.wait_ge(m_yw[1], 16 * (MT // 2) + 16)
            pool.wait_ge(l1_ld, 80)
            slot_rows(0, pre=0)
            slot_rows(1, pre=1)
            first_root(0)
            add_bias(0, bias_bc[:, 3 * D:4 * D], n_hs, n_hb)
            first_root(1)
            slot_rows(2, pre=2)
            add_bias(1, bias_bc[:, 3 * D:4 * D], n_hs, n_hb)
            slot_rows(3)
            mask_second(0, 0)
            first_root(2)
            pool_late(0, tail=False)
            with pool.Fori(0, NB - 5) as bb:
                pool.sem_clear(pch)
                done[0] = 0
                pool_late(bb + 1)
            pool_late(NB - 4, ahead2=False)
            pool_late(NB - 3, ahead=False, ahead2=False)
            pool_late(NB - 2, prep=False, ahead=False, ahead2=False)
            pool_late(NB - 1, group=False, prep=False, ahead=False, ahead2=False)
            inverse_root(NB - 1, mvq, small[:, 24:26], n_var2, n_pow2)
            add_bias(NB - 1, bias_bc[:, 4 * D:5 * D], n_hs2, n_fb)

        @block.scalar
        def _(act):
            act.wait_ge(ld_w, 48)
            nc.scalar.activation(wA[:, :, 0, :], wst, ACT.Copy, scale=WS).then_inc(w_hi, 1)
            nc.scalar.activation(wB[:, :, 0, :], wst2, ACT.Copy, scale=WS).then_inc(w_hi, 1)
            nc.scalar.activation(wR[:, :, 0, :], wst3, ACT.Copy, scale=WS).then_inc(w_hi, 1)
            for t in range(TAB):
                act.wait_ge(t_mm, t + 1)
                nc.scalar.activation(u[:, t].rearrange("p (g a n) -> p a g n", g=4, a=2),
                                     psS[:, 2 * (t % 2), :].rearrange("p (a g n) -> p a g n", a=2, g=4),
                                     ACT.Copy, scale=1.0 / WS).then_inc(t_u, 1)
                nc.scalar.activation(tv[:, t, :, 0:HD], psS[:, 2 * (t % 2) + 1, 0:D].rearrange("p (a b) -> p a b", b=HD),
                                     ACT.Copy, scale=1.0 / WS).then_inc(t_v, 1)
            act.wait_ge(t_sum, 1)
            nc.scalar.activation(srt, ssq, ACT.Sqrt).then_inc(t_root, 1)
            act.wait_ge(f_m, 1)
            nc.scalar.activation(wM[:, :, 0, :], psS[:, 0:2, 0:D], ACT.Copy, scale=WS / D).then_inc(f_mh, 1)
            act.wait_ge(t_wr, 48 * TAB)

            def exponentials(b, p):
                act.wait_ge(sc_r, b * 8 + p + 1)
                wait(act, av_r, b * 8 + p - 1)
                nc.scalar.activation(E[:, p % 2, :, :], psS[:, 2 * (p % 2):2 * (p % 2) + 2, :], ACT.Exp,
                                     scale=HD ** -0.5).then_inc(ex_r, 1)

            def rows_from(b, pg):
                act.wait_ge(tr_r, b * 4 + pg + 1)
                qk = qkT[:, 2 * pg:2 * pg + 2].rearrange("p a b t -> p (a b) t")
                nc.scalar.activation(qk.rearrange("p q (s t) -> p s q t", s=2), psTf, ACT.Copy).then_inc(qk_r, 1)

            def sums_out(b, gp):
                act.wait_ge(av_r, b * 8 + 4 * gp + 4)
                wait(act, oT_r, b * 2 + gp)
                nc.scalar.activation(oTs, psO[gp][:], ACT.Copy).then_inc(oc_r, 1)

            def act_body(b, first=False):
                for p in range(8):
                    if p == 0 and not first:
                        sums_out(b - 1, 1)
                    if p < 7:
                        exponentials(b, p + 1)
                    else:
                        exponentials(b + 1, 0)
                    if p == 4:
                        sums_out(b, 0)
                    if p == 0:
                        if not first:
                            rows_from(b, 3)
                    elif p % 2 == 0:
                        rows_from(b + 1, p // 2 - 1)
                    else:
                        q = p // 2
                        act.wait_ge(st_ld[q % 2], b * 32 + 16 * (q // 2) + 16)
                        nc.scalar.activation(WX[:, bass.ds(b, 1), q, 0, :].rearrange("p e n -> p (e n)"),
                                             stage[:, q % 2, :], ACT.Copy, scale=WS).then_inc(st_hi, 1)

            for pg in range(4):
                rows_from(0, pg)
            exponentials(0, 0)
            act_body(0, True)
            with act.Fori(0, NB - 1) as bb:
                act_body(bb + 1)
            sums_out(NB - 1, 1)

            act.wait_ge(rt_d, 1)
            nc.scalar.activation(pe8, pe8, ACT.Exp).then_inc(rt_e, 1)
            nc.scalar.activation(rqm, rqm, ACT.Exp).then_inc(rt_e, 1)
            act.wait_ge(rt_idx, 1)

            def gelu(j, i):
                e = act.value_load(ej[0:1, bass.ds(j, 1)], min_val=0, max_val=NE - 1)
                for q in range(2):
                    act.wait_ge(m_g1, j * 2 + q + 3)
                    act.wait_ge(m_gs, j * 2 + q + 1)
                    for c in range(4 * q, 4 * q + 4):
                        last = nc.scalar.activation(g[:, i, c, :], psS[:, 2 * i + q, (c % 4) * P:(c % 4 + 1) * P],
                                                    ACT.Gelu_apprx_tanh, bias=b1s[:, bass.ds(e, 1), c], scale=1.0 / WS)
                    last.then_inc(m_act, 1)

            with act.Fori(0, MT // 2) as jj:
                for i in range(2):
                    gelu(jj * 2 + i, i)
            gelu(MT - 1, 0)
            act.wait_ge(w1_ld, 32)
            nc.scalar.activation(wA[:, :, 0, :], wst1, ACT.Copy, scale=WS).then_inc(w1_hi, 1)
            nc.scalar.activation(wB[:, :, 0, :], wst1o, ACT.Copy, scale=WS).then_inc(w1_hi, 1)
            def second_head(b, p):
                act.wait_ge(n_sc, b * 8 + p + 1)
                wait(act, n_av, b * 8 + p - 1)
                nc.scalar.activation(lE[:, p % 2, 1].rearrange("p a b -> p (a b)"), psS[:, 2 * (p % 2) + 1, 0:3 * P], ACT.Copy).then_inc(n_mid, 1)

            def late_exp(b, half):
                act.wait_ge(n_x, b * 3 + half + 1)
                nc.scalar.activation(lmn[:, half], lx[:, half], ACT.Exp, bias=neg1[:]).then_inc(n_exp, 1)

            def late_parts(b, pg):
                z = lhl[:, pg % 2]
                act.wait_ge(n_hl, b * 4 + pg + 1)
                nc.scalar.activation(z[:, :, 0, :, 2:4, :].rearrange("p a c d e -> p a c (d e)"),
                                     z[:, :, 0, :, 0:2, :].rearrange("p a c d e -> p a c (d e)"), ACT.Copy)
                nc.scalar.activation(z[:, :, 1, :, 2, :], z[:, :, 1, :, 1, :], ACT.Copy)
                nc.scalar.activation(z[:, :, 1, :, 3, :], z[:, :, 1, :, 0, :], ACT.Copy).then_inc(n_spl, 1)

            def late_rows_from(b, pg):
                act.wait_ge(n_tr, b * 4 + pg + 1)
                qk = lqkT[:, 2 * pg:2 * pg + 2].rearrange("p a b t -> p (a b) t")
                nc.scalar.activation(qk.rearrange("p q (s t) -> p s q t", s=2), psTf, ACT.Copy).then_inc(n_qk, 1)

            def late_sums_out(b, gp):
                act.wait_ge(n_av, b * 8 + 4 * gp + 4)
                wait(act, n_oT, b * 2 + gp)
                nc.scalar.activation(loTs, psO[gp][:], ACT.Copy).then_inc(n_oc, 1)

            def late_rows_back(b, ready, bank, dst, done_sem):
                act.wait_ge(ready, b + 1)
                nc.scalar.activation(dst.rearrange("p a b c d -> p (a b c d)"), bank.bitcast(fp16), ACT.Copy).then_inc(done_sem, 1)

            def values_in(b, gp):
                act.wait_ge(n_x, b * 3 + 3)
                wait(act, n_av, b * 8 - 4 + 4 * gp)
                src = lv[:, bass.ds(b, 1), :, gp * P:(gp + 1) * P].rearrange("p a s (h c) -> p (a s) h c", c=HD)
                nc.scalar.activation(lvaug[:, gp, :, :, 0:HD], src, ACT.Copy).then_inc(n_vc, 1)

            def act_late(b, tail=True, group=True, prep=True):
                for p in range(8):
                    if p == 0 and tail:
                        late_sums_out(b - 1, 1)
                        late_rows_from(b, 3)
                    if p and p % 2 == 0 and group:
                        late_rows_from(b + 1, p // 2 - 1)
                    if p == 1 and prep:
                        late_rows_back(b + 2, n_hT, psT[0][:], lxT, n_hTc)
                    if p == 7 and tail:
                        late_rows_back(b - 1, n_gT, psW, lyT, n_gTc)
                    if p < 7:
                        second_head(b, p + 1)
                    elif group:
                        second_head(b + 1, 0)
                    if p == 2 and tail:
                        late_rows_back(b - 1, n_lT, psW, lyT, n_lTc)
                    if group and p and p % 2 == 0:
                        late_parts(b + 1, p // 2)
                    if prep and p == 7:
                        late_parts(b + 2, 0)
                    if p == 0:
                        values_in(b, 1)
                    if p == 4:
                        late_sums_out(b, 0)
                    if prep and p in (3, 5):
                        late_exp(b + 2, (p - 3) // 2)
                    if group and p == 5:
                        values_in(b + 1, 0)

            late_rows_back(0, n_hT, psT[0][:], lxT, n_hTc)
            for half in range(2):
                late_exp(0, half)
            values_in(0, 0)
            late_rows_back(1, n_hT, psW, lxT, n_hTc)
            for pg in range(4):
                late_parts(0, pg)
                late_rows_from(0, pg)
            for half in range(2):
                late_exp(1, half)
            second_head(0, 0)
            late_parts(1, 0)
            act_late(0, tail=False)
            with act.Fori(0, NB - 3) as bb:
                act_late(bb + 1)
            act_late(NB - 2, prep=False)
            act_late(NB - 1, group=False, prep=False)
            late_sums_out(NB - 1, 1)
            late_rows_back(NB - 1, n_lT, psW, lyT, n_lTc)
            late_rows_back(NB - 1, n_gT, psW, lyT, n_gTc)

        @block.vector
        def _(dve):
            done = [0]

            def link(ins):
                ins.then_inc(dch, 1)
                done[0] = done[0] + 1
                dve.wait_ge(dch, done[0])

            V = nc.vector
            link(V.memset(pos_i[:], 0))
            for i in range(2):
                V.memset(psO[i][:], 0.0)
            dve.wait_ge(ld_x, 32)
            tk, tj = tokf[0:NB, :], jrow[0:NB, :]
            link(V.tensor_copy(tk, tokx_i[0:NB, :]))
            V.tensor_scalar(tm[0:NB, :], tk, 1.0, None, ALU.not_equal)
            link(V.scalar_tensor_tensor(tsp[0:NB, :], tk, 4.0, tj, ALU.is_equal, ALU.mult))
            V.tensor_tensor_scan(tva[0:NB, :], tm[0:NB, :], tm[0:NB, :], 1.0, ALU.mult, ALU.mult)
            link(V.tensor_tensor_scan(tls[0:NB, :], tsp[0:NB, :], tsp[0:NB, :], 0.0, ALU.max, ALU.max))
            link(V.tensor_tensor(tls[0:NB, :], tj, tls[0:NB, :], ALU.subtract))
            link(V.scalar_tensor_tensor(tls[0:NB, :], tls[0:NB, :], 1.0, tva[0:NB, :], ALU.add, ALU.mult))
            V.tensor_scalar(tls[0:NB, :], tls[0:NB, :], 1.0, None, ALU.add).then_inc(pos_r, 1)
            dve.wait_ge(ld_tab, 16)
            for t in range(TAB):
                last = V.bn_stats(st_t[:, t, :], tb[:, t, :])
            link(last)
            for t in range(TAB):
                last = V.bn_aggr(mv_t[:, t, :], st_t[:, t, :])
            last.then_inc(t_var, 1)
            dve.wait_ge(posT_r, 1)
            V.tensor_copy(pos_i[:, 0:NT].rearrange("p (b s) -> p s b", s=2),
                          psT[1][:, 0:NT].rearrange("p (s b) -> p s b", s=2)).then_inc(posi_r, 2)
            for w, st, n in ((wA, wst, 1), (wB, wst2, 2), (wR, wst3, 3)):
                dve.wait_ge(w_hi, n)
                V.scalar_tensor_tensor(w[:, :, 1, :], st, WS, w[:, :, 0, :], ALU.mult, ALU.subtract).then_inc(w_lo, 1)
            dve.wait_ge(t_pow, 1)
            for t in range(TAB):
                last = V.tensor_scalar(thn[:, t], tb[:, t, :], mv_t[:, t, 0:1], small[:, 26 + t:27 + t], ALU.subtract, ALU.mult)
            link(last)
            link(V.tensor_copy(ths[:, :, 0, :], thn))
            V.tensor_tensor(ths[:, :, 1, :], thn, ths[:, :, 0, :], ALU.subtract).then_inc(t_split, 1)
            dve.wait_ge(t_T, 1)
            V.tensor_copy(txT[:, 0:2].rearrange("p t a b c -> p (t a b c)"), psT[0][:].bitcast(fp16)).then_inc(t_xT, 1)
            dve.wait_ge(t_T, 2)
            V.tensor_copy(txT[:, 2].rearrange("p a b c -> p (a b) c"), psTh[1]).then_inc(t_xT, 1)
            for t in range(TAB):
                dve.wait_ge(t_u, t + 1)
                link(V.tensor_tensor(usq[:, t], u[:, t], u[:, t], ALU.mult))
                last = V.tensor_reduce(ssq[:, t], usq[:, t].rearrange("p (a b) -> p a b", b=HD), AX.X, ALU.add)
            link(last)
            V.tensor_scalar(ssq, ssq, EPS_QK, None, ALU.add).then_inc(t_sum, 1)
            dve.wait_ge(t_root, 1)
            link(V.reciprocal(sin_, srt))
            link(V.tensor_tensor(scr, sin_, sin_, ALU.mult))
            link(V.tensor_tensor(scr, scr, ssq, ALU.mult))
            link(V.tensor_scalar(scr, scr, -0.5, 1.5, ALU.mult, ALU.add))
            link(V.tensor_tensor(sin_, sin_, scr, ALU.mult))
            for t in range(TAB):
                V.tensor_tensor(u[:, t].rearrange("p (a b) -> p a b", b=HD), u[:, t].rearrange("p (a b) -> p a b", b=HD),
                                sin_[:, t].unsqueeze(2).to_broadcast([P, 2 * H, HD]), ALU.mult).then_inc(t_out, 1)
            dve.wait_ge(f_ac, 1)
            V.tensor_copy(fa.rearrange("p a b c -> p (a b) c"), psS[:, :, 0:D]).then_inc(f_ac, 1)
            dve.wait_ge(f_mh, 1)
            V.scalar_tensor_tensor(wM[:, :, 1, :], psS[:, 0:2, 0:D], WS / D, wM[:, :, 0, :], ALU.mult, ALU.subtract).then_inc(f_ml, 1)
            dve.wait_ge(t_wr, 48 * TAB)
            V.memset(small[:, 0:1], 0.0).then_inc(st_free, 2)

            def split_group(b, pg):
                y, z = rp[:, pg % 2].rearrange("p a b c -> p (a b) c"), hl[:, pg % 2]
                zv = z.rearrange("p a b c d e -> p (a b c) d e")
                dve.wait_ge(rope_r, b * 4 + pg + 1)
                wait(dve, tr_r, b * 4 + pg - 1)
                link(V.tensor_copy(zv[:, :, 0, :], y))
                link(V.tensor_tensor(zv[:, :, 1, :], y, zv[:, :, 0, :], ALU.subtract))
                V.tensor_copy(z[:, :, 0, :, 2:4, :].rearrange("p a c d e -> p a c (d e)"),
                              z[:, :, 0, :, 0:2, :].rearrange("p a c d e -> p a c (d e)"))
                V.tensor_copy(z[:, :, 1, :, 2, :], z[:, :, 1, :, 1, :])
                V.tensor_copy(z[:, :, 1, :, 3, :], z[:, :, 1, :, 0, :]).then_inc(split_r, 1)

            def head_outputs(b, gp):
                dve.wait_ge(oT_r, b * 2 + gp + 1)
                av = psW.rearrange("p (t h c) -> p t h c", t=2, c=32)
                link(V.reciprocal(rden2, av[:, :, :, HD]))
                link(V.tensor_tensor(o.rearrange("p t (h c) -> p t h c", c=HD), av[:, :, :, 0:HD],
                                     rden2.unsqueeze(3).to_broadcast([P, 2, 8, HD]), ALU.mult))
                hi = osp[:, :, 0, gp * P:(gp + 1) * P]
                link(V.tensor_copy(hi, o))
                V.tensor_tensor(osp[:, :, 1, gp * P:(gp + 1) * P], o, hi, ALU.subtract).then_inc(osp_r, 1)

            def rows_back(sem_in, sem_out, b):
                dve.wait_ge(sem_in, b + 1)
                V.tensor_copy(xTa.rearrange("p a b c d -> p (a b c d)"), psW.bitcast(fp16)).then_inc(sem_out, 1)

            def residual(b):
                hb = h[:, bass.ds(b * 2, 2), :]
                dve.wait_ge(wo_r, b + 1)
                dve.wait_ge(ob_r, b + 1)
                link(V.scalar_tensor_tensor(hb, psW.rearrange("p (a b) -> p a b", a=2), 1.0 / WS, hb, ALU.mult, ALU.add))
                for half in range(2):
                    last = V.bn_stats(bst[half], h[:, bass.ds(b * 2 + half, 1), :].rearrange("p a b -> p (a b)"))
                link(last)
                for half in range(2):
                    last = V.bn_aggr(mvp[:, half, :], bst[half])
                last.then_inc(var_r, 1)

            def normalise(b):
                dve.wait_ge(pw_r, b + 1)
                for half in range(2):
                    last = V.tensor_scalar(hn2[:, half, :], h[:, bass.ds(b * 2 + half, 1), :].rearrange("p a b -> p (a b)"),
                                           mvp[:, half, 0:1], small[:, 4 + half:5 + half], ALU.subtract, ALU.mult)
                link(last)
                wait(dve, xn_w, b * 16)
                link(V.tensor_copy(hsa[:, :, 0, :], hn2))
                V.tensor_tensor(hsa[:, :, 1, :], hn2, hsa[:, :, 0, :], ALU.subtract).then_inc(hs_r, 1)

            def top2(b):
                dve.wait_ge(lgp_r, b + 1)
                link(V.tensor_scalar(lg[:], psW.rearrange("p (a b) -> p a b", a=2)[:, :, 0:NE], 1.0 / WS, None, ALU.mult))
                V.max(mx8[:, 0, :], lg[:, 0, :])
                link(V.max(mx8[:, 1, :], lg[:, 1, :]))
                V.max_index(ix8[:, 0, :], mx8[:, 0, :], lg[:, 0, :])
                link(V.max_index(ix8[:, 1, :], mx8[:, 1, :], lg[:, 1, :]))
                V.tensor_copy(lgt[:, bass.ds(b * 2, 2), :], lg[:])
                V.tensor_copy(mxt[:, bass.ds(b * 2, 2), :], mx8[:, :, 0:2])
                V.tensor_copy(ixt[:, bass.ds(b * 2, 2), :], ix8[:, :, 0:2]).then_inc(lgs_r, 1)
                dve.wait_ge(lgs_r, b + 1)

            def stage_low(b, q):
                dve.wait_ge(st_hi, b * 4 + q + 1)
                hi = WX[:, bass.ds(b, 1), q, 0, :].rearrange("p e n -> p (e n)")
                lo = WX[:, bass.ds(b, 1), q, 1, :].rearrange("p e n -> p (e n)")
                V.scalar_tensor_tensor(lo, stage[:, q % 2, :], WS, hi, ALU.mult, ALU.subtract).then_inc(st_free, 1)

            def dve_body(b, first=False):
                split_group(b + 1, 0)
                if not first:
                    head_outputs(b - 1, 1)
                split_group(b + 1, 1)
                if not first:
                    rows_back(ot_r, otc_r, b - 1)
                split_group(b + 1, 2)
                stage_low(b, 0)
                if not first:
                    residual(b - 1)
                stage_low(b, 1)
                if not first:
                    normalise(b - 1)
                head_outputs(b, 0)
                split_group(b + 1, 3)
                stage_low(b, 2)
                if not first:
                    rows_back(ht_r, htc_r, b - 1)
                if not first:
                    top2(b - 1)
                stage_low(b, 3)

            for pg in range(4):
                split_group(0, pg)
            dve_body(0, True)
            with dve.Fori(0, NB - 1) as bb:
                dve.sem_clear(dch)
                done[0] = 0
                dve_body(bb + 1)
            dve.sem_clear(dch)
            done[0] = 0
            head_outputs(NB - 1, 1)
            rows_back(ot_r, otc_r, NB - 1)
            residual(NB - 1)
            normalise(NB - 1)
            rows_back(ht_r, htc_r, NB - 1)
            top2(NB - 1)

            dve.wait_ge(rt_ld, 64)
            dve.wait_ge(tr_r, 4 * (NB + 1))
            dve.wait_ge(qk_r, 4 * (NB + 1) - 1)
            dve.wait_ge(ex_r, 8 * NB + 1)
            dve.wait_ge(g_v[0], 32 * (NB + 1))
            mx0 = mxt[:, :, 0]
            V.memset(onec, 1.0)
            V.memset(rq_e, 0.0)
            V.tensor_copy(ioh[:, 0:P + MT], iota[:, 0:P + MT])
            V.tensor_copy(tokh, tokid)
            V.memset(e8[:, 3, :], 0.0)
            V.memset(slot_i[:], 0)
            V.tensor_tensor(m0, ioe.unsqueeze(1).to_broadcast([P, NT, NE]), ixt[:, :, 0:1].to_broadcast([P, NT, NE]), ALU.is_equal)
            link(V.tensor_tensor(m1, ioe.unsqueeze(1).to_broadcast([P, NT, NE]), ixt[:, :, 1:2].to_broadcast([P, NT, NE]), ALU.is_equal))
            V.tensor_tensor(mc, m0, m1, ALU.add).then_inc(rt_c, 1)
            V.tensor_tensor(rqm, mxt[:, :, 1], mx0, ALU.subtract)
            V.tensor_tensor(pe8, lgt[:], mxt[:, :, 0:1].to_broadcast([P, NT, NE]), ALU.subtract).then_inc(rt_d, 1)
            dve.wait_ge(rt_tot, 1)
            V.tensor_copy(totb, psO[0][:, 0:1].to_broadcast([P, P])).then_inc(rt_totc, 1)
            dve.wait_ge(rt_e, 2)
            link(V.tensor_reduce(rqs, pe8, AX.X, ALU.add))
            link(V.reciprocal(gate[:, :, 0], rqs))
            V.tensor_tensor(gate[:, :, 1], gate[:, :, 0], rqm, ALU.mult)
            dve.wait_ge(rt_pre, 1)
            link(V.tensor_scalar(e8i, psT[0][:, 0:NE], float(P - 1), None, ALU.add))
            link(V.tensor_scalar(e8i, e8i, 7, None, ALU.logical_shift_right))
            link(V.tensor_copy(e8[:, 1, :], e8i))
            link(V.tensor_tensor_scan(e8[:, 2, :], e8[:, 1, :], e8[:, 3, :], 0.0, ALU.add, ALU.add))
            link(V.tensor_tensor(e8[:, 4, :], e8[:, 2, :], e8[:, 1, :], ALU.subtract))
            link(V.tensor_scalar(e8[:, 5, :], e8[:, 4, :], float(P), None, ALU.mult))
            link(V.tensor_tensor(p1, psO[1][:, 0:P].rearrange("p (a b) -> p a b", b=NE),
                                 e8[:, 5:6, :].to_broadcast([P, NT, NE]), ALU.add))
            V.tensor_tensor(m0, m0, p1, ALU.mult)
            link(V.tensor_tensor(m1, m1, p1, ALU.mult))
            V.tensor_reduce(sf[:, :, 0], m0, AX.X, ALU.add)
            link(V.tensor_reduce(sf[:, :, 1], m1, AX.X, ALU.add))
            link(V.tensor_copy(slot_i[:, 0:NT, :], sf))
            si = slot_i[:, 0:NT, :].rearrange("p a b -> p (a b)")
            V.tensor_scalar(ri, si, 7, None, ALU.logical_shift_right)
            link(V.tensor_scalar(ri2, si, P - 1, None, ALU.bitwise_and))
            V.tensor_copy(ra, ri)
            link(V.tensor_copy(rb, ri2))
            V.tensor_tensor(ohb, ioh[:, 0:P].unsqueeze(1).to_broadcast([P, 2 * NT, P]), rb.unsqueeze(2).to_broadcast([P, 2 * NT, P]), ALU.is_equal)
            link(V.tensor_tensor(oha, ioh[:, P:P + MT].unsqueeze(1).to_broadcast([P, 2 * NT, MT]), ra.unsqueeze(2).to_broadcast([P, 2 * NT, MT]), ALU.is_equal))
            oh2 = oha.rearrange("p (a b) c -> p a (b c)", b=2)
            V.tensor_tensor(oh2, oh2, tokh.unsqueeze(2).to_broadcast([P, NT, 2 * MT]), ALU.mult).then_inc(rt_oh, 1)
            link(V.tensor_tensor(ecmp[0:1], ioa[0:1].unsqueeze(2).to_broadcast([1, MT, NE]),
                                 e8[0:1, 2:3, :].to_broadcast([1, MT, NE]), ALU.is_ge))
            link(V.tensor_reduce(rq_e[0:1, 0:MT], ecmp[0:1], AX.X, ALU.add))
            link(V.tensor_scalar(rq_e[0:1, 0:MT], rq_e[0:1, 0:MT], float(NE - 1), None, ALU.min))
            V.tensor_copy(ej[:], rq_e[0:1, 0:MT])
            last = rq_e[0:1, 0:UN * GR:UN]
            for k in range(1, UN + 1):
                dst = pkf[0:1] if k < UN else epk[:]
                link(V.scalar_tensor_tensor(dst, rq_e[0:1, k:k + UN * (GR - 1) + 1:UN], float(NE ** k), last, ALU.mult, ALU.add))
                last = pkf[0:1]
            dve.wait_ge(rt_inv, 1)
            V.tensor_copy(inv_i[:], psT[1][:, 0:MT]).then_inc(rt_idx, 1)
            dve.sem_inc(m_y, 2)
            dve.sem_inc(m_yw[0], 16)
            dve.sem_inc(m_yw[1], 16)
            dve.sem_inc(m_gs, 4)

            def rows_in(j, i):
                dve.wait_ge(m_T, j + 3)
                V.tensor_copy(exT[:, i, :, :, :].rearrange("p a b c -> p (a b) c"), psTh[i]).then_inc(m_Tc, 1)

            def split_hidden(j, i):
                for q in range(2):
                    c = slice(4 * q, 4 * q + 4)
                    dve.wait_ge(m_act, j * 2 + q + 1)
                    dve.wait_ge(m_g2, j + 1)
                    V.tensor_copy(gs[:, i, 0, c, :], g[:, i, c, :]).then_inc(m_hi, 1)
                    dve.wait_ge(m_hi, j * 2 + q + 1)
                    V.tensor_tensor(gs[:, i, 1, c, :], g[:, i, c, :], gs[:, i, 0, c, :], ALU.subtract).then_inc(m_gs, 1)

            def y_in(j, i):
                e = dve.value_load(ej[0:1, bass.ds(j, 1)], min_val=0, max_val=NE - 1)
                dve.wait_ge(m_g2, j + 3)
                V.scalar_tensor_tensor(y[:, i, :], psO[i][:, 0:D], 1.0 / WS, b2bc[:, bass.ds(e, 1), :].rearrange("p a b -> p (a b)"),
                                       ALU.mult, ALU.add).then_inc(m_y, 1)

            rows_in(0, 0)
            rows_in(1, 1)
            split_hidden(0, 0)
            dve.wait_ge(m_b2, 16)
            with dve.Fori(0, MT // 2 - 1) as jj:
                for i in (1, 0):
                    j = jj * 2 + (1 if i else 2)
                    rows_in(j + 1, 1 - i)
                    split_hidden(j, i)
                    dve.wait_ge(m_yw[1 - i], jj * 16 + 16)
                    y_in(j - 1, 1 - i)
            for j in (MT - 2, MT - 1):
                i = j % 2
                if j + 1 < MT:
                    rows_in(j + 1, 1 - i)
                split_hidden(j, i)
                dve.wait_ge(m_yw[1 - i], 16 * ((j - 1) // 2) + 16)
                y_in(j - 1, 1 - i)
            dve.wait_ge(m_yw[0], 16 * ((MT - 1) // 2) + 16)
            y_in(MT - 1, 0)
            for w, st, n in ((wA, wst1, 1), (wB, wst1o, 2)):
                dve.wait_ge(w1_hi, n)
                V.scalar_tensor_tensor(w[:, :, 1, :], st, WS, w[:, :, 0, :], ALU.mult, ALU.subtract).then_inc(w1_lo, 1)

            dve.wait_ge(l1_ld, 80)
            V.memset(mask3[:, 1, :], 1.0)
            V.tensor_scalar(bias_bc[:, 0:2 * D], bias_bc[:, 0:2 * D], 1.0, None, ALU.add)
            link(V.memset(lvaug[:, :, :, :, HD:VW], 1.0))
            for i in range(2):
                V.memset(psO[i][:], 0.0)

            def seq(b):
                return h[:, bass.ds(b * 2, 2), :]

            def row(b, half):
                return h[:, bass.ds(b * 2 + half, 1), :].rearrange("p a b -> p (a b)")

            def statistics(b, stats, ready):
                for half in range(2):
                    last = V.bn_stats(bst[half], row(b, half))
                link(last)
                for half in range(2):
                    last = V.bn_aggr(stats[:, half, :], bst[half])
                last.then_inc(ready, 1)

            def combine(b, pre=None, slots=(0, 1)):
                if pre is None:
                    buf = yg
                    dve.wait_ge(n_y, b * 64 - 128)
                else:
                    buf = ygp[:, pre]
                    dve.wait_ge(n_yp[pre], 64)
                for k in slots:
                    for half in range(2):
                        gt = gate[:, bass.ds(b * 2 + half, 1), :].rearrange("p a b -> p (a b)")
                        last = V.scalar_tensor_tensor(row(b, half), buf[:, k, half, :], gt[:, k:k + 1], row(b, half), ALU.mult, ALU.add)
                    link(last)
                if 1 in slots:
                    statistics(b, mvp, n_var)

            def late_normalise(b, stats, root, powered, rows, ready):
                dve.wait_ge(powered, b + 1)
                for half in range(2):
                    last = V.tensor_scalar(lhn[:, half, :], row(b, half), stats[:, half, 0:1], small[:, root + half:root + half + 1],
                                           ALU.subtract, ALU.mult)
                link(last)
                link(V.tensor_copy(rows[:, :, 0, :], lhn))
                V.tensor_tensor(rows[:, :, 1, :], lhn, rows[:, :, 0, :], ALU.subtract).then_inc(ready, 1)

            def prep_rows(b):
                late_normalise(b, mvp, 4, n_pow, lps, n_hs)

            def tail_rows(b):
                late_normalise(b, mvq, 24, n_pow2, lhs, n_hs2)

            def q_and_k(b, half, bank=psT[0][:]):
                dve.wait_ge(n_qkv, b * 3 + half + 1)
                V.scalar_tensor_tensor(lx[:, half], bank, 1.0 / WS, bias_bc[:, 0:2 * D], ALU.mult, ALU.add).then_inc(n_x, 1)

            def values(b, bank=psT[0][:]):
                dve.wait_ge(n_qkv, b * 3 + 3)
                V.scalar_tensor_tensor(lv[:, bass.ds(b, 1), :, :].rearrange("p a s n -> p (a s) n"),
                                       bank.rearrange("p (s n) -> p s n", s=2),
                                       1.0 / WS, bias_bc[:, 2 * D:3 * D].unsqueeze(1).to_broadcast([P, 2, D]),
                                       ALU.mult, ALU.add).then_inc(n_x, 1)

            def elu1(b, half):
                dve.wait_ge(n_exp, b * 2 + half + 1)
                return V.scalar_tensor_tensor(lr[:, half].rearrange("p a b c -> p (a b c)"), lmn[:, half], 1.0, lx[:, half],
                                              ALU.min, ALU.max)

            def late_split(b, pg):
                z = lhl[:, pg % 2].rearrange("p a b c d e -> p (a b) c d e")
                y = lr[:, :, :, 4 * pg:4 * pg + 4, :].rearrange("p a b c e -> p (a b) c e")
                wait(dve, n_tr, b * 4 + pg - 1)
                link(V.tensor_copy(z[:, :, :, 0, :], y))
                V.tensor_tensor(z[:, :, :, 1, :], y, z[:, :, :, 0, :], ALU.subtract).then_inc(n_hl, 1)

            def first_head(b, p):
                dve.wait_ge(n_sc, b * 8 + p + 1)
                wait(dve, n_av, b * 8 + p - 1)
                V.tensor_tensor(lE[:, p % 2, 0], psS[:, 2 * (p % 2), 0:3 * P].rearrange("p (a b) -> p a b", b=P),
                                mask3, ALU.mult).then_inc(n_ms, 1)

            def late_heads(b, gp):
                dve.wait_ge(n_oT, b * 2 + gp + 1)
                av = psW.rearrange("p (t h c) -> p t h c", t=2, c=32)
                link(V.tensor_scalar(rden2, av[:, :, :, HD], EPS_L1, None, ALU.add))
                link(V.reciprocal(rden2, rden2))
                link(V.tensor_tensor(lo.rearrange("p t (h c) -> p t h c", c=HD), av[:, :, :, 0:HD],
                                     rden2.unsqueeze(3).to_broadcast([P, 2, 8, HD]), ALU.mult))
                hi = losp[:, :, 0, gp * P:(gp + 1) * P]
                link(V.tensor_copy(hi, lo))
                V.tensor_tensor(losp[:, :, 1, gp * P:(gp + 1) * P], lo, hi, ALU.subtract).then_inc(n_osp, 1)

            def late_residual(b):
                dve.wait_ge(n_wo, b + 1)
                dve.wait_ge(n_hb, b + 1)
                link(V.scalar_tensor_tensor(seq(b), psW.rearrange("p (a b) -> p a b", a=2), 1.0 / WS, seq(b), ALU.mult, ALU.add))
                statistics(b, mvq, n_var2)

            def result(b):
                dve.wait_ge(n_ff, b + 1)
                dve.wait_ge(n_fb, b + 1)
                V.scalar_tensor_tensor(seq(b), psW.rearrange("p (a b) -> p a b", a=2), 1.0 / WS, seq(b), ALU.mult, ALU.add).then_inc(n_out, 1)

            def dve_late(b, tail=True, group=True, prep=True, ahead=True):
                first_head(b, 1)
                if tail:
                    late_heads(b - 1, 1)
                first_head(b, 2)
                if group:
                    late_split(b + 1, 1)
                first_head(b, 3)
                if ahead:
                    combine(b + 3, slots=(0,))
                if prep:
                    q_and_k(b + 2, 0)
                if ahead:
                    combine(b + 3, slots=(1,))
                first_head(b, 4)
                if group:
                    late_split(b + 1, 2)
                if tail:
                    late_residual(b - 1)
                if ahead:
                    prep_rows(b + 3)
                first_head(b, 5)
                if prep:
                    q_and_k(b + 2, 1)
                first_head(b, 6)
                if group:
                    late_split(b + 1, 3)
                if tail:
                    tail_rows(b - 1)
                late_heads(b, 0)
                first_head(b, 7)
                if prep:
                    values(b + 2)
                if group:
                    first_head(b + 1, 0)
                if prep:
                    dve.wait_ge(n_hl, b * 4 + 8)
                    elu1(b + 2, 0)
                    link(elu1(b + 2, 1))
                    late_split(b + 2, 0)
                if tail:
                    result(b - 1)

            def elu_both(b):
                elu1(b, 0)
                link(elu1(b, 1))

            combine(0, 0)
            prep_rows(0)
            combine(1, 1)
            q_and_k(0, 0, psS[:, 0, :])
            q_and_k(0, 1, psS[:, 1, :])
            prep_rows(1)
            elu_both(0)
            values(0, psS[:, 2, :])
            late_split(0, 0)
            late_split(0, 1)
            late_split(0, 2)
            late_split(0, 3)
            q_and_k(1, 0, psS[:, 3, :])
            q_and_k(1, 1, psS[:, 0, :])
            values(1, psS[:, 1, :])
            combine(2, 2)
            first_head(0, 0)
            elu_both(1)
            late_split(1, 0)
            prep_rows(2)
            dve_late(0, tail=False)
            with dve.Fori(0, NB - 4) as bb:
                dve.sem_clear(dch)
                done[0] = 0
                dve_late(bb + 1)
            dve_late(NB - 3, ahead=False)
            dve_late(NB - 2, prep=False, ahead=False)
            dve_late(NB - 1, group=False, prep=False, ahead=False)
            late_heads(NB - 1, 1)
            late_residual(NB - 1)
            tail_rows(NB - 1)
            result(NB - 1)

        @block.tensor
        def _(pe):
            M, TR = nc.tensor.matmul, nc.tensor.transpose

            def transpose_rows(ps, rows):
                for a in range(2):
                    for c in range(KC):
                        last = TR(ps[:, a * KC + c, :], rows[:, a, c * P:(c + 1) * P], identh[:])
                return last

            pe.wait_ge(ld_ident, 32)
            pe.wait_ge(pos_r, 1)
            for sq in range(2):
                last = TR(psT[1][:, sq * NB:(sq + 1) * NB], tls[0:NB, sq * P:(sq + 1) * P], ident[0:NB, 0:NB])
            last.then_inc(posT_r, 1)
            pe.wait_ge(w_lo, 3)
            pe.wait_ge(t_split, 1)
            pe.wait_ge(posi_r, 2)
            for t in range(2):
                last = transpose_rows(psTf[:, t], ths[:, t])
            last.then_inc(t_T, 1)
            transpose_rows(psTh[1], ths[:, 2]).then_inc(t_T, 1)
            for t in range(TAB):
                pe.wait_ge(t_xT, 1 + t // 2)
                wait(pe, t_v, t - 1)
                split3(psS[:, 2 * (t % 2), :], txT[:, t], wA, 0, 2 * D)
                split3(psS[:, 2 * (t % 2) + 1, :], txT[:, t], wA, 2 * D, 3 * D).then_inc(t_mm, 1)
            pe.wait_ge(f_a, 48)
            pe.wait_ge(t_v, TAB)
            for part in range(2):
                for m in range(KC):
                    for k in range(KC):
                        for w in range(2):
                            tab = ((0, 1), (1, 2))[part][w]
                            last = M(psS[:, part * KC + m, 0:D], fw[:, w, k, m * P:(m + 1) * P], dft[:, tab, k, :],
                                     start=(k == 0 and w == 0), stop=(k == KC - 1 and w == 1))
            last.then_inc(f_ac, 1)
            pe.wait_ge(f_ac, 2)
            for m in range(KC):
                for n in range(KC):
                    for part in range(2):
                        last = M(psS[:, m, 0:D], fa[:, part, n, m * P:(m + 1) * P], dft[:, part, n, :],
                                 start=(n == 0 and part == 0), stop=(n == KC - 1 and part == 1))
            last.then_inc(f_m, 1)

            def group_T(b, pg):
                pe.wait_ge(split_r, b * 4 + pg + 1)
                wait(pe, qk_r, b * 4 + pg)
                for half in range(2):
                    for a in range(2):
                        for qk in range(2):
                            last = TR(psTf[:, half, 2 * a + qk, :],
                                      hl[:, pg % 2, half, qk, 2 * a:2 * a + 2].rearrange("p a b c -> p (a b c)"), identh[:])
                last.then_inc(tr_r, 1)

            def scores(b, p):
                pe.wait_ge(qk_r, b * 4 + p // 2 + 1)
                if isinstance(b, int) and b == 0 and p < 2:
                    pe.wait_ge(f_ml, 1)
                wait(pe, ex_r, b * 8 + p - 1)
                for e in range(2):
                    rows = slice(64 * e, 64 * e + 64)
                    for st in range(2):
                        last = M(psS[:, 2 * (p % 2) + e, st * T:(st + 1) * T],
                                 qkT[rows, p, 1, st * P:(st + 1) * P], qkT[rows, p, 0, :], start=True, stop=True)
                last.then_inc(sc_r, 1)

            def weighted(b, p):
                gp = p // 4
                pe.wait_ge(ex_r, b * 8 + p + 1)
                if p % 4 == 0:
                    pe.wait_ge(g_v[gp], b * 32 + 32)
                    wait(pe, oc_r, b * 2 + gp - 1)
                for e in range(2):
                    hd = 2 * (p % 4) + e
                    for st in range(2):
                        last = M(psO[gp][32 * (hd % 4):32 * (hd % 4) + VW, (hd // 4) * T:(hd // 4 + 1) * T],
                                 vaug[:, gp, st, hd, :], E[:, p % 2, e, st * T:(st + 1) * T], start=(st == 0), stop=(st == 1))
                last.then_inc(av_r, 1)

            def sums_T(b, gp):
                pe.wait_ge(oc_r, b * 2 + gp + 1)
                if gp:
                    wait(pe, lgs_r, b)
                    pe.wait_ge(osp_r, b * 2 + 1)
                else:
                    wait(pe, var_r, b)
                for tt in range(2):
                    for st in range(2):
                        last = TR(psW[:, (2 * tt + st) * P:(2 * tt + st + 1) * P], oTs[:, st * T + tt * P:st * T + (tt + 1) * P], ident[:])
                last.then_inc(oT_r, 1)

            def out_T(b):
                pe.wait_ge(osp_r, b * 2 + 2)
                for half in range(2):
                    last = transpose_rows(psWh[:, half], osp[:, half, :, :])
                last.then_inc(ot_r, 1)

            def project(b):
                pe.wait_ge(otc_r, b + 1)
                for half in range(2):
                    last = split3(psW[:, half * D:], xTa[:, half], wB, 0, D)
                last.then_inc(wo_r, 1)

            def norm_T(b):
                pe.wait_ge(hs_r, b + 1)
                for half in range(2):
                    last = transpose_rows(psWh[:, half], hsa[:, half, :, :])
                last.then_inc(ht_r, 1)

            def route(b):
                pe.wait_ge(htc_r, b + 1)
                for half in range(2):
                    last = split3(psW[:, half * D:], xTa[:, half], wR, 0, NE)
                last.then_inc(lgp_r, 1)

            def pe_body(b, first=False):
                for p in range(8):
                    if p < 7:
                        scores(b, p + 1)
                    else:
                        scores(b + 1, 0)
                    weighted(b, p)
                    if p % 2:
                        group_T(b + 1, p // 2)
                    if not first:
                        if p == 0:
                            sums_T(b - 1, 1)
                        if p == 1:
                            out_T(b - 1)
                        if p == 3:
                            project(b - 1)
                        if p == 6:
                            pe.wait_ge(osp_r, b * 2 + 1)
                            norm_T(b - 1)
                        if p == 7:
                            route(b - 1)
                    if p == 5:
                        sums_T(b, 0)

            for pg in range(4):
                group_T(0, pg)
            scores(0, 0)
            pe_body(0, True)
            with pe.Fori(0, NB - 1) as bb:
                pe_body(bb + 1)
            sums_T(NB - 1, 1)
            out_T(NB - 1)
            project(NB - 1)
            norm_T(NB - 1)
            route(NB - 1)

            pe.wait_ge(rt_c, 1)
            M(psO[0][:, 0:1], mc.rearrange("p a b -> p (a b)"), onec, start=True, stop=True).then_inc(rt_tot, 1)
            pe.wait_ge(rt_totc, 1)
            M(psO[1][:, 0:P], totb, tpre, start=True, stop=False)
            M(psO[1][:, 0:P], ltri, mc.rearrange("p a b -> p (a b)"), start=False, stop=True)
            M(psT[0][:, 0:NE], totb, tsum, start=True, stop=True).then_inc(rt_pre, 1)
            pe.wait_ge(rt_oh, 1)
            for k in range(2 * NT):
                last = M(psT[1][:, 0:MT], ohb[:, k, :], oha[:, k, :], start=(k == 0), stop=(k == 2 * NT - 1))
            last.then_inc(rt_inv, 1)
            pe.wait_ge(rt_idx, 1)
            pe.sem_inc(m_g1, 2)
            pe.sem_inc(m_g2, 2)

            def experts(g):
                w = pe.value_load(epk[0:1, bass.ds(g, 1)], min_val=0, max_val=NE ** (UN + 1) - 1)
                return [(w >> (3 * k)) & (NE - 1) for k in range(UN + 1)]

            def rows_T(j, i, n):
                pe.wait_ge(m_x[i], n * 16 + 16)
                transpose_rows(psTh[i], xs[:, i, :, :]).then_inc(m_T, 1)

            def hidden(j, i, e):
                pe.wait_ge(m_Tc, j + 1)
                for q in range(2):
                    pe.wait_ge(m_gs, j * 2 + q + 1)
                    for c in range(4 * q, 4 * q + 4):
                        k = 0
                        for kc in range(KC):
                            for wp, xp in ((0, 0), (0, 1), (1, 0)):
                                w = WX[:, bass.ds(e, 1), kc, wp, c * P:(c + 1) * P].rearrange("p a b -> p (a b)")
                                last = M(psS[:, 2 * i + q, (c % 4) * P:(c % 4 + 1) * P], w, exT[:, i, xp, kc, :],
                                         start=(k == 0), stop=(k == 5))
                                k += 1
                    last.then_inc(m_g1, 1)

            def outputs(j, i, e):
                k = 0
                for c in range(CH):
                    if c % 4 == 0:
                        pe.wait_ge(m_gs, j * 2 + c // 4 + 5)
                    if c == 0:
                        pe.wait_ge(m_y, j + 1)
                    for xp, wp in ((0, 0), (0, 1), (1, 0)):
                        w = WX[:, bass.ds(e, 1), 2 + c // 4, wp, (c % 4) * D:(c % 4 + 1) * D].rearrange("p a b -> p (a b)")
                        last = M(psO[i][:, 0:D], gs[:, i, xp, c, :], w, start=(k == 0), stop=(k == 3 * CH - 1))
                        k += 1
                last.then_inc(m_g2, 1)

            rows_T(0, 0, 0)
            rows_T(1, 1, 0)
            hidden(0, 0, experts(0)[0])
            steps = (MT - 2) // UN
            with pe.Fori(0, steps) as jj:
                e = experts(jj)
                for k in range(UN):
                    j = jj * UN + k
                    hidden(j + 1, (k + 1) % 2, e[k + 1])
                    rows_T(j + 2, k % 2, jj * (UN // 2) + (k + 2) // 2)
                    outputs(j, k % 2, e[k])
            e = experts(steps)
            for j in range(steps * UN, MT):
                if j + 1 < MT:
                    hidden(j + 1, (j + 1) % 2, e[j + 1 - steps * UN])
                if j + 2 < MT:
                    rows_T(j + 2, j % 2, (j + 2) // 2)
                outputs(j, j % 2, e[j - steps * UN])

            pe.wait_ge(m_y, MT + 2)
            pe.wait_ge(w1_lo, 2)

            def late_norm_T(b, free, count, bank=psTb):
                pe.wait_ge(n_hs, b + 1)
                wait(pe, free, count)
                for half in range(2):
                    last = transpose_rows(bank[:, half], lps[:, half, :, :])
                last.then_inc(n_hT, 1)

            def late_qkv(b, part, free, count, bank=psT[0][:]):
                pe.wait_ge(n_hTc, b + 1)
                wait(pe, free, count)
                if part < 2:
                    last = split3(bank, lxT[:, part], wA, 0, 2 * D)
                else:
                    for half in range(2):
                        last = split3(bank, lxT[:, half], wA, 2 * D, 3 * D, half * D)
                last.then_inc(n_qkv, 1)

            def late_group_T(b, pg, free, count):
                pe.wait_ge(n_spl, b * 4 + pg + 1)
                wait(pe, free, count)
                for half in range(2):
                    for a in range(2):
                        for qk in range(2):
                            last = TR(psTf[:, half, 2 * a + qk, :],
                                      lhl[:, pg % 2, half, qk, 2 * a:2 * a + 2].rearrange("p a b c -> p (a b c)"), identh[:])
                last.then_inc(n_tr, 1)

            def late_scores(b, p):
                pe.wait_ge(n_qk, b * 4 + p // 2 + 1)
                wait(pe, n_ms, b * 8 + p - 1)
                wait(pe, n_mid, b * 8 + p - 1)
                for e in range(2):
                    rows = slice(64 * e, 64 * e + 64)
                    ps = psS[:, 2 * (p % 2) + e, :]
                    M(ps[:, 0:T], lqkT[rows, p, 1, 0:P], lqkT[rows, p, 0, :], start=True, stop=True)
                    last = M(ps[:, T:T + P], lqkT[rows, p, 1, P:T], lqkT[rows, p, 0, P:T], start=True, stop=True)
                last.then_inc(n_sc, 1)

            def late_weighted(b, p):
                gp = p // 4
                pe.wait_ge(n_ms, b * 8 + p + 1)
                pe.wait_ge(n_pm, b * 8 + p + 1)
                if p % 4 == 0:
                    pe.wait_ge(n_vc, b * 2 + gp + 1)
                    wait(pe, n_oc, b * 2 + gp - 1)
                for e in range(2):
                    hd = 2 * (p % 4) + e
                    rows, c0 = slice(32 * (hd % 4), 32 * (hd % 4) + VW), (hd // 4) * T
                    M(psO[gp][rows, c0:c0 + T], lvaug[:, gp, 0, hd, :], lE[:, p % 2, e, 0:2, :].rearrange("p a b -> p (a b)"),
                      start=True, stop=False)
                    last = M(psO[gp][rows, c0 + P:c0 + T], lvaug[:, gp, 1, hd, :], lE[:, p % 2, e, 2, :], start=False, stop=True)
                last.then_inc(n_av, 1)

            def late_sums_T(b, gp):
                pe.wait_ge(n_oc, b * 2 + gp + 1)
                if gp:
                    wait(pe, n_out, b)
                    pe.wait_ge(n_osp, b * 2 + 1)
                else:
                    wait(pe, n_var2, b)
                for tt in range(2):
                    for st in range(2):
                        last = TR(psW[:, (2 * tt + st) * P:(2 * tt + st + 1) * P], loTs[:, st * T + tt * P:st * T + (tt + 1) * P], ident[:])
                last.then_inc(n_oT, 1)

            def late_T(b, ready, rows, value, done_sem):
                pe.wait_ge(ready, value)
                for half in range(2):
                    last = transpose_rows(psWh[:, half], rows[:, half, :, :])
                last.then_inc(done_sem, 1)

            def late_product(b, ready, w, done_sem):
                pe.wait_ge(ready, b + 1)
                for half in range(2):
                    last = split3(psW[:, half * D:], lyT[:, half], w, 0, D)
                last.then_inc(done_sem, 1)

            def pe_late(b, tail=True, group=True, prep=True):
                for p in range(8):
                    if p < 7:
                        late_scores(b, p + 1)
                    elif group:
                        late_scores(b + 1, 0)
                    late_weighted(b, p)
                    if p == 0:
                        if tail:
                            late_sums_T(b - 1, 1)
                        if prep:
                            late_norm_T(b + 2, n_qk, b * 4 + 4)
                    elif p % 2 == 0 and prep:
                        late_qkv(b + 2, p // 2 - 1, n_qk, b * 4 + 4 + p // 2)
                    if p % 2 and group:
                        if not prep:
                            late_group_T(b + 1, p // 2, n_qk, b * 4 + 4 + p // 2)
                        elif p == 1:
                            late_group_T(b + 1, 0, n_hTc, b + 3)
                        else:
                            late_group_T(b + 1, p // 2, n_x, b * 3 + 6 + p // 2)
                    if tail:
                        if p == 1:
                            late_T(b - 1, n_osp, losp, b * 2, n_lT)
                        if p == 3:
                            late_product(b - 1, n_lTc, wB, n_wo)
                        if p == 6:
                            pe.wait_ge(n_osp, b * 2 + 1)
                            late_T(b - 1, n_hs2, lhs, b, n_gT)
                        if p == 7:
                            late_product(b - 1, n_gTc, wM, n_ff)
                    if p == 5:
                        late_sums_T(b, 0)

            late_norm_T(0, n_qk, 0)
            for part in range(3):
                late_qkv(0, part, n_x, 0, psS[:, part, :])
            late_norm_T(1, n_hTc, 1, psWh)
            for pg in range(4):
                late_group_T(0, pg, n_qk if pg else n_hTc, pg if pg else 1)
                if pg:
                    late_qkv(1, pg - 1, n_x, pg, psS[:, (3, 0, 1)[pg - 1], :])
            pe.wait_ge(n_x, 6)
            late_scores(0, 0)
            pe_late(0, tail=False)
            with pe.Fori(0, NB - 3) as bb:
                pe_late(bb + 1)
            pe_late(NB - 2, prep=False)
            pe_late(NB - 1, group=False, prep=False)
            late_sums_T(NB - 1, 1)
            late_T(NB - 1, n_osp, losp, NB * 2, n_lT)
            late_product(NB - 1, n_lTc, wB, n_wo)
            late_T(NB - 1, n_hs2, lhs, NB, n_gT)
            late_product(NB - 1, n_gTc, wM, n_ff)


_HOST = ["x", "L0_tok_weights", "L0_attn_Wqkv", "L0_attn_Wo", "L0_attn_bo", "L0_ffn_w_router", "L0_ffn_w1", "L0_ffn_b1",
         "L0_ffn_w2", "L0_ffn_b2", "L1_attn_w_qkv", "L1_attn_b_qkv", "L1_attn_w_out", "L1_attn_b_out",
         "L1_ffn_w_freq_real", "L1_ffn_w_freq_imag", "L1_ffn_bias"]


def constants():
    import numpy as np
    f = np.float32
    pos = np.arange(T, dtype=f)
    inv = (1.0 / np.power(f(10000.0), np.arange(HD // 2, dtype=f) / f(HD // 2))).astype(f)
    ang = pos[:, None] * inv[None, :]
    cos = np.concatenate([np.cos(ang), np.cos(ang)], 1)
    sin = np.concatenate([-np.sin(ang), np.sin(ang)], 1)
    rope = np.stack([cos, sin], 1).reshape(2, P, 2, HD).transpose(1, 0, 2, 3)
    te = np.arange(P)
    tile, ex = te // NE, te % NE
    lt = (te[:, None] < te[None, :])
    k = np.arange(D)
    ang2 = 2.0 * np.pi * ((k[:, None] * k[None, :]) % D) / D
    dft = np.stack([np.cos(ang2), np.sin(ang2), -np.cos(ang2)]).reshape(3, KC, P, D).transpose(2, 0, 1, 3)
    iota = np.concatenate([np.tile(np.arange(P), (P, 1)), np.tile(np.arange(MT), (P, 1)), np.tile(np.arange(NE), (P, 1)),
                           np.arange(NT)[None, :] * P + te[:, None]], 1)
    c = {
        "c_ident": np.eye(P, dtype=f), "c_identh": np.eye(P, dtype=np.float16), "c_rope": rope,
        "c_j": np.tile(np.arange(T), (NB, 1)),
        "c_ltri": lt, "c_tpre": (ex[:, None] == ex[None, :]) & (tile[:, None] < tile[None, :]),
        "c_tsum": ex[:, None] == np.arange(NE)[None, :],
        "c_causal": te[:, None] <= te[None, :], "c_dft": dft, "c_iota": iota,
    }
    return {n: np.ascontiguousarray(a if a.dtype == np.float16 else a.astype(f)) for n, a in c.items()}


def kernel(**inputs):
    import numpy as _np
    import concourse.bacc as _bacc
    from concourse.bass_utils import run_bass_kernel_spmd as _run

    nc = _bacc.Bacc("TRN2", target_bir_lowering=False, num_devices=1)
    arrays, args = {}, []
    given = {n: _np.asarray(inputs[n]) for n in _HOST}
    given["L0_ffn_b1"] = given["L0_ffn_b1"].reshape(NE, CH, P).transpose(2, 0, 1)
    given["L1_attn_w_qkv"] = given["L1_attn_w_qkv"].T
    given["L1_attn_w_out"] = given["L1_attn_w_out"].T
    given.update(constants())
    for name, a in given.items():
        a = _np.ascontiguousarray(a)
        arrays["in_" + name] = a
        args.append(nc.dram_tensor("in_" + name, a.shape, mybir.dt.from_np(a.dtype), kind="ExternalInput").ap())
    out = nc.dram_tensor("out_0", (NB, T, D), fp32, kind="ExternalOutput").ap()
    lm_tower(nc, *args, out)
    r = _run(nc, [arrays], core_ids=[0])
    return r.results[0]["out_0"]
```
